# Optimizing a Trainium2 kernel written in Bass

```python
import numpy as np
import jax
import jax.numpy as jnp

def _softmax(x, axis=-1):
    return jax.nn.softmax(x, axis=axis)

def _gelu(x):
    return jax.nn.gelu(x, approximate=True)

def _silu(x):
    return jax.nn.silu(x)

def _sigmoid(x):
    return jax.nn.sigmoid(x)

def _layernorm(x, axis=-1, eps=1e-05):
    m = jnp.mean(x, axis=axis, keepdims=True)
    v = jnp.var(x, axis=axis, keepdims=True)
    return (x - m) / jnp.sqrt(v + eps)

def _scatter_add(tgt, idx, src, axis=0):
    return tgt.at[idx].add(src)

def _segment_sum(src, seg, n):
    return jax.ops.segment_sum(src, seg, n)
kernel_name = 'mk_perceiver_d4_seqx_r8_6680eb'

def setup_inputs(seed: int=0):
    np.random.seed(seed)
    _w = jnp.asarray

    def _rec_inputs():
        import jax
        import jax.numpy as jnp
        _rk = jax.random.key(seed)
        x = -0.0003929 + 0.9999 * jax.random.normal(jax.random.fold_in(_rk, 1), (64, 64, 128), jnp.float32)
        _lenS = 64 - jax.random.randint(jax.random.fold_in(_rk, 7), (64,), 0, max(1, 64 // 4) + 1, jnp.int32)
        _lenS2 = 128 - jax.random.randint(jax.random.fold_in(_rk, 8), (64,), 0, max(1, 128 // 4) + 1, jnp.int32)
        _ctx_768P = jax.random.normal(jax.random.fold_in(_rk, 11), (64, 16, 96), jnp.float32)
        _ctx_768c = jax.random.dirichlet(jax.random.fold_in(_rk, 511), 0.3 * jnp.ones((16,), jnp.float32), (64, 128))
        _ctx_768t = jnp.einsum('bsk,bkd->bsd', _ctx_768c, _ctx_768P)
        _ctx_768t = _ctx_768t * jax.lax.rsqrt(jnp.mean(jnp.square(_ctx_768t)) + 1e-12) * 0.953939
        ctx_768 = -7.36909e-05 + 0.999899 * (_ctx_768t + 0.3 * jax.random.normal(jax.random.fold_in(_rk, 611), (64, 128, 96), jnp.float32))
        _validS = jnp.arange(64)[None, :] < _lenS[:, None]
        _validS2 = jnp.arange(128)[None, :] < _lenS2[:, None]
        _causal = jnp.tril(jnp.ones((64, 64), dtype=bool))
        mask_BxS2_bk0 = jnp.logical_not(jnp.broadcast_to(_validS2[:, :], (64, 128)))
        return (x, ctx_768, mask_BxS2_bk0)
    x, ctx_768, mask_BxS2_bk0 = _rec_inputs()

    def _L0_xattn_setup():
        import jax, jax.numpy as jnp
        import numpy as np
        EPS = 1e-08
        key = jax.random.key(seed)
        kv, kt, k1, k2, k3, k4 = jax.random.split(key, 6)
        B, S = (16, 128)
        VD, TD, H = (128, 96, 64)
        visual_features = jax.random.normal(kv, (B, S, VD), dtype=jnp.float32)
        text_features = jax.random.normal(kt, (B, S, TD), dtype=jnp.float32)
        Wv = jax.random.normal(k1, (H, VD), dtype=jnp.float32) * (1.0 / np.sqrt(VD))
        bv = jax.random.normal(k2, (H,), dtype=jnp.float32) * 0.01
        Wt = jax.random.normal(k3, (H, TD), dtype=jnp.float32) * (1.0 / np.sqrt(TD))
        bt = jax.random.normal(k4, (H,), dtype=jnp.float32) * 0.01
        return {'visual_features': visual_features, 'text_features': text_features, 'Wv': Wv, 'bv': bv, 'Wt': Wt, 'bt': bt}
    _L0_xattn_all = _L0_xattn_setup()
    _L0_xattn_in = {k: v for k, v in _L0_xattn_all.items() if k in ('Wv', 'bv', 'Wt', 'bt')}
    del _L0_xattn_all

    def _L0_attn_setup():
        import jax, jax.numpy as jnp
        import numpy as np
        D_MODEL = 128
        NHEAD = 8
        HEAD_DIM = D_MODEL // NHEAD
        D_FF = 512
        EPS_ATTN = 1e-06
        EPS_LN = 1e-05

        def _layernorm(x, g, b):
            mu = jnp.mean(x, axis=-1, keepdims=True)
            var = jnp.var(x, axis=-1, keepdims=True)
            return (x - mu) * jax.lax.rsqrt(var + EPS_LN) * g + b

        def _linear_attention(q, k, v):
            Q = jax.nn.elu(q) + 1.0
            K = jax.nn.elu(k) + 1.0
            v_length = v.shape[1]
            v = v / v_length
            KV = jnp.einsum('nshd,nshv->nhdv', K, v)
            Z = 1.0 / (jnp.einsum('nlhd,nhd->nlh', Q, K.sum(axis=1)) + EPS_ATTN)
            out = jnp.einsum('nlhd,nhdv,nlh->nlhv', Q, KV, Z) * v_length
            return out
        key = jax.random.key(seed)
        ks = jax.random.split(key, 12)
        s = 1.0 / np.sqrt(D_MODEL)
        sf = 1.0 / np.sqrt(D_FF)
        return {'x': jax.random.normal(ks[0], (2, 512, D_MODEL), jnp.float32), 'wq': jax.random.normal(ks[1], (D_MODEL, D_MODEL), jnp.float32) * s, 'wk': jax.random.normal(ks[2], (D_MODEL, D_MODEL), jnp.float32) * s, 'wv': jax.random.normal(ks[3], (D_MODEL, D_MODEL), jnp.float32) * s, 'w1': jax.random.normal(ks[4], (D_FF, D_MODEL), jnp.float32) * s, 'b1': jnp.zeros((D_FF,), jnp.float32), 'w2': jax.random.normal(ks[5], (D_MODEL, D_FF), jnp.float32) * sf, 'b2': jnp.zeros((D_MODEL,), jnp.float32), 'g1': jnp.ones((D_MODEL,), jnp.float32), 'be1': jnp.zeros((D_MODEL,), jnp.float32), 'g2': jnp.ones((D_MODEL,), jnp.float32), 'be2': jnp.zeros((D_MODEL,), jnp.float32)}
    _L0_attn_all = _L0_attn_setup()
    _L0_attn_in = {k: v for k, v in _L0_attn_all.items() if k in ('wq', 'wk', 'wv', 'w1', 'b1', 'w2', 'b2', 'g1', 'be1', 'g2', 'be2')}
    del _L0_attn_all

    def _L0_ffn_setup():
        import jax, jax.numpy as jnp
        import numpy as np
        from jax import lax
        TOP_K = 4
        N_GROUP = 4
        TOPK_GROUP = 2
        ROUTED_SCALE = 2.5
        NEG_INF = -1000000000.0

        def _route(xf, router_weight, router_bias):
            T = xf.shape[0]
            E = router_weight.shape[0]
            logits = xf @ router_weight.T
            scores = jax.nn.sigmoid(logits)
            s_choice = scores + router_bias
            per_group = E // N_GROUP
            sg = s_choice.reshape(T, N_GROUP, per_group)
            group_scores = lax.top_k(sg, 2)[0].sum(-1)
            _, gidx = lax.top_k(group_scores, TOPK_GROUP)
            gmask = jnp.zeros((T, N_GROUP), dtype=bool).at[jnp.arange(T)[:, None], gidx].set(True)
            masked = jnp.where(gmask[:, :, None], sg, NEG_INF).reshape(T, E)
            _, topk_idx = lax.top_k(masked, TOP_K)
            w = jnp.take_along_axis(scores, topk_idx, axis=1)
            w = w / (w.sum(-1, keepdims=True) + 1e-20) * ROUTED_SCALE
            combine = jnp.zeros((T, E), dtype=xf.dtype).at[jnp.arange(T)[:, None], topk_idx].add(w)
            return combine
        key = jax.random.key(seed)
        ks = jax.random.split(key, 6)
        B, S, H, I, E = (2, 256, 128, 64, 16)
        x = jax.random.normal(ks[0], (B, S, H), dtype=jnp.float32)
        router_weight = jax.random.normal(ks[1], (E, H), dtype=jnp.float32) * 0.02
        router_bias = jnp.zeros((E,), dtype=jnp.float32)
        w_gate = jax.random.normal(ks[2], (E, I, H), dtype=jnp.float32) * 0.02
        w_up = jax.random.normal(ks[3], (E, I, H), dtype=jnp.float32) * 0.02
        w_down = jax.random.normal(ks[4], (E, H, I), dtype=jnp.float32) * 0.02
        return {'x': x, 'router_weight': router_weight, 'router_bias': router_bias, 'w_gate': w_gate, 'w_up': w_up, 'w_down': w_down}
    _L0_ffn_all = _L0_ffn_setup()
    _L0_ffn_in = {k: v for k, v in _L0_ffn_all.items() if k in ('router_weight', 'router_bias', 'w_gate', 'w_up', 'w_down')}
    del _L0_ffn_all

    def _L1_xattn_setup():
        import jax, jax.numpy as jnp
        import numpy as np
        DIM_IN, DIM_LAT, DIM_HEAD = (96, 128, 64)
        INNER = max(DIM_LAT, DIM_IN)
        HEADS = INNER // DIM_HEAD
        SCALE = DIM_HEAD ** (-0.5)
        RMS_EPS = 1e-08
        LN_EPS = 1e-05

        def layernorm(x, g, b):
            mu = jnp.mean(x, axis=-1, keepdims=True)
            var = jnp.mean((x - mu) ** 2, axis=-1, keepdims=True)
            return (x - mu) * jax.lax.rsqrt(var + LN_EPS) * g + b

        def rmsnorm(x, gamma):
            norm = jnp.sqrt(jnp.sum(x * x, axis=-1, keepdims=True)) * x.shape[-1] ** (-0.5)
            return x / jnp.maximum(norm, RMS_EPS) * gamma
        key = jax.random.key(seed)
        ks = jax.random.split(key, 12)
        b, n, m = (4, 512, 64)
        x = jax.random.normal(ks[0], (b, n, DIM_IN), jnp.float32)
        latents = jax.random.normal(ks[1], (b, m, DIM_LAT), jnp.float32)
        mask = jax.random.randint(ks[2], (b, n), 0, 2).astype(bool)
        s = lambda k, sh, fan: jax.random.normal(k, sh, jnp.float32) * fan ** (-0.5)
        return {'x': x, 'latents': latents, 'mask': mask, 'ln_x_g': jnp.ones((DIM_IN,), jnp.float32), 'ln_x_b': jnp.zeros((DIM_IN,), jnp.float32), 'ln_l_g': jnp.ones((DIM_LAT,), jnp.float32), 'ln_l_b': jnp.zeros((DIM_LAT,), jnp.float32), 'qn_g': jnp.ones((DIM_HEAD,), jnp.float32), 'kn_g': jnp.ones((DIM_HEAD,), jnp.float32), 'Wq': s(ks[3], (INNER, DIM_LAT), DIM_LAT), 'Wkv': s(ks[4], (2 * INNER, DIM_IN), DIM_IN), 'Wlkv': s(ks[5], (2 * INNER, DIM_LAT), DIM_LAT), 'Wo': s(ks[6], (DIM_LAT, INNER), INNER), 'bo': jnp.zeros((DIM_LAT,), jnp.float32)}
    _L1_xattn_all = _L1_xattn_setup()
    _L1_xattn_in = {k: v for k, v in _L1_xattn_all.items() if k in ('ln_x_g', 'ln_x_b', 'ln_l_g', 'ln_l_b', 'qn_g', 'kn_g', 'Wq', 'Wkv', 'Wlkv', 'Wo', 'bo')}
    del _L1_xattn_all

    def _L1_attn_setup():
        import jax, jax.numpy as jnp
        import numpy as np
        D = 128
        H = 16
        HD = D // H
        R = HD
        N, T = (2, 256)
        W_LEFT, W_RIGHT = (127, 128)
        ROPE_BASE = 10000.0

        def _rope(x, cos, sin):
            x1 = x[..., :R // 2]
            x2 = x[..., R // 2:R]
            rot = jnp.concatenate([x1 * cos - x2 * sin, x2 * cos + x1 * sin], axis=-1)
            if R < x.shape[-1]:
                rot = jnp.concatenate([rot, x[..., R:]], axis=-1)
            return rot
        key = jax.random.key(seed)
        k1, k2, k3, k4 = jax.random.split(key, 4)
        x = jax.random.normal(k1, (N, T, D), dtype=jnp.float32)
        w_qkv = jax.random.normal(k2, (3 * D, D), dtype=jnp.float32) * 0.02
        w_out = jax.random.normal(k3, (D, D), dtype=jnp.float32) * 0.02
        b_out = jax.random.normal(k4, (D,), dtype=jnp.float32) * 0.02
        return {'x': x, 'w_qkv': w_qkv, 'w_out': w_out, 'b_out': b_out}
    _L1_attn_all = _L1_attn_setup()
    _L1_attn_in = {k: v for k, v in _L1_attn_all.items() if k in ('w_qkv', 'w_out', 'b_out')}
    del _L1_attn_all

    def _L1_ffn_setup():
        import jax, jax.numpy as jnp
        import numpy as np
        B, S, D_MODEL, D_FF, E, R, TOP_K = (4, 256, 128, 512, 8, 16, 2)
        key = jax.random.key(seed)
        ks = jax.random.split(key, 9)
        sd = 1.0 / np.sqrt(D_MODEL)
        return {'hidden_states': jax.random.normal(ks[0], (B, S, D_MODEL), jnp.float32), 'wi': jax.random.normal(ks[1], (D_FF, D_MODEL), jnp.float32) * sd, 'bi': jax.random.normal(ks[2], (D_FF,), jnp.float32) * 0.01, 'wo': jax.random.normal(ks[3], (D_MODEL, D_FF), jnp.float32) * (1.0 / np.sqrt(D_FF)), 'bo': jax.random.normal(ks[4], (D_MODEL,), jnp.float32) * 0.01, 'lora_A': jax.random.normal(ks[5], (E, R, D_MODEL), jnp.float32) * sd, 'lora_B': jax.random.normal(ks[6], (E, D_FF, R), jnp.float32) * 0.02, 'gate_w': jax.random.normal(ks[7], (E, D_MODEL), jnp.float32) * sd, 'gate_b': jax.random.normal(ks[8], (E,), jnp.float32) * 0.01}
    _L1_ffn_all = _L1_ffn_setup()
    _L1_ffn_in = {k: v for k, v in _L1_ffn_all.items() if k in ('wi', 'bi', 'wo', 'bo', 'lora_A', 'lora_B', 'gate_w', 'gate_b')}
    del _L1_ffn_all

    def _L2_xattn_setup():
        import jax, jax.numpy as jnp
        import numpy as np
        NUM_HEADS = 16
        CLAMP = 10000.0
        key = jax.random.key(seed)
        ks = jax.random.split(key, 8)
        B, Nq, Nkv, Cq, Ckv = (4, 256, 256, 128, 96)
        s_q = 1.0 / np.sqrt(Cq)
        s_kv = 1.0 / np.sqrt(Ckv)
        return {'query': jax.random.normal(ks[0], (B, Nq, Cq), jnp.float32), 'key_value': jax.random.normal(ks[1], (B, Nkv, Ckv), jnp.float32), 'Wq': jax.random.normal(ks[2], (Cq, Cq), jnp.float32) * s_q, 'bq': jnp.zeros((Cq,), jnp.float32), 'Wk': jax.random.normal(ks[3], (Ckv, Cq), jnp.float32) * s_kv, 'bk': jnp.zeros((Cq,), jnp.float32), 'Wv': jax.random.normal(ks[4], (Ckv, Cq), jnp.float32) * s_kv, 'bv': jnp.zeros((Cq,), jnp.float32), 'Wo': jax.random.normal(ks[5], (Cq, Cq), jnp.float32) * s_q, 'bo': jnp.zeros((Cq,), jnp.float32)}
    _L2_xattn_all = _L2_xattn_setup()
    _L2_xattn_in = {k: v for k, v in _L2_xattn_all.items() if k in ('Wq', 'bq', 'Wk', 'bk', 'Wv', 'bv', 'Wo', 'bo')}
    del _L2_xattn_all

    def _L2_attn_setup():
        import jax, jax.numpy as jnp
        import numpy as np
        NUM_HEADS = 16
        EPS = 1e-06

        def _phi(x):
            return jax.nn.elu(x) + 1.0
        key = jax.random.key(seed)
        ks = jax.random.split(key, 5)
        B, L, D = (4, 1024, 128)
        scale = 0.02
        return {'x': jax.random.normal(ks[0], (B, L, D), dtype=jnp.float32), 'Wq': jax.random.normal(ks[1], (D, D), dtype=jnp.float32) * scale, 'Wk': jax.random.normal(ks[2], (D, D), dtype=jnp.float32) * scale, 'Wv': jax.random.normal(ks[3], (D, D), dtype=jnp.float32) * scale, 'Wo': jax.random.normal(ks[4], (D, D), dtype=jnp.float32) * scale}
    _L2_attn_all = _L2_attn_setup()
    _L2_attn_in = {k: v for k, v in _L2_attn_all.items() if k in ('Wq', 'Wk', 'Wv', 'Wo')}
    del _L2_attn_all

    def _L2_ffn_setup():
        import jax, jax.numpy as jnp
        import numpy as np
        B, T, C = (2, 256, 128)
        H, D = (16, 64)
        CR = 8
        R = C // CR
        ROPE = D // 2
        NOPE = D - ROPE
        E, K, I, S = (8, 2, 64, 1)
        THETA = 100000.0
        EPS = 1e-05

        def _rmsnorm(x, w):
            rms = jnp.sqrt(jnp.mean(x * x, axis=-1, keepdims=True) + EPS)
            return w * (x / rms)

        def _rope(xh):
            d = xh.shape[-1]
            t = jnp.arange(xh.shape[2], dtype=jnp.float32)
            freqs = 1.0 / THETA ** (jnp.arange(0, d, 2, dtype=jnp.float32) / d)
            ang = jnp.outer(t, freqs)
            cos, sin = (jnp.cos(ang), jnp.sin(ang))
            xr = xh.reshape(xh.shape[:-1] + (d // 2, 2))
            x0, x1 = (xr[..., 0], xr[..., 1])
            rot = jnp.stack([x0 * cos - x1 * sin, x0 * sin + x1 * cos], axis=-1)
            return rot.reshape(xh.shape)

        def _attention(x, Wq, Wkva, Wkvb, Wo):
            b, t, _ = x.shape
            q = (x @ Wq).reshape(b, t, H, D).transpose(0, 2, 1, 3)
            ckv = x @ Wkva
            kv_latent, k_rope = (ckv[:, :, :R], ckv[:, :, R:])
            kv = (kv_latent @ Wkvb).reshape(b, t, H, NOPE).transpose(0, 2, 1, 3)
            k_rope = jnp.broadcast_to(k_rope[:, None, :, :], (b, H, t, ROPE))
            q_nope, q_rope = (q[..., :NOPE], q[..., NOPE:])
            q = jnp.concatenate([q_nope, _rope(q_rope)], axis=-1)
            k = jnp.concatenate([kv, _rope(k_rope)], axis=-1)
            v = jnp.concatenate([kv, jnp.zeros_like(k_rope)], axis=-1)
            att = jnp.einsum('bhqd,bhkd->bhqk', q, k) / jnp.sqrt(jnp.float32(D))
            mask = jnp.tril(jnp.ones((t, t), dtype=bool))
            att = jnp.where(mask, att, jnp.float32(-jnp.inf))
            att = jax.nn.softmax(att, axis=-1)
            y = jnp.einsum('bhqk,bhkd->bhqd', att, v)
            y = y.transpose(0, 2, 1, 3).reshape(b, t, H * D)
            return y @ Wo

        def _experts(x_flat, Wg, Wu, Wd):
            g = jax.nn.silu(jnp.einsum('nc,eci->nei', x_flat, Wg))
            u = jnp.einsum('nc,eci->nei', x_flat, Wu)
            return jnp.einsum('nei,eic->nec', g * u, Wd)

        def _moe(x, Wgate, expert_bias, Wg, Wu, Wd, sWg, sWu, sWd):
            b, t, c = x.shape
            xf = x.reshape(-1, c)
            shared = jnp.mean(_experts(xf, sWg, sWu, sWd), axis=1)
            logits = xf @ Wgate + expert_bias
            probs = jax.nn.softmax(logits, axis=-1)
            topk_p, topk_i = jax.lax.top_k(probs, K)
            topk_p = topk_p / jnp.sum(topk_p, axis=-1, keepdims=True)
            comb = jnp.sum(jax.nn.one_hot(topk_i, E, dtype=xf.dtype) * topk_p[..., None], axis=1)
            routed = jnp.einsum('ne,nec->nc', comb, _experts(xf, Wg, Wu, Wd))
            return (shared + routed).reshape(b, t, c)
        key = jax.random.key(seed)
        ks = jax.random.split(key, 16)
        w = lambda k, shp: jax.random.normal(k, shp, dtype=jnp.float32) * 0.02
        return {'x': jax.random.normal(ks[0], (B, T, C), dtype=jnp.float32), 'w_ln1': jnp.ones((C,), jnp.float32), 'Wq': w(ks[1], (C, H * D)), 'Wkva': w(ks[2], (C, R + ROPE)), 'Wkvb': w(ks[3], (R, H * NOPE)), 'Wo': w(ks[4], (H * D, C)), 'w_ln2': jnp.ones((C,), jnp.float32), 'Wgate': w(ks[5], (C, E)), 'expert_bias': jnp.zeros((E,), jnp.float32), 'Wg': w(ks[6], (E, C, I)), 'Wu': w(ks[7], (E, C, I)), 'Wd': w(ks[8], (E, I, C)), 'sWg': w(ks[9], (S, C, I)), 'sWu': w(ks[10], (S, C, I)), 'sWd': w(ks[11], (S, I, C))}
    _L2_ffn_all = _L2_ffn_setup()
    _L2_ffn_in = {k: v for k, v in _L2_ffn_all.items() if k in ('w_ln1', 'Wq', 'Wkva', 'Wkvb', 'Wo', 'w_ln2', 'Wgate', 'expert_bias', 'Wg', 'Wu', 'Wd', 'sWg', 'sWu', 'sWd')}
    del _L2_ffn_all

    def _L3_xattn_setup():
        import jax, jax.numpy as jnp
        import numpy as np
        IMAGE_DIM = 128
        TEXT_DIM = 96
        NUM_HEADS = 16
        HEAD_DIM = IMAGE_DIM // NUM_HEADS
        key = jax.random.key(seed)
        ks = jax.random.split(key, 14)
        B, N, M = (4, 512, 64)
        s_img = 1.0 / np.sqrt(IMAGE_DIM)
        s_txt = 1.0 / np.sqrt(TEXT_DIM)
        s_ff = 1.0 / np.sqrt(2 * IMAGE_DIM)
        return {'x': jax.random.normal(ks[0], (B, N, IMAGE_DIM), jnp.float32), 'y': jax.random.normal(ks[1], (B, M, TEXT_DIM), jnp.float32), 'Wq': jax.random.normal(ks[2], (IMAGE_DIM, IMAGE_DIM), jnp.float32) * s_img, 'bq': jax.random.normal(ks[3], (IMAGE_DIM,), jnp.float32) * s_img, 'Wk': jax.random.normal(ks[4], (TEXT_DIM, IMAGE_DIM), jnp.float32) * s_txt, 'bk': jax.random.normal(ks[5], (IMAGE_DIM,), jnp.float32) * s_txt, 'Wv': jax.random.normal(ks[6], (TEXT_DIM, IMAGE_DIM), jnp.float32) * s_txt, 'bv': jax.random.normal(ks[7], (IMAGE_DIM,), jnp.float32) * s_txt, 'W1': jax.random.normal(ks[8], (IMAGE_DIM, 2 * IMAGE_DIM), jnp.float32) * s_img, 'b1': jax.random.normal(ks[9], (2 * IMAGE_DIM,), jnp.float32) * s_img, 'W2': jax.random.normal(ks[10], (2 * IMAGE_DIM, IMAGE_DIM), jnp.float32) * s_ff, 'b2': jax.random.normal(ks[11], (IMAGE_DIM,), jnp.float32) * s_ff}
    _L3_xattn_all = _L3_xattn_setup()
    _L3_xattn_in = {k: v for k, v in _L3_xattn_all.items() if k in ('Wq', 'bq', 'Wk', 'bk', 'Wv', 'bv', 'W1', 'b1', 'W2', 'b2')}
    del _L3_xattn_all

    def _L3_attn_setup():
        import jax, jax.numpy as jnp
        import numpy as np
        B, T, D = (4, 256, 128)
        H = 4
        K = D
        V = D
        DK = K // H
        DV = V // H
        LOW = 16
        GLN = 16.0

        def _layernorm(x, w, b, eps=1e-05):
            mu = x.mean(-1, keepdims=True)
            xc = x - mu
            var = (xc * xc).mean(-1, keepdims=True)
            return xc * jax.lax.rsqrt(var + eps) * w + b

        def _rmsnorm(x, w, eps=1e-05):
            ms = (x * x).mean(-1, keepdims=True)
            return x * jax.lax.rsqrt(ms + eps) * w

        def _gla_scan(q, k, v, gk):
            scale = DK ** (-0.5)
            qT = jnp.moveaxis(q * scale, 1, 0)
            kT = jnp.moveaxis(k, 1, 0)
            vT = jnp.moveaxis(v, 1, 0)
            gT = jnp.moveaxis(gk, 1, 0)

            def step(h, inp):
                qt, kt, vt, gt = inp
                h = h * jnp.exp(gt)[..., None] + kt[..., :, None] * vt[..., None, :]
                o = jnp.einsum('bhk,bhkv->bhv', qt, h)
                return (h, o)
            h0 = jnp.zeros((q.shape[0], H, DK, DV), q.dtype)
            _, oT = jax.lax.scan(step, h0, (qT, kT, vT, gT))
            return jnp.moveaxis(oT, 0, 1)
        key = jax.random.key(seed)
        ks = jax.random.split(key, 12)
        rn = lambda k, s: jax.random.normal(k, s, jnp.float32) * 0.02
        return {'x': jax.random.normal(ks[0], (B, T, D), jnp.float32), 'ln1_w': jnp.ones((D,), jnp.float32), 'ln1_b': jnp.zeros((D,), jnp.float32), 'Wq': rn(ks[1], (D, K)), 'Wk': rn(ks[2], (D, K)), 'Wv': rn(ks[3], (D, V)), 'Wg': rn(ks[4], (D, V)), 'Wgk1': rn(ks[5], (D, LOW)), 'Wgk2': rn(ks[6], (LOW, K)), 'bgk2': jnp.zeros((K,), jnp.float32), 'rms_w': jnp.ones((DV,), jnp.float32), 'Wo': rn(ks[7], (V, D)), 'ln2_w': jnp.ones((D,), jnp.float32), 'ln2_b': jnp.zeros((D,), jnp.float32), 'W1': rn(ks[8], (D, 3 * D)), 'b1': jnp.zeros((3 * D,), jnp.float32), 'W2': rn(ks[9], (3 * D, D)), 'b2': jnp.zeros((D,), jnp.float32)}
    _L3_attn_all = _L3_attn_setup()
    _L3_attn_in = {k: v for k, v in _L3_attn_all.items() if k in ('ln1_w', 'ln1_b', 'Wq', 'Wk', 'Wv', 'Wg', 'Wgk1', 'Wgk2', 'bgk2', 'rms_w', 'Wo', 'ln2_w', 'ln2_b', 'W1', 'b1', 'W2', 'b2')}
    del _L3_attn_all

    def _L3_ffn_setup():
        import jax, jax.numpy as jnp
        import numpy as np
        B, T, D = (4, 512, 128)
        E = 8
        TOP_K = 2
        FFN = 384
        HALF = FFN // 2

        def _kaiming_uniform(key, shape, fan_in):
            bound = 1.0 / np.sqrt(fan_in)
            return jax.random.uniform(key, shape, jnp.float32, -bound, bound)
        key = jax.random.key(seed)
        ks = jax.random.split(key, 7)
        x = jax.random.normal(ks[0], (B, T, D), jnp.float32)
        gate_w = _kaiming_uniform(ks[1], (E, D), D) * 0.01
        w_up = _kaiming_uniform(ks[2], (E, FFN, D), D)
        w_down = _kaiming_uniform(ks[3], (E, D, HALF), HALF)
        sg_gate = _kaiming_uniform(ks[4], (HALF, D), D)
        sg_up = _kaiming_uniform(ks[5], (HALF, D), D)
        sg_down = _kaiming_uniform(ks[6], (D, HALF), HALF)
        return {'x': x, 'gate_w': gate_w, 'w_up': w_up, 'w_down': w_down, 'sg_gate': sg_gate, 'sg_up': sg_up, 'sg_down': sg_down}
    _L3_ffn_all = _L3_ffn_setup()
    _L3_ffn_in = {k: v for k, v in _L3_ffn_all.items() if k in ('gate_w', 'w_up', 'w_down', 'sg_gate', 'sg_up', 'sg_down')}
    del _L3_ffn_all
    return {'x': x, 'ctx_768': ctx_768, 'mask_BxS2_bk0': mask_BxS2_bk0, 'L0_xattn_Wv': _L0_xattn_in['Wv'], 'L0_xattn_bv': _L0_xattn_in['bv'], 'L0_xattn_Wt': _L0_xattn_in['Wt'], 'L0_xattn_bt': _L0_xattn_in['bt'], 'L0_attn_wq': _L0_attn_in['wq'], 'L0_attn_wk': _L0_attn_in['wk'], 'L0_attn_wv': _L0_attn_in['wv'], 'L0_attn_w1': _L0_attn_in['w1'], 'L0_attn_b1': _L0_attn_in['b1'], 'L0_attn_w2': _L0_attn_in['w2'], 'L0_attn_b2': _L0_attn_in['b2'], 'L0_attn_g1': _L0_attn_in['g1'], 'L0_attn_be1': _L0_attn_in['be1'], 'L0_attn_g2': _L0_attn_in['g2'], 'L0_attn_be2': _L0_attn_in['be2'], 'L0_ffn_router_weight': _L0_ffn_in['router_weight'], 'L0_ffn_router_bias': _L0_ffn_in['router_bias'], 'L0_ffn_w_gate': _L0_ffn_in['w_gate'], 'L0_ffn_w_up': _L0_ffn_in['w_up'], 'L0_ffn_w_down': _L0_ffn_in['w_down'], 'L1_xattn_ln_x_g': _L1_xattn_in['ln_x_g'], 'L1_xattn_ln_x_b': _L1_xattn_in['ln_x_b'], 'L1_xattn_ln_l_g': _L1_xattn_in['ln_l_g'], 'L1_xattn_ln_l_b': _L1_xattn_in['ln_l_b'], 'L1_xattn_qn_g': _L1_xattn_in['qn_g'], 'L1_xattn_kn_g': _L1_xattn_in['kn_g'], 'L1_xattn_Wq': _L1_xattn_in['Wq'], 'L1_xattn_Wkv': _L1_xattn_in['Wkv'], 'L1_xattn_Wlkv': _L1_xattn_in['Wlkv'], 'L1_xattn_Wo': _L1_xattn_in['Wo'], 'L1_xattn_bo': _L1_xattn_in['bo'], 'L1_attn_w_qkv': _L1_attn_in['w_qkv'], 'L1_attn_w_out': _L1_attn_in['w_out'], 'L1_attn_b_out': _L1_attn_in['b_out'], 'L1_ffn_wi': _L1_ffn_in['wi'], 'L1_ffn_bi': _L1_ffn_in['bi'], 'L1_ffn_wo': _L1_ffn_in['wo'], 'L1_ffn_bo': _L1_ffn_in['bo'], 'L1_ffn_lora_A': _L1_ffn_in['lora_A'], 'L1_ffn_lora_B': _L1_ffn_in['lora_B'], 'L1_ffn_gate_w': _L1_ffn_in['gate_w'], 'L1_ffn_gate_b': _L1_ffn_in['gate_b'], 'L2_xattn_Wq': _L2_xattn_in['Wq'], 'L2_xattn_bq': _L2_xattn_in['bq'], 'L2_xattn_Wk': _L2_xattn_in['Wk'], 'L2_xattn_bk': _L2_xattn_in['bk'], 'L2_xattn_Wv': _L2_xattn_in['Wv'], 'L2_xattn_bv': _L2_xattn_in['bv'], 'L2_xattn_Wo': _L2_xattn_in['Wo'], 'L2_xattn_bo': _L2_xattn_in['bo'], 'L2_attn_Wq': _L2_attn_in['Wq'], 'L2_attn_Wk': _L2_attn_in['Wk'], 'L2_attn_Wv': _L2_attn_in['Wv'], 'L2_attn_Wo': _L2_attn_in['Wo'], 'L2_ffn_w_ln1': _L2_ffn_in['w_ln1'], 'L2_ffn_Wq': _L2_ffn_in['Wq'], 'L2_ffn_Wkva': _L2_ffn_in['Wkva'], 'L2_ffn_Wkvb': _L2_ffn_in['Wkvb'], 'L2_ffn_Wo': _L2_ffn_in['Wo'], 'L2_ffn_w_ln2': _L2_ffn_in['w_ln2'], 'L2_ffn_Wgate': _L2_ffn_in['Wgate'], 'L2_ffn_expert_bias': _L2_ffn_in['expert_bias'], 'L2_ffn_Wg': _L2_ffn_in['Wg'], 'L2_ffn_Wu': _L2_ffn_in['Wu'], 'L2_ffn_Wd': _L2_ffn_in['Wd'], 'L2_ffn_sWg': _L2_ffn_in['sWg'], 'L2_ffn_sWu': _L2_ffn_in['sWu'], 'L2_ffn_sWd': _L2_ffn_in['sWd'], 'L3_xattn_Wq': _L3_xattn_in['Wq'], 'L3_xattn_bq': _L3_xattn_in['bq'], 'L3_xattn_Wk': _L3_xattn_in['Wk'], 'L3_xattn_bk': _L3_xattn_in['bk'], 'L3_xattn_Wv': _L3_xattn_in['Wv'], 'L3_xattn_bv': _L3_xattn_in['bv'], 'L3_xattn_W1': _L3_xattn_in['W1'], 'L3_xattn_b1': _L3_xattn_in['b1'], 'L3_xattn_W2': _L3_xattn_in['W2'], 'L3_xattn_b2': _L3_xattn_in['b2'], 'L3_attn_ln1_w': _L3_attn_in['ln1_w'], 'L3_attn_ln1_b': _L3_attn_in['ln1_b'], 'L3_attn_Wq': _L3_attn_in['Wq'], 'L3_attn_Wk': _L3_attn_in['Wk'], 'L3_attn_Wv': _L3_attn_in['Wv'], 'L3_attn_Wg': _L3_attn_in['Wg'], 'L3_attn_Wgk1': _L3_attn_in['Wgk1'], 'L3_attn_Wgk2': _L3_attn_in['Wgk2'], 'L3_attn_bgk2': _L3_attn_in['bgk2'], 'L3_attn_rms_w': _L3_attn_in['rms_w'], 'L3_attn_Wo': _L3_attn_in['Wo'], 'L3_attn_ln2_w': _L3_attn_in['ln2_w'], 'L3_attn_ln2_b': _L3_attn_in['ln2_b'], 'L3_attn_W1': _L3_attn_in['W1'], 'L3_attn_b1': _L3_attn_in['b1'], 'L3_attn_W2': _L3_attn_in['W2'], 'L3_attn_b2': _L3_attn_in['b2'], 'L3_ffn_gate_w': _L3_ffn_in['gate_w'], 'L3_ffn_w_up': _L3_ffn_in['w_up'], 'L3_ffn_w_down': _L3_ffn_in['w_down'], 'L3_ffn_sg_gate': _L3_ffn_in['sg_gate'], 'L3_ffn_sg_up': _L3_ffn_in['sg_up'], 'L3_ffn_sg_down': _L3_ffn_in['sg_down']}

def reference(x, ctx_768, mask_BxS2_bk0, L0_xattn_Wv, L0_xattn_bv, L0_xattn_Wt, L0_xattn_bt, L0_attn_wq, L0_attn_wk, L0_attn_wv, L0_attn_w1, L0_attn_b1, L0_attn_w2, L0_attn_b2, L0_attn_g1, L0_attn_be1, L0_attn_g2, L0_attn_be2, L0_ffn_router_weight, L0_ffn_router_bias, L0_ffn_w_gate, L0_ffn_w_up, L0_ffn_w_down, L1_xattn_ln_x_g, L1_xattn_ln_x_b, L1_xattn_ln_l_g, L1_xattn_ln_l_b, L1_xattn_qn_g, L1_xattn_kn_g, L1_xattn_Wq, L1_xattn_Wkv, L1_xattn_Wlkv, L1_xattn_Wo, L1_xattn_bo, L1_attn_w_qkv, L1_attn_w_out, L1_attn_b_out, L1_ffn_wi, L1_ffn_bi, L1_ffn_wo, L1_ffn_bo, L1_ffn_lora_A, L1_ffn_lora_B, L1_ffn_gate_w, L1_ffn_gate_b, L2_xattn_Wq, L2_xattn_bq, L2_xattn_Wk, L2_xattn_bk, L2_xattn_Wv, L2_xattn_bv, L2_xattn_Wo, L2_xattn_bo, L2_attn_Wq, L2_attn_Wk, L2_attn_Wv, L2_attn_Wo, L2_ffn_w_ln1, L2_ffn_Wq, L2_ffn_Wkva, L2_ffn_Wkvb, L2_ffn_Wo, L2_ffn_w_ln2, L2_ffn_Wgate, L2_ffn_expert_bias, L2_ffn_Wg, L2_ffn_Wu, L2_ffn_Wd, L2_ffn_sWg, L2_ffn_sWu, L2_ffn_sWd, L3_xattn_Wq, L3_xattn_bq, L3_xattn_Wk, L3_xattn_bk, L3_xattn_Wv, L3_xattn_bv, L3_xattn_W1, L3_xattn_b1, L3_xattn_W2, L3_xattn_b2, L3_attn_ln1_w, L3_attn_ln1_b, L3_attn_Wq, L3_attn_Wk, L3_attn_Wv, L3_attn_Wg, L3_attn_Wgk1, L3_attn_Wgk2, L3_attn_bgk2, L3_attn_rms_w, L3_attn_Wo, L3_attn_ln2_w, L3_attn_ln2_b, L3_attn_W1, L3_attn_b1, L3_attn_W2, L3_attn_b2, L3_ffn_gate_w, L3_ffn_w_up, L3_ffn_w_down, L3_ffn_sg_gate, L3_ffn_sg_up, L3_ffn_sg_down):
    import jax
    import jax.numpy as jnp

    def _L0_xattn_ref(visual_features, text_features, Wv, bv, Wt, bt):
        import jax, jax.numpy as jnp
        import numpy as np
        EPS = 1e-08
        v = jnp.einsum('bsd,hd->bsh', visual_features, Wv) + bv
        t = jnp.einsum('bsd,hd->bsh', text_features, Wt) + bt
        dots = jnp.einsum('bih,bjh->bij', v, t)
        vn = jnp.linalg.norm(v, axis=-1)
        tn = jnp.linalg.norm(t, axis=-1)
        denom = jnp.maximum(vn[:, :, None] * tn[:, None, :], EPS)
        return dots / denom

    def _L0_attn_ref(x, wq, wk, wv, w1, b1, w2, b2, g1, be1, g2, be2):
        import jax, jax.numpy as jnp
        import numpy as np
        D_MODEL = 128
        NHEAD = 8
        HEAD_DIM = D_MODEL // NHEAD
        D_FF = 512
        EPS_ATTN = 1e-06
        EPS_LN = 1e-05

        def _layernorm(x, g, b):
            mu = jnp.mean(x, axis=-1, keepdims=True)
            var = jnp.var(x, axis=-1, keepdims=True)
            return (x - mu) * jax.lax.rsqrt(var + EPS_LN) * g + b

        def _linear_attention(q, k, v):
            Q = jax.nn.elu(q) + 1.0
            K = jax.nn.elu(k) + 1.0
            v_length = v.shape[1]
            v = v / v_length
            KV = jnp.einsum('nshd,nshv->nhdv', K, v)
            Z = 1.0 / (jnp.einsum('nlhd,nhd->nlh', Q, K.sum(axis=1)) + EPS_ATTN)
            out = jnp.einsum('nlhd,nhdv,nlh->nlhv', Q, KV, Z) * v_length
            return out
        N, L, C = x.shape
        x2 = _layernorm(x, g1, be1)
        q = (x2 @ wq.T).reshape(N, L, NHEAD, HEAD_DIM)
        k = (x2 @ wk.T).reshape(N, L, NHEAD, HEAD_DIM)
        v = (x2 @ wv.T).reshape(N, L, NHEAD, HEAD_DIM)
        msg = _linear_attention(q, k, v).reshape(N, L, C)
        x = x + msg
        x2 = _layernorm(x, g2, be2)
        h = jax.nn.gelu(x2 @ w1.T + b1, approximate=False)
        x = x + (h @ w2.T + b2)
        return x

    def _L0_ffn_ref(x, router_weight, router_bias, w_gate, w_up, w_down):
        import jax, jax.numpy as jnp
        import numpy as np
        from jax import lax
        TOP_K = 4
        N_GROUP = 4
        TOPK_GROUP = 2
        ROUTED_SCALE = 2.5
        NEG_INF = -1000000000.0

        def _route(xf, router_weight, router_bias):
            T = xf.shape[0]
            E = router_weight.shape[0]
            logits = xf @ router_weight.T
            scores = jax.nn.sigmoid(logits)
            s_choice = scores + router_bias
            per_group = E // N_GROUP
            sg = s_choice.reshape(T, N_GROUP, per_group)
            group_scores = lax.top_k(sg, 2)[0].sum(-1)
            _, gidx = lax.top_k(group_scores, TOPK_GROUP)
            gmask = jnp.zeros((T, N_GROUP), dtype=bool).at[jnp.arange(T)[:, None], gidx].set(True)
            masked = jnp.where(gmask[:, :, None], sg, NEG_INF).reshape(T, E)
            _, topk_idx = lax.top_k(masked, TOP_K)
            w = jnp.take_along_axis(scores, topk_idx, axis=1)
            w = w / (w.sum(-1, keepdims=True) + 1e-20) * ROUTED_SCALE
            combine = jnp.zeros((T, E), dtype=xf.dtype).at[jnp.arange(T)[:, None], topk_idx].add(w)
            return combine
        B, S, H = x.shape
        E = w_gate.shape[0]
        xf = x.reshape(-1, H)
        combine = _route(xf, router_weight, router_bias)
        out = jnp.zeros_like(xf)
        for e in range(E):
            g = xf @ w_gate[e].T
            u = xf @ w_up[e].T
            y_e = jax.nn.silu(g) * u @ w_down[e].T
            out = out + combine[:, e:e + 1] * y_e
        return out.reshape(B, S, H)

    def _L1_xattn_ref(x, latents, mask, ln_x_g, ln_x_b, ln_l_g, ln_l_b, qn_g, kn_g, Wq, Wkv, Wlkv, Wo, bo):
        import jax, jax.numpy as jnp
        import numpy as np
        DIM_IN, DIM_LAT, DIM_HEAD = (96, 128, 64)
        INNER = max(DIM_LAT, DIM_IN)
        HEADS = INNER // DIM_HEAD
        SCALE = DIM_HEAD ** (-0.5)
        RMS_EPS = 1e-08
        LN_EPS = 1e-05

        def layernorm(x, g, b):
            mu = jnp.mean(x, axis=-1, keepdims=True)
            var = jnp.mean((x - mu) ** 2, axis=-1, keepdims=True)
            return (x - mu) * jax.lax.rsqrt(var + LN_EPS) * g + b

        def rmsnorm(x, gamma):
            norm = jnp.sqrt(jnp.sum(x * x, axis=-1, keepdims=True)) * x.shape[-1] ** (-0.5)
            return x / jnp.maximum(norm, RMS_EPS) * gamma
        b, n, _ = x.shape
        m = latents.shape[1]
        xn = layernorm(x, ln_x_g, ln_x_b)
        ln = layernorm(latents, ln_l_g, ln_l_b)
        q = ln @ Wq.T
        kv = jnp.concatenate([xn @ Wkv.T, ln @ Wlkv.T], axis=1)
        k, v = (kv[..., :INNER], kv[..., INNER:])
        split_heads = lambda t: t.reshape(t.shape[0], t.shape[1], HEADS, DIM_HEAD).transpose(0, 2, 1, 3)
        q, k, v = (split_heads(q), split_heads(k), split_heads(v))
        qn = rmsnorm(q, qn_g) * SCALE
        kn = rmsnorm(k, kn_g)
        attn = jnp.einsum('bhid,bhjd->bhij', qn, kn)
        full_mask = jnp.pad(mask, ((0, 0), (0, m)), constant_values=True)
        attn = jnp.where(full_mask[:, None, None, :], attn, -jnp.finfo(attn.dtype).max)
        attn = jax.nn.softmax(attn, axis=-1)
        out = jnp.einsum('bhij,bhjd->bhid', attn, v)
        out = out.transpose(0, 2, 1, 3).reshape(b, m, INNER)
        return out @ Wo.T + bo

    def _L1_attn_ref(x, w_qkv, w_out, b_out):
        import jax, jax.numpy as jnp
        import numpy as np
        D = 128
        H = 16
        HD = D // H
        R = HD
        N, T = (2, 256)
        W_LEFT, W_RIGHT = (127, 128)
        ROPE_BASE = 10000.0

        def _rope(x, cos, sin):
            x1 = x[..., :R // 2]
            x2 = x[..., R // 2:R]
            rot = jnp.concatenate([x1 * cos - x2 * sin, x2 * cos + x1 * sin], axis=-1)
            if R < x.shape[-1]:
                rot = jnp.concatenate([rot, x[..., R:]], axis=-1)
            return rot
        n, t, _ = x.shape
        qkv = (x @ w_qkv.T).reshape(n, t, 3, H, HD)
        q, k, v = (qkv[:, :, 0], qkv[:, :, 1], qkv[:, :, 2])
        pos = jnp.arange(t, dtype=jnp.float32)
        inv_freq = 1.0 / ROPE_BASE ** (jnp.arange(0, R, 2, dtype=jnp.float32) / R)
        freqs = pos[:, None] * inv_freq[None, :]
        cos = jnp.cos(freqs)[None, :, None, :]
        sin = jnp.sin(freqs)[None, :, None, :]
        q = _rope(q, cos, sin)
        k = _rope(k, cos, sin)
        i = jnp.arange(t)[:, None]
        j = jnp.arange(t)[None, :]
        band = (j >= i - W_LEFT) & (j <= i + W_RIGHT)
        bias = jnp.where(band, 0.0, -jnp.inf).astype(x.dtype)
        scale = np.float32(1.0 / np.sqrt(HD))
        scores = jnp.einsum('nthd,nshd->nhts', q, k) * scale + bias
        probs = jax.nn.softmax(scores, axis=-1)
        attn = jnp.einsum('nhts,nshd->nthd', probs, v).reshape(n, t, D)
        return attn @ w_out.T + b_out

    def _L1_ffn_ref(hidden_states, wi, bi, wo, bo, lora_A, lora_B, gate_w, gate_b):
        import jax, jax.numpy as jnp
        import numpy as np
        B, S, D_MODEL, D_FF, E, R, TOP_K = (4, 256, 128, 512, 8, 16, 2)
        logits = jnp.einsum('bsd,ed->bse', hidden_states, gate_w) + gate_b
        scores = jax.nn.softmax(logits, axis=-1)
        top_v, top_i = jax.lax.top_k(scores, TOP_K)
        val_sum = top_v.sum(axis=-1)
        out = jnp.zeros_like(hidden_states)
        for e in range(E):
            count = (top_i == e).sum(axis=-1).astype(hidden_states.dtype)
            gate = count * val_sum
            inter = jnp.einsum('bsd,fd->bsf', hidden_states, wi) + bi + jnp.einsum('bsr,fr->bsf', jnp.einsum('bsd,rd->bsr', hidden_states, lora_A[e]), lora_B[e])
            h = jax.nn.relu(inter)
            expert_out = jnp.einsum('bsf,df->bsd', h, wo) + bo
            out = out + gate[..., None] * expert_out
        return out

    def _L2_xattn_ref(query, key_value, Wq, bq, Wk, bk, Wv, bv, Wo, bo):
        import jax, jax.numpy as jnp
        import numpy as np
        NUM_HEADS = 16
        CLAMP = 10000.0
        B, Nq, Cq = query.shape
        Nkv = key_value.shape[1]
        H = NUM_HEADS
        D = Cq // H
        scale = D ** (-0.5)
        q = (query @ Wq + bq).reshape(B, Nq, H, D).transpose(0, 2, 1, 3)
        k = (key_value @ Wk + bk).reshape(B, Nkv, H, D).transpose(0, 2, 1, 3)
        v = (key_value @ Wv + bv).reshape(B, Nkv, H, D).transpose(0, 2, 1, 3)
        attn = jnp.einsum('bhqd,bhkd->bhqk', q, k) * scale
        attn = jnp.clip(attn, -CLAMP, CLAMP)
        attn = jax.nn.softmax(attn, axis=-1)
        attn = jnp.where(jnp.any(jnp.isnan(attn)), jnp.asarray(1.0 / Nkv, attn.dtype), attn)
        x = jnp.einsum('bhqk,bhkd->bqhd', attn, v).reshape(B, Nq, Cq)
        return x @ Wo + bo

    def _L2_attn_ref(x, Wq, Wk, Wv, Wo):
        import jax, jax.numpy as jnp
        import numpy as np
        NUM_HEADS = 16
        EPS = 1e-06

        def _phi(x):
            return jax.nn.elu(x) + 1.0
        B, L, D = x.shape
        H = NUM_HEADS
        dh = D // H
        Q = x @ Wq
        K = x @ Wk
        V = x @ Wv
        Qh = Q.reshape(B, L, H, dh).transpose(0, 2, 1, 3)
        Kh = K.reshape(B, L, H, dh).transpose(0, 2, 1, 3)
        Vh = V.reshape(B, L, H, dh).transpose(0, 2, 1, 3)
        Qf = _phi(Qh)
        Kf = _phi(Kh)
        Kv = jnp.einsum('bhlm,bhln->bhmn', Kf, Vh)
        K1 = jnp.sum(Kf, axis=2)
        num = jnp.einsum('bhlm,bhmn->bhln', Qf, Kv)
        den = jnp.einsum('bhlm,bhm->bhl', Qf, K1) + EPS
        out = num / den[..., None]
        out = out.transpose(0, 2, 1, 3).reshape(B, L, D)
        return out @ Wo

    def _L2_ffn_ref(x, w_ln1, Wq, Wkva, Wkvb, Wo, w_ln2, Wgate, expert_bias, Wg, Wu, Wd, sWg, sWu, sWd):
        import jax, jax.numpy as jnp
        import numpy as np
        B, T, C = (2, 256, 128)
        H, D = (16, 64)
        CR = 8
        R = C // CR
        ROPE = D // 2
        NOPE = D - ROPE
        E, K, I, S = (8, 2, 64, 1)
        THETA = 100000.0
        EPS = 1e-05

        def _rmsnorm(x, w):
            rms = jnp.sqrt(jnp.mean(x * x, axis=-1, keepdims=True) + EPS)
            return w * (x / rms)

        def _rope(xh):
            d = xh.shape[-1]
            t = jnp.arange(xh.shape[2], dtype=jnp.float32)
            freqs = 1.0 / THETA ** (jnp.arange(0, d, 2, dtype=jnp.float32) / d)
            ang = jnp.outer(t, freqs)
            cos, sin = (jnp.cos(ang), jnp.sin(ang))
            xr = xh.reshape(xh.shape[:-1] + (d // 2, 2))
            x0, x1 = (xr[..., 0], xr[..., 1])
            rot = jnp.stack([x0 * cos - x1 * sin, x0 * sin + x1 * cos], axis=-1)
            return rot.reshape(xh.shape)

        def _attention(x, Wq, Wkva, Wkvb, Wo):
            b, t, _ = x.shape
            q = (x @ Wq).reshape(b, t, H, D).transpose(0, 2, 1, 3)
            ckv = x @ Wkva
            kv_latent, k_rope = (ckv[:, :, :R], ckv[:, :, R:])
            kv = (kv_latent @ Wkvb).reshape(b, t, H, NOPE).transpose(0, 2, 1, 3)
            k_rope = jnp.broadcast_to(k_rope[:, None, :, :], (b, H, t, ROPE))
            q_nope, q_rope = (q[..., :NOPE], q[..., NOPE:])
            q = jnp.concatenate([q_nope, _rope(q_rope)], axis=-1)
            k = jnp.concatenate([kv, _rope(k_rope)], axis=-1)
            v = jnp.concatenate([kv, jnp.zeros_like(k_rope)], axis=-1)
            att = jnp.einsum('bhqd,bhkd->bhqk', q, k) / jnp.sqrt(jnp.float32(D))
            mask = jnp.tril(jnp.ones((t, t), dtype=bool))
            att = jnp.where(mask, att, jnp.float32(-jnp.inf))
            att = jax.nn.softmax(att, axis=-1)
            y = jnp.einsum('bhqk,bhkd->bhqd', att, v)
            y = y.transpose(0, 2, 1, 3).reshape(b, t, H * D)
            return y @ Wo

        def _experts(x_flat, Wg, Wu, Wd):
            g = jax.nn.silu(jnp.einsum('nc,eci->nei', x_flat, Wg))
            u = jnp.einsum('nc,eci->nei', x_flat, Wu)
            return jnp.einsum('nei,eic->nec', g * u, Wd)

        def _moe(x, Wgate, expert_bias, Wg, Wu, Wd, sWg, sWu, sWd):
            b, t, c = x.shape
            xf = x.reshape(-1, c)
            shared = jnp.mean(_experts(xf, sWg, sWu, sWd), axis=1)
            logits = xf @ Wgate + expert_bias
            probs = jax.nn.softmax(logits, axis=-1)
            topk_p, topk_i = jax.lax.top_k(probs, K)
            topk_p = topk_p / jnp.sum(topk_p, axis=-1, keepdims=True)
            comb = jnp.sum(jax.nn.one_hot(topk_i, E, dtype=xf.dtype) * topk_p[..., None], axis=1)
            routed = jnp.einsum('ne,nec->nc', comb, _experts(xf, Wg, Wu, Wd))
            return (shared + routed).reshape(b, t, c)
        x = x + _attention(_rmsnorm(x, w_ln1), Wq, Wkva, Wkvb, Wo)
        residual = x
        xn = _rmsnorm(x, w_ln2)
        x_out = _moe(xn, Wgate, expert_bias, Wg, Wu, Wd, sWg, sWu, sWd)
        return residual + x_out

    def _L3_xattn_ref(x, y, Wq, bq, Wk, bk, Wv, bv, W1, b1, W2, b2):
        import jax, jax.numpy as jnp
        import numpy as np
        IMAGE_DIM = 128
        TEXT_DIM = 96
        NUM_HEADS = 16
        HEAD_DIM = IMAGE_DIM // NUM_HEADS
        B, N, _ = x.shape
        M = y.shape[1]
        q = (x @ Wq + bq).reshape(B, N, NUM_HEADS, HEAD_DIM)
        k = (y @ Wk + bk).reshape(B, M, NUM_HEADS, HEAD_DIM)
        v = (y @ Wv + bv).reshape(B, M, NUM_HEADS, HEAD_DIM)
        scale = 1.0 / np.sqrt(HEAD_DIM)
        scores = jnp.einsum('bnhd,bmhd->bhnm', q, k) * scale
        attn = jax.nn.softmax(scores, axis=-1)
        out = jnp.einsum('bhnm,bmhd->bnhd', attn, v).reshape(B, N, IMAGE_DIM)
        h = jax.nn.relu(out @ W1 + b1)
        return h @ W2 + b2

    def _L3_attn_ref(x, ln1_w, ln1_b, Wq, Wk, Wv, Wg, Wgk1, Wgk2, bgk2, rms_w, Wo, ln2_w, ln2_b, W1, b1, W2, b2):
        import jax, jax.numpy as jnp
        import numpy as np
        B, T, D = (4, 256, 128)
        H = 4
        K = D
        V = D
        DK = K // H
        DV = V // H
        LOW = 16
        GLN = 16.0

        def _layernorm(x, w, b, eps=1e-05):
            mu = x.mean(-1, keepdims=True)
            xc = x - mu
            var = (xc * xc).mean(-1, keepdims=True)
            return xc * jax.lax.rsqrt(var + eps) * w + b

        def _rmsnorm(x, w, eps=1e-05):
            ms = (x * x).mean(-1, keepdims=True)
            return x * jax.lax.rsqrt(ms + eps) * w

        def _gla_scan(q, k, v, gk):
            scale = DK ** (-0.5)
            qT = jnp.moveaxis(q * scale, 1, 0)
            kT = jnp.moveaxis(k, 1, 0)
            vT = jnp.moveaxis(v, 1, 0)
            gT = jnp.moveaxis(gk, 1, 0)

            def step(h, inp):
                qt, kt, vt, gt = inp
                h = h * jnp.exp(gt)[..., None] + kt[..., :, None] * vt[..., None, :]
                o = jnp.einsum('bhk,bhkv->bhv', qt, h)
                return (h, o)
            h0 = jnp.zeros((q.shape[0], H, DK, DV), q.dtype)
            _, oT = jax.lax.scan(step, h0, (qT, kT, vT, gT))
            return jnp.moveaxis(oT, 0, 1)
        b, t = (x.shape[0], x.shape[1])
        xn = _layernorm(x, ln1_w, ln1_b)
        q = (xn @ Wq).reshape(b, t, H, DK)
        k = (xn @ Wk).reshape(b, t, H, DK)
        v = (xn @ Wv).reshape(b, t, H, DV)
        gk = (jax.nn.log_sigmoid(xn @ Wgk1 @ Wgk2 + bgk2) / GLN).reshape(b, t, H, DK)
        o = _gla_scan(q, k, v, gk)
        g = (xn @ Wg).reshape(b, t, H, DV)
        o = _rmsnorm(o, rms_w) * (g * jax.nn.sigmoid(g))
        o = o.reshape(b, t, V) @ Wo
        x = x + o
        xn2 = _layernorm(x, ln2_w, ln2_b)
        h = jax.nn.leaky_relu(xn2 @ W1 + b1, 0.01)
        h = h * h
        x = x + (h @ W2 + b2)
        return x

    def _L3_ffn_ref(x, gate_w, w_up, w_down, sg_gate, sg_up, sg_down):
        import jax, jax.numpy as jnp
        import numpy as np
        B, T, D = (4, 512, 128)
        E = 8
        TOP_K = 2
        FFN = 384
        HALF = FFN // 2

        def _kaiming_uniform(key, shape, fan_in):
            bound = 1.0 / np.sqrt(fan_in)
            return jax.random.uniform(key, shape, jnp.float32, -bound, bound)
        b, t, d = x.shape
        xf = x.reshape(b * t, d)
        N = xf.shape[0]
        logits = xf @ gate_w.T
        topk_logits, topk_idx = jax.lax.top_k(logits, TOP_K)
        topk_w = jax.nn.softmax(topk_logits.astype(jnp.float32), axis=-1).astype(x.dtype)
        comb = jnp.zeros((N, E), x.dtype).at[jnp.arange(N)[:, None], topk_idx].add(topk_w)
        wg = w_up[:, :HALF, :]
        wu = w_up[:, HALF:, :]
        out = jnp.zeros_like(xf)
        for e in range(E):
            g = xf @ wg[e].T
            u = xf @ wu[e].T
            y = jax.nn.silu(g) * u @ w_down[e].T
            out = out + comb[:, e:e + 1] * y
        shared = jax.nn.silu(xf @ sg_gate.T) * (xf @ sg_up.T) @ sg_down.T
        return (shared + out).reshape(b, t, d)
    x = x + _L0_xattn_ref(_layernorm(x, axis=-1), ctx_768, L0_xattn_Wv, L0_xattn_bv, L0_xattn_Wt, L0_xattn_bt)
    x = x + _L0_attn_ref(_layernorm(x, axis=-1), L0_attn_wq, L0_attn_wk, L0_attn_wv, L0_attn_w1, L0_attn_b1, L0_attn_w2, L0_attn_b2, L0_attn_g1, L0_attn_be1, L0_attn_g2, L0_attn_be2)
    x = x + _L0_ffn_ref(_layernorm(x, axis=-1), L0_ffn_router_weight, L0_ffn_router_bias, L0_ffn_w_gate, L0_ffn_w_up, L0_ffn_w_down)
    x = x + _L1_xattn_ref(ctx_768, _layernorm(x, axis=-1), mask_BxS2_bk0, L1_xattn_ln_x_g, L1_xattn_ln_x_b, L1_xattn_ln_l_g, L1_xattn_ln_l_b, L1_xattn_qn_g, L1_xattn_kn_g, L1_xattn_Wq, L1_xattn_Wkv, L1_xattn_Wlkv, L1_xattn_Wo, L1_xattn_bo)
    x = x + _L1_attn_ref(_layernorm(x, axis=-1), L1_attn_w_qkv, L1_attn_w_out, L1_attn_b_out)
    x = x + _L1_ffn_ref(_layernorm(x, axis=-1), L1_ffn_wi, L1_ffn_bi, L1_ffn_wo, L1_ffn_bo, L1_ffn_lora_A, L1_ffn_lora_B, L1_ffn_gate_w, L1_ffn_gate_b)
    x = x + _L2_xattn_ref(_layernorm(x, axis=-1), ctx_768, L2_xattn_Wq, L2_xattn_bq, L2_xattn_Wk, L2_xattn_bk, L2_xattn_Wv, L2_xattn_bv, L2_xattn_Wo, L2_xattn_bo)
    x = x + _L2_attn_ref(_layernorm(x, axis=-1), L2_attn_Wq, L2_attn_Wk, L2_attn_Wv, L2_attn_Wo)
    x = x + _L2_ffn_ref(_layernorm(x, axis=-1), L2_ffn_w_ln1, L2_ffn_Wq, L2_ffn_Wkva, L2_ffn_Wkvb, L2_ffn_Wo, L2_ffn_w_ln2, L2_ffn_Wgate, L2_ffn_expert_bias, L2_ffn_Wg, L2_ffn_Wu, L2_ffn_Wd, L2_ffn_sWg, L2_ffn_sWu, L2_ffn_sWd)
    x = x + _L3_xattn_ref(_layernorm(x, axis=-1), ctx_768, L3_xattn_Wq, L3_xattn_bq, L3_xattn_Wk, L3_xattn_bk, L3_xattn_Wv, L3_xattn_bv, L3_xattn_W1, L3_xattn_b1, L3_xattn_W2, L3_xattn_b2)
    x = x + _L3_attn_ref(_layernorm(x, axis=-1), L3_attn_ln1_w, L3_attn_ln1_b, L3_attn_Wq, L3_attn_Wk, L3_attn_Wv, L3_attn_Wg, L3_attn_Wgk1, L3_attn_Wgk2, L3_attn_bgk2, L3_attn_rms_w, L3_attn_Wo, L3_attn_ln2_w, L3_attn_ln2_b, L3_attn_W1, L3_attn_b1, L3_attn_W2, L3_attn_b2)
    x = x + _L3_ffn_ref(_layernorm(x, axis=-1), L3_ffn_gate_w, L3_ffn_w_up, L3_ffn_w_down, L3_ffn_sg_gate, L3_ffn_sg_up, L3_ffn_sg_down)
    return x

_drawn_inputs = setup_inputs


def setup_inputs(seed=0):
    import zlib

    import numpy as np

    out = dict(_drawn_inputs(seed))
    spreads = {'L0_attn_b1': (0.0, 0.1),
     'L0_attn_b2': (0.0, 0.1),
     'L0_attn_g1': (1.0, 0.6),
     'L0_attn_be1': (0.0, 0.1),
     'L0_attn_g2': (1.0, 0.2),
     'L0_attn_be2': (0.0, 0.1),
     'L0_ffn_router_bias': (0.0, 0.8),
     'L1_xattn_ln_x_g': (1.0, 0.6),
     'L1_xattn_ln_x_b': (0.0, 0.62),
     'L1_xattn_ln_l_g': (1.0, 0.2),
     'L1_xattn_ln_l_b': (0.0, 0.1),
     'L1_xattn_qn_g': (1.0, 0.6),
     'L1_xattn_kn_g': (1.0, 0.6),
     'L1_xattn_bo': (0.0, 0.1),
     'L2_xattn_bq': (0.0, 0.8),
     'L2_xattn_bk': (0.0, 2.0),
     'L2_xattn_bv': (0.0, 0.1),
     'L2_xattn_bo': (0.0, 0.1),
     'L2_ffn_w_ln1': (1.0, 0.6),
     'L2_ffn_w_ln2': (1.0, 0.6),
     'L2_ffn_expert_bias': (0.0, 0.8),
     'L3_attn_ln1_w': (1.0, 0.6),
     'L3_attn_ln1_b': (0.0, 0.8),
     'L3_attn_bgk2': (0.0, 0.8),
     'L3_attn_rms_w': (1.0, 0.6),
     'L3_attn_ln2_w': (1.0, 0.6),
     'L3_attn_ln2_b': (0.0, 0.8),
     'L3_attn_b1': (0.0, 0.8),
     'L3_attn_b2': (0.0, 2.0)}
    factors = {'L0_xattn_bv': 8.0,
     'L0_xattn_bt': 8.0,
     'L0_attn_wq': 4.871,
     'L0_attn_wk': 2.715,
     'L0_ffn_router_weight': 8.0,
     'L0_ffn_w_gate': 8.0,
     'L0_ffn_w_up': 8.0,
     'L0_ffn_w_down': 8.0,
     'L1_attn_w_qkv': 8.0,
     'L1_attn_w_out': 8.0,
     'L1_attn_b_out': 5.984,
     'L1_ffn_bi': 8.0,
     'L1_ffn_bo': 8.0,
     'L1_ffn_lora_A': 3.052,
     'L1_ffn_lora_B': 3.042,
     'L1_ffn_gate_b': 8.0,
     'L2_attn_Wq': 8.0,
     'L2_attn_Wk': 8.0,
     'L2_attn_Wv': 7.47,
     'L2_attn_Wo': 7.018,
     'L2_ffn_Wq': 8.0,
     'L2_ffn_Wkva': 8.0,
     'L2_ffn_Wkvb': 8.0,
     'L2_ffn_Wo': 8.0,
     'L2_ffn_Wgate': 8.0,
     'L2_ffn_Wg': 8.0,
     'L2_ffn_Wu': 8.0,
     'L2_ffn_Wd': 8.0,
     'L2_ffn_sWg': 8.0,
     'L2_ffn_sWu': 8.0,
     'L2_ffn_sWd': 8.0,
     'L3_xattn_bq': 8.0,
     'L3_xattn_bk': 64.0,
     'L3_xattn_bv': 2.836,
     'L3_xattn_b1': 3.061,
     'L3_xattn_b2': 2.825,
     'L3_attn_Wq': 8.0,
     'L3_attn_Wk': 8.0,
     'L3_attn_Wv': 8.0,
     'L3_attn_Wg': 8.0,
     'L3_attn_Wgk1': 8.0,
     'L3_attn_Wgk2': 8.0,
     'L3_attn_Wo': 8.0,
     'L3_attn_W1': 8.0,
     'L3_attn_W2': 7.543,
     'L3_ffn_gate_w': 3.84,
     'L3_ffn_w_up': 3.335,
     'L3_ffn_w_down': 3.358,
     'L3_ffn_sg_gate': 8.0,
     'L3_ffn_sg_up': 8.0,
     'L3_ffn_sg_down': 8.0}
    for name, (base, spread) in spreads.items():
        noise = np.random.default_rng([zlib.crc32(name.encode()), seed]).standard_normal(out[name].shape)
        drawn = base * np.exp(spread * noise) if base else spread * noise
        out[name] = jnp.asarray(drawn.astype(out[name].dtype))
    for name, factor in factors.items():
        out[name] = (out[name] * factor).astype(out[name].dtype)
    return out
```

```python
from contextlib import ExitStack

import numpy as np
import concourse.bass as bass
from concourse import mybir

F32 = mybir.dt.float32
U8 = mybir.dt.uint8
I32 = mybir.dt.int32
ALU = mybir.AluOpType
ACT = mybir.ActivationFunctionType
AX = mybir.AxisListType.X

P = 128
S = 64
D = 128
CX = 96
SC = 128
TILES = 4
SEQS = 2 * TILES
TOK = TILES * P
CTOK = SEQS * SC
BANK = 512
NEG = -1.0e30
LN_EPS = 1e-5



def chunks(w, rows=P):
    k = w.shape[0] // rows
    return w.reshape(k, rows, w.shape[1]).transpose(1, 0, 2).reshape(rows, k * w.shape[1])


def col(v):
    return v.reshape(-1, P).T if v.size >= P else v.reshape(-1, 1)


def row(v):
    return np.broadcast_to(v.reshape(1, -1), (P, v.size))


def rope_partner(n_heads, width):
    f = np.arange(n_heads * width)
    return f - f % width + (f % width + width // 2) % width


EXPERTS0, HID0 = 16, 64
EXPERTS1, RANK1, FF1 = 8, 16, 512
EXPERTS2, HID2 = 8, 64
EXPERTS3, HID3 = 8, 192


def pad_rows(w, rows):
    return np.concatenate([w, np.zeros((rows - w.shape[0], w.shape[1]), w.dtype)], 0)


def weight_table():
    t = {}
    t["L0x"] = [
        ("wv", P, 64, lambda a: a["L0_xattn_Wv"].T), ("wt", CX, 64, lambda a: a["L0_xattn_Wt"].T),
        ("bv", 64, 1, lambda a: col(a["L0_xattn_bv"])), ("bt", 64, 1, lambda a: col(a["L0_xattn_bt"]))]
    t["L0a"] = [
        ("wq", P, P, lambda a: a["L0_attn_wq"].T),
        ("wk", P, P, lambda a: a["L0_attn_wk"].T), ("wv", P, P, lambda a: a["L0_attn_wv"].T),
        ("w1", P, 512, lambda a: a["L0_attn_w1"].T), ("w2", P, 512, lambda a: chunks(a["L0_attn_w2"].T)),
        ("b1", P, 4, lambda a: col(a["L0_attn_b1"])), ("b2", P, P, lambda a: row(a["L0_attn_b2"])),
        ("g1", P, 1, lambda a: col(a["L0_attn_g1"])), ("be1", P, 1, lambda a: col(a["L0_attn_be1"])),
        ("g2", P, 1, lambda a: col(a["L0_attn_g2"])), ("be2", P, 1, lambda a: col(a["L0_attn_be2"]))]
    t["L0f"] = [
        ("router", P, 16, lambda a: a["L0_ffn_router_weight"].T),
        ("rbias", P, 16, lambda a: row(a["L0_ffn_router_bias"])),
        ("gate", P, 1024, lambda a: a["L0_ffn_w_gate"].reshape(-1, D).T),
        ("up", P, 1024, lambda a: a["L0_ffn_w_up"].reshape(-1, D).T),
        ("down", P, 1024, lambda a: chunks(a["L0_ffn_w_down"].transpose(0, 2, 1).reshape(-1, D)))]
    t["L1x"] = [
        ("wql", P, 384, lambda a: np.concatenate([a["L1_xattn_Wq"].T, a["L1_xattn_Wlkv"].T], 1)),
        ("wkv", CX, 256, lambda a: a["L1_xattn_Wkv"].T), ("wo", P, P, lambda a: a["L1_xattn_Wo"].T),
        ("bo", P, P, lambda a: row(a["L1_xattn_bo"])),
        ("xg", CX, 1, lambda a: col(a["L1_xattn_ln_x_g"])), ("xb", CX, 1, lambda a: col(a["L1_xattn_ln_x_b"])),
        ("lg", P, 1, lambda a: col(a["L1_xattn_ln_l_g"])), ("lb", P, 1, lambda a: col(a["L1_xattn_ln_l_b"])),
        ("qg", P, 1, lambda a: col(np.tile(a["L1_xattn_qn_g"], 2))),
        ("kg", P, 1, lambda a: col(np.tile(a["L1_xattn_kn_g"], 2)))]
    perm8 = rope_partner(16, 8)
    t["L1a"] = [
        ("wq", P, P, lambda a: a["L1_attn_w_qkv"][:D].T), ("wqp", P, P, lambda a: a["L1_attn_w_qkv"][:D][perm8].T),
        ("wk", P, P, lambda a: a["L1_attn_w_qkv"][D:2 * D].T),
        ("wkp", P, P, lambda a: a["L1_attn_w_qkv"][D:2 * D][perm8].T),
        ("wv", P, P, lambda a: a["L1_attn_w_qkv"][2 * D:].T), ("wo", P, P, lambda a: a["L1_attn_w_out"].T),
        ("bo", P, P, lambda a: row(a["L1_attn_b_out"]))]
    t["L1f"] = [
        ("gate", P, 8, lambda a: a["L1_ffn_gate_w"].T), ("gb", P, 8, lambda a: row(a["L1_ffn_gate_b"])),
        ("wi", P, 512, lambda a: a["L1_ffn_wi"].T), ("bi", P, 4, lambda a: col(a["L1_ffn_bi"])),
        ("wo", P, 512, lambda a: chunks(a["L1_ffn_wo"].T)), ("bo", P, P, lambda a: row(a["L1_ffn_bo"])),
        ("la", P, P, lambda a: a["L1_ffn_lora_A"].reshape(-1, D).T),
        ("lb", P, 512, lambda a: a["L1_ffn_lora_B"].transpose(0, 2, 1).reshape(P, 512))]
    t["L2x"] = [
        ("wq", P, P, lambda a: a["L2_xattn_Wq"]), ("wk", CX, P, lambda a: a["L2_xattn_Wk"]),
        ("wv", CX, P, lambda a: a["L2_xattn_Wv"]), ("wo", P, P, lambda a: a["L2_xattn_Wo"]),
        ("bq", P, 1, lambda a: col(a["L2_xattn_bq"])), ("bk", P, 1, lambda a: col(a["L2_xattn_bk"])),
        ("bv", P, P, lambda a: row(a["L2_xattn_bv"])), ("bo", P, P, lambda a: row(a["L2_xattn_bo"]))]
    t["L2a"] = [
        ("wq", P, P, lambda a: a["L2_attn_Wq"]), ("wk", P, P, lambda a: a["L2_attn_Wk"]),
        ("wv", P, P, lambda a: a["L2_attn_Wv"]), ("wo", P, P, lambda a: a["L2_attn_Wo"])]
    pair = np.arange(32) ^ 1
    t["L2f"] = [
        ("g1", P, 1, lambda a: col(a["L2_ffn_w_ln1"])), ("g2", P, 1, lambda a: col(a["L2_ffn_w_ln2"])),
        ("wqn", P, 512, lambda a: a["L2_ffn_Wq"].reshape(D, 16, 64)[:, :, :32].reshape(D, 512)),
        ("wqr", P, 512, lambda a: a["L2_ffn_Wq"].reshape(D, 16, 64)[:, :, 32:].reshape(D, 512)),
        ("wqp", P, 512, lambda a: a["L2_ffn_Wq"].reshape(D, 16, 64)[:, :, 32:][:, :, pair].reshape(D, 512)),
        ("wkl", P, 16, lambda a: a["L2_ffn_Wkva"][:, :16]),
        ("wkr", P, P, lambda a: np.tile(a["L2_ffn_Wkva"][:, 16:], (1, 4))),
        ("wkp", P, P, lambda a: np.tile(a["L2_ffn_Wkva"][:, 16:][:, pair], (1, 4))),
        ("wkvb", 16, 512, lambda a: a["L2_ffn_Wkvb"]),
        ("wo", P, 512, lambda a: chunks(a["L2_ffn_Wo"].reshape(16, 64, D)[:, :32].reshape(512, D))),
        ("router", P, 8, lambda a: a["L2_ffn_Wgate"]), ("rbias", P, 8, lambda a: row(a["L2_ffn_expert_bias"])),
        ("gate", P, 576, lambda a: np.concatenate([a["L2_ffn_Wg"], a["L2_ffn_sWg"]]).transpose(1, 0, 2).reshape(D, 576)),
        ("up", P, 576, lambda a: np.concatenate([a["L2_ffn_Wu"], a["L2_ffn_sWu"]]).transpose(1, 0, 2).reshape(D, 576)),
        ("down", P, 640, lambda a: chunks(pad_rows(np.concatenate([a["L2_ffn_Wd"], a["L2_ffn_sWd"]]).reshape(576, D), 640)))]
    t["L3x"] = [
        ("wq", P, P, lambda a: a["L3_xattn_Wq"]), ("wk", CX, P, lambda a: a["L3_xattn_Wk"]),
        ("wv", CX, P, lambda a: a["L3_xattn_Wv"]), ("bq", P, 1, lambda a: col(a["L3_xattn_bq"])),
        ("bk", P, 1, lambda a: col(a["L3_xattn_bk"])), ("bv", P, P, lambda a: row(a["L3_xattn_bv"])),
        ("w1", P, 256, lambda a: a["L3_xattn_W1"]), ("b1", P, 2, lambda a: col(a["L3_xattn_b1"])),
        ("w2", P, 256, lambda a: chunks(a["L3_xattn_W2"])), ("b2", P, P, lambda a: row(a["L3_xattn_b2"]))]
    t["L3a"] = [
        ("g1", P, 1, lambda a: col(a["L3_attn_ln1_w"])), ("be1", P, 1, lambda a: col(a["L3_attn_ln1_b"])),
        ("g2", P, 1, lambda a: col(a["L3_attn_ln2_w"])), ("be2", P, 1, lambda a: col(a["L3_attn_ln2_b"])),
        ("rms", P, 1, lambda a: col(np.tile(a["L3_attn_rms_w"], 4))),
        ("wq", P, P, lambda a: a["L3_attn_Wq"]), ("wk", P, P, lambda a: a["L3_attn_Wk"]),
        ("wv", P, P, lambda a: a["L3_attn_Wv"]), ("wg", P, P, lambda a: a["L3_attn_Wg"]),
        ("gk1", P, 16, lambda a: a["L3_attn_Wgk1"]), ("gk2", 16, P, lambda a: a["L3_attn_Wgk2"]),
        ("bgk", P, P, lambda a: row(a["L3_attn_bgk2"])), ("wo", P, P, lambda a: a["L3_attn_Wo"]),
        ("w1", P, 384, lambda a: a["L3_attn_W1"]), ("b1", P, 3, lambda a: col(a["L3_attn_b1"])),
        ("w2", P, 384, lambda a: chunks(a["L3_attn_W2"])), ("b2", P, P, lambda a: row(a["L3_attn_b2"]))]
    half = HID3
    t["L3f"] = [
        ("router", P, 8, lambda a: a["L3_ffn_gate_w"].T),
        ("gate", P, 1728, lambda a: np.concatenate([a["L3_ffn_w_up"][:, :half].reshape(-1, D), a["L3_ffn_sg_gate"]]).T),
        ("up", P, 1728, lambda a: np.concatenate([a["L3_ffn_w_up"][:, half:].reshape(-1, D), a["L3_ffn_sg_up"]]).T),
        ("down", P, 1792, lambda a: chunks(pad_rows(np.concatenate(
            [a["L3_ffn_w_down"].transpose(0, 2, 1).reshape(-1, D), a["L3_ffn_sg_down"].T]), 1792)))]
    return t


def weight_places(table):
    places, at = {}, 0
    for block, entries in table.items():
        inside, n = {}, 0
        for name, rows, cols, _ in entries:
            inside[name] = (n, rows, cols)
            n += cols
        places[block] = (at, n, inside)
        at += n
    return places, at


def expert_spread(hidden, experts, total):
    e = np.minimum(np.arange(total) // hidden, experts)
    return (np.arange(experts + 1)[:, None] == e[None, :]).astype(np.float32)


def constant_table():
    p = np.arange(P)
    c = {"ident": np.eye(P), "ones": np.ones((P, P)), "halves": np.full((P, 32), -0.5)}
    c["same16"] = p[:, None] // 16 == p[None, :] // 16
    c["head16"] = p[:, None] // 16 == np.arange(8)[None, :]
    c["same8"] = p[:, None] // 8 == p[None, :] // 8
    c["head8"] = p[:, None] // 8 == np.arange(16)[None, :]
    c["lane4"] = (p[:, None] % 32) // 8 == np.arange(4)[None, :]
    c["parity"] = p[:, None] // 64 == np.arange(16)[None, :] % 2
    c["first"] = np.broadcast_to(16.0 - np.arange(16), (P, 16))
    c["spread0"] = expert_spread(HID0, EXPERTS0, EXPERTS0 * HID0)[:EXPERTS0]
    c["spread1"] = expert_spread(RANK1, EXPERTS1, P)[:EXPERTS1]
    c["spread2"] = expert_spread(HID2, EXPERTS2, 5 * P)
    c["spread3"] = expert_spread(HID3, EXPERTS3, 14 * P)
    pos = np.arange(S, dtype=np.float32)
    inv = (1.0 / np.float32(10000.0) ** (np.arange(0, 8, 2, dtype=np.float32) / np.float32(8))).astype(np.float32)
    ang = (pos[None, :] * inv[p % 4][:, None]).astype(np.float32)
    c["cos8"] = np.cos(ang)
    c["sin8"] = np.sin(ang) * np.where(p % 8 < 4, -1.0, 1.0)[:, None]
    inv = (1.0 / np.float32(100000.0) ** (np.arange(0, 32, 2, dtype=np.float32) / np.float32(32))).astype(np.float32)
    ang = (pos[None, :] * inv[(p % 32) // 2][:, None]).astype(np.float32)
    c["cos32"] = np.cos(ang)
    c["sin32"] = np.sin(ang) * np.where(p % 2 == 0, -1.0, 1.0)[:, None]
    c["causal"] = np.where(np.arange(S)[None, :] <= (p % S)[:, None], 0.0, NEG)
    same = p[:, None] // S == p[None, :] // S
    upto = (p[:, None] <= p[None, :]).astype(np.float64)
    c["decay"] = same * (upto - (p % S < S // 2)[:, None]) / 16.0
    c["past"] = (p % S)[:, None] <= np.arange(S)[None, :]
    return {k: np.asarray(v, np.float32) for k, v in c.items()}



class Lane:

    def __init__(self, nc, engine, name, per_round, chained, idle):
        self.engine, self.name, self.per_round, self.chained = engine, name, per_round, chained
        self.sem = nc.alloc_semaphore(name)
        self.idle = idle
        self.count, self.reached, self.last = 0, {}, None
        self.round_start = None
        engine.sem_inc(self.sem, per_round)

    def wait(self, token):
        lane, count = token
        if self.reached.get(lane.name, -lane.per_round - 1) >= count:
            return False
        self.reached[lane.name] = count
        self.engine.wait_ge(lane.sem, self.round_start * lane.per_round + (lane.per_round + count))
        return True

    def product(self, out, stationary, moving, after=(), **kwargs):
        small = stationary.shape[0] <= 64 and int(np.prod(stationary.shape[1:])) <= 64
        return self.do(self.engine.matmul, out, stationary, moving, after=after, alone=small, **kwargs)

    def do(self, instruction, *args, after=(), alone=False, **kwargs):
        waits = sum(self.wait(token) for token in after)
        if self.chained:
            waits += self.wait((self, self.count))
        if alone and waits:
            self.engine.sem_inc(self.idle, 1)
        self.last = instruction(*args, **kwargs)
        if self.chained:
            return self.mark()
        return None

    def mark(self):
        self.last.then_inc(self.sem, 1)
        self.count += 1
        return (self, self.count)

    def now(self):
        return (self, self.count)

    def previous(self):
        return (self, 0)


class Block:

    def __init__(self, core, name, plan):
        self.core, self.nc, self.name, self.plan = core, core.nc, name, plan
        nc = core.nc
        self.lanes = {}
        for key, engine, chained in (("pe", nc.tensor, False), ("dve", nc.vector, True), ("act", nc.scalar, True),
                                     ("pool", nc.gpsimd, True)):
            self.lanes[key] = Lane(nc, engine, f"{name}_{key}", plan.get((name, key), 1), chained,
                                    core.idle[key])
        self.pe, self.dve, self.act, self.pool = (self.lanes[k] for k in ("pe", "dve", "act", "pool"))

    def weight(self, name):
        at, rows, cols = self.core.places[self.name][2][name]
        return self.core.weight_room[self.name][0:rows, at:at + cols]

    def start_round(self, i):
        for lane in self.lanes.values():
            lane.round_start, lane.count, lane.reached = i, 0, {}
        for lane in self.lanes.values():
            for other in self.lanes.values():
                if other is not lane or lane.chained:
                    lane.wait(other.previous())

    def end_round(self):
        for key, lane in self.lanes.items():
            if lane.count == 0:
                lane.engine.sem_inc(lane.sem, 1)
                lane.count = 1
            if not lane.chained and lane.last is None:
                raise ValueError("an unused lane")
            self.plan[(self.name, key)] = lane.count


class Core:
    pass


def bcast(ap, axis, n):
    return ap.unsqueeze(axis).to_broadcast([*ap.shape[:axis], n, *ap.shape[axis:]])


def layer_norm(b, out, x, eps, scratch, after=()):
    stats, moments, rstd = scratch
    n = x.shape[1]
    for t in range(n):
        b.dve.do(b.nc.vector.bn_stats, stats[:, t, :], x[:, t, :], after=after)
    for t in range(n):
        b.dve.do(b.nc.vector.bn_aggr, moments[:, t, :], stats[:, t, :], alone=True)
    scaled = inverse_root(b, rstd[:, 0:n], moments[:, 0:n, 1], 1.0, eps)
    for t in range(n):
        token = b.dve.do(b.nc.vector.tensor_scalar, out[:, t, :], x[:, t, :], moments[:, t, 0:1], rstd[:, t:t + 1],
                         ALU.subtract, ALU.mult, after=(scaled,))
    return token


def inverse_root(b, out, x, scale, eps, guard=ALU.add):
    summed = b.dve.do(b.nc.vector.tensor_scalar, out, x, scale, eps, ALU.mult, guard)
    return b.pool.do(b.nc.gpsimd.tensor_tensor, out, out, b.core.c["halves"][:, 0:out.shape[1]], ALU.pow,
                     after=(summed,))


def norm_room(nc, ctx, n, name):
    return (ctx.enter_context(nc.sbuf_tensor(f"{name}_stats", [P, n, 6], F32)),
            ctx.enter_context(nc.sbuf_tensor(f"{name}_moments", [P, n, 2], F32)),
            ctx.enter_context(nc.sbuf_tensor(f"{name}_rstd", [P, n], F32)))


def to_features(b, outT, x, bank, after, scale=None, bias=None):
    nc, width = b.nc, x.shape[2]
    done = None
    for first in range(0, x.shape[1], 4):
        n = min(4, x.shape[1] - first)
        room = b.core.psum[:, bank + first // 4, :]
        for t in range(n):
            b.pe.do(nc.tensor.transpose, room[0:width, t * P:(t + 1) * P], x[:, first + t, :], b.core.c["ident"],
                    after=after)
        turned = b.pe.mark()
        src = room[0:width, 0:n * P]
        dst = outT[0:width, first * P:(first + n) * P]
        if scale is None:
            done = b.act.do(nc.scalar.copy, dst, src, after=(turned,))
        else:
            done = b.act.do(nc.scalar.activation, dst, src, ACT.Identity, bias=bias, scale=scale, after=(turned,))
    return done


def down_project(b, out, hT, w, after, rows_of=None):
    n = hT.shape[1]
    for f in range(n):
        rows = P if rows_of is None else rows_of(f)
        for t in range(TILES):
            b.pe.product(out[:, t * P:(t + 1) * P], hT[0:rows, f, t * P:(t + 1) * P],
                    w[0:rows, f * P:(f + 1) * P], start=(f == 0 and t == 0), stop=(f == n - 1),
                    skip_group_check=True, after=after)
    return b.pe.mark()


def pick_largest(b, picked, value, best, weight, first, n_picks, after=()):
    T, E = value.shape[1], value.shape[2]
    nc, dve = b.nc, b.dve
    order = bcast(first[:, 0:E], 1, T)
    token = None
    for r in range(n_picks):
        top = best[:, 0:T]
        dve.do(nc.vector.tensor_reduce, top, value, AX, ALU.max, after=after)
        dve.do(nc.vector.tensor_tensor, weight, value, bcast(top, 2, E), ALU.is_equal)
        dve.do(nc.vector.tensor_tensor, weight, weight, order, ALU.mult)
        dve.do(nc.vector.tensor_reduce, top, weight, AX, ALU.max)
        token = dve.do(nc.vector.tensor_tensor, picked[r], weight, bcast(top, 2, E), ALU.is_equal)
        if r < n_picks - 1:
            dve.do(nc.vector.scalar_tensor_tensor, value, picked[r], NEG, value, ALU.mult, ALU.add)
    return token


def block_L0x(b, i, m):
    nc, psum, c = b.nc, b.core.psum, b.core.c
    x = b.core.x[:, bass.ts(i, TILES), :]
    got_ctx = b.pool.do(nc.gpsimd.tensor_copy, m["ctxT"][:], b.core.ctxT[:, bass.ts(i, CTOK)], alone=True)
    normed = layer_norm(b, m["xn"], x, LN_EPS, m["norm"])
    turned = to_features(b, m["xT"], m["xn"], 0, (normed,))
    for h in range(2):
        b.pe.product(psum[0:64, 2 + h, :], b.weight("wt"), m["ctxT"][:, h * BANK:(h + 1) * BANK],
                start=True, stop=True, after=(got_ctx,))
    pt = b.pe.mark()
    b.pe.product(psum[0:64, 1, :], b.weight("wv"), m["xT"][:], start=True, stop=True, after=(turned,))
    pv = b.pe.mark()
    t_done = b.act.do(nc.scalar.activation, m["tT"][:], psum[0:64, 2:4, :].rearrange("p a b -> p (a b)"), ACT.Identity,
                      bias=b.weight("bt"), scale=1.0, after=(pt,))
    v_done = b.act.do(nc.scalar.activation, m["vT"][:], psum[0:64, 1, :], ACT.Identity, bias=b.weight("bv"), scale=1.0,
                      after=(pv,))
    t_sq = b.pool.do(nc.gpsimd.tensor_tensor, m["t2"][:], m["tT"][:], m["tT"][:], ALU.mult, after=(t_done,))
    v_sq = b.pool.do(nc.gpsimd.tensor_tensor, m["v2"][:], m["vT"][:], m["vT"][:], ALU.mult, after=(v_done,))
    for s in range(SEQS):
        q = slice(64 * (s % 2), 64 * (s % 2) + 64)
        b.pe.product(psum[q, 4, (s // 2) * P:(s // 2 + 1) * P], m["vT"][:, s * S:(s + 1) * S],
                m["tT"][:, s * SC:(s + 1) * SC], start=True, stop=True, after=(v_done, t_done))
    for s in range(SEQS):
        q = slice(64 * (s % 2), 64 * (s % 2) + 64)
        b.pe.product(psum[q, 6, (s // 2) * P:(s // 2 + 1) * P], c["ones"][0:64, 0:64],
                m["t2"][:, s * SC:(s + 1) * SC], start=True, stop=True, after=(t_sq,))
    for t in range(TILES):
        b.pe.product(psum[:, 5, t:t + 1], m["v2"][:, t * P:(t + 1) * P], c["ones"][0:64, 0:1],
                start=True, stop=True, after=(v_sq,))
    pd = b.pe.mark()
    b.dve.do(nc.vector.tensor_copy, m["vn"][:], psum[:, 5, 0:TILES], after=(pd,))
    for t in range(TILES):
        b.dve.do(nc.vector.tensor_scalar, m["r"][:, t, :], psum[:, 6, t * P:(t + 1) * P], m["vn"][:, t:t + 1], 1e-16,
                 ALU.mult, ALU.max)
    scaled = b.act.do(nc.scalar.activation, m["r"][:], m["r"][:], ACT.Sqrt, after=(b.dve.now(),))
    b.dve.do(nc.vector.reciprocal, m["r"][:], m["r"][:], after=(scaled,))
    b.dve.do(nc.vector.tensor_tensor, m["r"][:], m["r"][:], psum[:, 4, :].rearrange("p (t d) -> p t d", t=TILES),
             ALU.mult)
    b.dve.do(nc.vector.tensor_tensor, x, x, m["r"][:], ALU.add)


def room_L0x(nc, ctx):
    sb = lambda n, *shape: ctx.enter_context(nc.sbuf_tensor(f"L0x_{n}", list(shape), F32))
    return {"norm": norm_room(nc, ctx, TILES, "L0x_norm"), "xn": sb("xn", P, TILES, D), "xT": sb("xT", P, TOK),
            "ctxT": sb("ctxT", CX, CTOK), "tT": sb("tT", 64, CTOK), "vT": sb("vT", 64, TOK), "t2": sb("t2", 64, CTOK),
            "v2": sb("v2", 64, TOK), "vn": sb("vn", P, TILES), "r": sb("r", P, TILES, D)}


def phi(b, out, src, low, after):
    nc = b.nc
    cut = b.dve.do(nc.vector.tensor_scalar, low, src, 0.0, None, ALU.min, after=after)
    grown = b.act.do(nc.scalar.activation, low, low, ACT.Exp, after=(cut,))
    return b.dve.do(nc.vector.scalar_tensor_tensor, out, src, 0.0, low, ALU.max, ALU.add, after=(grown,))


def linear_attention(b, m, xT, ready, same, head, heads, eps):
    nc, psum = b.nc, b.core.psum
    b.pe.product(psum[:, 0, :], b.weight("wq"), xT[:], start=True, stop=True, after=(ready,))
    pq = b.pe.mark()
    kv = psum[:, 1:3, :].rearrange("p a (t c) -> p (a t) c", c=256)
    for t in range(TILES):
        b.pe.product(kv[:, t, 0:P], xT[:, t * P:(t + 1) * P], b.weight("wk"), start=True, stop=True)
        b.pe.product(kv[:, t, P:256], xT[:, t * P:(t + 1) * P], b.weight("wv"), start=True, stop=True)
    pkv = b.pe.mark()
    v_done = b.act.do(nc.scalar.copy, m["va"][:, :, 0:P], kv[:, :, P:256], after=(pkv,))
    k_done = phi(b, m["k"][:], kv[:, :, 0:P], m["klow"][:], (v_done,))
    q_done = phi(b, m["qT"][:], psum[:, 0, :], m["qlow"][:], (pq,))
    cross = psum[:, 3:7, :].rearrange("p a (t c) -> p (a t) c", c=256)
    for t in range(TILES):
        for r in range(2):
            q = slice(64 * r, 64 * r + 64)
            b.pe.product(cross[:, r * TILES + t, 0:P + 1], m["k"][q, t, :], m["va"][q, t, :], start=True,
                    stop=True, after=(v_done, k_done))
    pc = b.pe.mark()
    b.dve.do(nc.vector.tensor_tensor, m["kv"][:, :, 0:P], cross[:, :, 0:P], bcast(same, 1, SEQS), ALU.mult, after=(pc,))
    kv_done = b.dve.do(nc.vector.tensor_tensor, m["kv"][:, :, P:P + heads],
                       cross[:, :, P:P + 1].to_broadcast([P, SEQS, heads]), bcast(head, 1, SEQS), ALU.mult)
    for t in range(TILES):
        for r in range(2):
            q = slice(64 * r, 64 * r + 64)
            b.pe.product(kv[q, t, 0:P + heads], m["qT"][:, t * P + 64 * r:t * P + 64 * r + 64],
                    m["kv"][:, r * TILES + t, :], start=True, stop=True, after=(kv_done, q_done))
    po = b.pe.mark()
    b.dve.do(nc.vector.tensor_scalar, m["z"][:], kv[:, :, P:P + heads], eps, None, ALU.add, after=(po,))
    b.dve.do(nc.vector.reciprocal, m["z"][:], m["z"][:])
    out = m["msg"][:].rearrange("p t (h d) -> p t h d", h=heads)
    return b.dve.do(nc.vector.tensor_tensor, out, kv[:, :, 0:P].rearrange("p t (h d) -> p t h d", h=heads),
                    bcast(m["z"][:], 3, P // heads), ALU.mult)


def room_linear(sb, heads):
    return {"qT": sb("qT", P, TOK), "qlow": sb("qlow", P, TOK), "k": sb("k", P, TILES, D), "klow": sb("klow", P, TILES, D),
            "va": sb("va", P, TILES, D + 1), "kv": sb("kv", P, SEQS, D + heads), "z": sb("z", P, TILES, heads),
            "msg": sb("msg", P, TILES, D)}


def block_L0a(b, i, m):
    nc, psum, c = b.nc, b.core.psum, b.core.c
    x = b.core.x[:, bass.ts(i, TILES), :]
    layer_norm(b, m["xin"], x, LN_EPS, m["norm"])
    normed = layer_norm(b, m["x2"], m["xin"], LN_EPS, m["norm"])
    ready = to_features(b, m["xT"], m["x2"], 7, (normed,), b.weight("g1"), b.weight("be1"))
    linear_attention(b, m, m["xT"], ready, c["same16"], c["head16"], 8, 1e-6)
    b.dve.do(nc.vector.tensor_tensor, m["xin"][:], m["xin"][:], m["msg"][:], ALU.add)
    normed = layer_norm(b, m["x2"], m["xin"], LN_EPS, m["norm"])
    ready = to_features(b, m["xT"], m["x2"], 7, (normed,), b.weight("g2"), b.weight("be2"))
    biased = b.pool.do(nc.gpsimd.tensor_tensor, m["xin"][:], m["xin"][:], bcast(b.weight("b2"), 1, TILES), ALU.add,
                       after=(normed,))
    for f in range(4):
        b.pe.product(psum[:, 3 + f, :], b.weight("w1")[:, f * P:(f + 1) * P], m["xT"][:], start=True,
                stop=True, after=(ready,))
        grown = b.act.do(nc.scalar.activation, m["hT"][:, f, :], psum[:, 3 + f, :], ACT.Gelu, bias=b.weight("b1")[:, f:f + 1],
                         scale=1.0, after=(b.pe.mark(),))
    down = down_project(b, psum[:, 0, :], m["hT"], b.weight("w2"), (grown,))
    b.dve.do(nc.vector.tensor_tensor, m["xin"][:], m["xin"][:], psum[:, 0, :].rearrange("p (t d) -> p t d", t=TILES),
             ALU.add, after=(down, biased))
    b.dve.do(nc.vector.tensor_tensor, x, x, m["xin"][:], ALU.add)


def room_L0a(nc, ctx):
    sb = lambda n, *shape: ctx.enter_context(nc.sbuf_tensor(f"L0a_{n}", list(shape), F32))
    m = {"norm": norm_room(nc, ctx, TILES, "L0a_norm"), "xin": sb("xin", P, TILES, D), "x2": sb("x2", P, TILES, D),
         "xT": sb("xT", P, TOK), "hT": sb("hT", P, 4, TOK)}
    m.update(room_linear(sb, 8))
    return m


def once_ones(b, m):
    b.nc.vector.memset(m["va"][:, :, D:D + 1], 1.0)


def experts(b, m, xT, combT, spread, hidden, out_bank, after):
    nc, psum = b.nc, b.core.psum
    n = -(-hidden // P)
    finished = []
    for f in range(n):
        rows = min(P, hidden - f * P)
        banks = (1, 2, 3) if f % 2 == 0 else (4, 5, 6)
        cols = slice(f * P, f * P + rows)
        free = (finished[f - 2],) if f >= 2 else ()
        b.pe.product(psum[0:rows, banks[0], :], b.weight("gate")[:, cols], xT[:], start=True, stop=True,
                after=(*after, *free))
        pg = b.pe.mark()
        b.pe.product(psum[0:rows, banks[1], :], b.weight("up")[:, cols], xT[:], start=True, stop=True)
        b.pe.product(psum[0:rows, banks[2], :], spread[:, cols], combT, start=True, stop=True)
        pc = b.pe.mark()
        if f >= 2:
            b.act.wait(down[f - 2])
        s_done = b.act.do(nc.scalar.activation, m["h"][0:rows, f % 2, :], psum[0:rows, banks[0], :], ACT.Silu, after=(pg,))
        h = m["h"][0:rows, f % 2, :]
        b.dve.do(nc.vector.tensor_tensor, h, h, psum[0:rows, banks[1], :], ALU.mult, after=(s_done, pc))
        finished.append(b.dve.do(nc.vector.tensor_tensor, h, h, psum[0:rows, banks[2], :], ALU.mult))
        if f == 0:
            down = []
        if f >= 1:
            down.append(expert_down(b, m, f - 1, n, hidden, out_bank, finished[f - 1]))
    down.append(expert_down(b, m, n - 1, n, hidden, out_bank, finished[n - 1]))
    return down[-1]


def expert_down(b, m, f, n, hidden, out_bank, ready):
    rows = min(P, hidden - f * P)
    for t in range(TILES):
        b.pe.product(b.core.psum[:, out_bank, t * P:(t + 1) * P], m["h"][0:rows, f % 2, t * P:(t + 1) * P],
                b.weight("down")[0:rows, f * P:(f + 1) * P], start=(f == 0 and t == 0), stop=(f == n - 1),
                skip_group_check=True, after=(ready,))
    return b.pe.mark()


def turn_combine(b, m, comb, experts_n, bank, after, out=None, free=()):
    nc = b.nc
    for t in range(TILES):
        b.pe.do(nc.tensor.transpose, b.core.psum[0:experts_n, bank, t * P:(t + 1) * P], comb[:, t, :], b.core.c["ident"],
                after=(*after, *free))
    return b.act.do(nc.scalar.copy, m["combT"][:] if out is None else out, b.core.psum[0:experts_n, bank, :], after=(b.pe.mark(),))


def logits_of(b, xT, w, n, bank, after):
    out = b.core.psum[:, bank, 0:TILES * n].rearrange("p (t e) -> p t e", t=TILES)
    for t in range(TILES):
        b.pe.product(out[:, t, :], xT[:, t * P:(t + 1) * P], w, start=True, stop=True, after=after)
    return out, b.pe.mark()


def block_L0f(b, i, m):
    nc, psum, c = b.nc, b.core.psum, b.core.c
    x = b.core.x[:, bass.ts(i, TILES), :]
    normed = layer_norm(b, m["xn"], x, LN_EPS, m["norm"])
    ready = to_features(b, m["xT"], m["xn"], 0, (normed,))
    logits, pl = logits_of(b, m["xT"], b.weight("router"), EXPERTS0, 7, (ready,))
    scored = b.act.do(nc.scalar.activation, m["score"][:], logits, ACT.Sigmoid, after=(pl,))
    dve, tt = b.dve, nc.vector.tensor_tensor
    dve.do(tt, m["choice"][:], m["score"][:], bcast(b.weight("rbias"), 1, TILES), ALU.add, after=(scored,))
    pair = m["choice"][:].rearrange("p t (g a c) -> p (t g) a c", g=4, a=2)
    hi, lo, a1, a2, gs = (m[k][:] for k in ("hi", "lo", "a1", "a2", "gs"))
    dve.do(tt, hi, pair[:, :, :, 0], pair[:, :, :, 1], ALU.max)
    dve.do(tt, lo, pair[:, :, :, 0], pair[:, :, :, 1], ALU.min)
    dve.do(tt, a1, hi[:, :, 0], hi[:, :, 1], ALU.max)
    dve.do(tt, a2, hi[:, :, 0], hi[:, :, 1], ALU.min)
    dve.do(tt, gs, lo[:, :, 0], lo[:, :, 1], ALU.max)
    dve.do(tt, gs, gs, a2, ALU.max)
    dve.do(tt, gs, gs, a1, ALU.add)
    groups = [m["pick"][:, r, :, 0:4] for r in range(2)]
    pick_largest(b, groups, gs.rearrange("p (t g) -> p t g", g=4), m["best"], m["w"][:, :, 0:4], c["first"], 2)
    dve.do(tt, groups[0], groups[0], groups[1], ALU.add)
    gmask = m["gmask"][:]
    dve.do(nc.vector.tensor_copy, gmask.rearrange("p t (g e) -> p t g e", g=4), bcast(groups[0], 3, 4))
    dve.do(tt, m["choice"][:], m["choice"][:], gmask, ALU.mult)
    dve.do(nc.vector.tensor_scalar, gmask, gmask, 1.0, 1e9, ALU.subtract, ALU.mult)
    dve.do(tt, m["choice"][:], m["choice"][:], gmask, ALU.add)
    picks = [m["pick"][:, r, :, :] for r in range(4)]
    pick_largest(b, picks, m["choice"][:], m["best"], m["w"][:], c["first"], 4)
    for r in range(1, 4):
        dve.do(tt, picks[0], picks[0], picks[r], ALU.add)
    dve.do(tt, m["w"][:], picks[0], m["score"][:], ALU.mult)
    dve.do(nc.vector.tensor_reduce, m["best"][:], m["w"][:], AX, ALU.add)
    dve.do(nc.vector.tensor_scalar, m["best"][:], m["best"][:], 1e-20, None, ALU.add)
    dve.do(nc.vector.reciprocal, m["best"][:], m["best"][:])
    combined = dve.do(nc.vector.scalar_tensor_tensor, m["w"][:], m["w"][:], 2.5, bcast(m["best"][:], 2, EXPERTS0),
                      ALU.mult, ALU.mult)
    comb_ready = turn_combine(b, m, m["w"], EXPERTS0, 7, (combined,))
    done = experts(b, m, m["xT"], m["combT"][:], c["spread0"], EXPERTS0 * HID0, 0, (comb_ready,))
    dve.do(tt, x, x, psum[:, 0, :].rearrange("p (t d) -> p t d", t=TILES), ALU.add, after=(done,))


def room_L0f(nc, ctx):
    sb = lambda n, *shape: ctx.enter_context(nc.sbuf_tensor(f"L0f_{n}", list(shape), F32))
    return {"norm": norm_room(nc, ctx, TILES, "L0f_norm"), "xn": sb("xn", P, TILES, D), "xT": sb("xT", P, TOK),
            "score": sb("score", P, TILES, 16), "choice": sb("choice", P, TILES, 16), "gmask": sb("gmask", P, TILES, 16),
            "hi": sb("hi", P, 4 * TILES, 2), "lo": sb("lo", P, 4 * TILES, 2), "a1": sb("a1", P, 4 * TILES),
            "a2": sb("a2", P, 4 * TILES), "gs": sb("gs", P, 4 * TILES), "pick": sb("pick", P, 4, TILES, 16),
            "best": sb("best", P, TILES), "w": sb("w", P, TILES, 16), "combT": sb("combT", 16, TOK),
            "h": sb("h", P, 2, TOK)}


def block_L1x(b, i, m):
    nc, psum, c = b.nc, b.core.psum, b.core.c
    dve, act, pool, pe = b.dve, b.act, b.pool, b.pe
    tt = nc.vector.tensor_tensor
    x = b.core.x[:, bass.ts(i, TILES), :]
    heads, width, keys = 2, 64, SC + S
    normed = layer_norm(b, m["cn"], m["ctx"][:, bass.ts(i, SEQS), :], LN_EPS, m["norm8"])
    c_ready = to_features(b, m["cT"], m["cn"], 0, (normed,), b.weight("xg"), b.weight("xb"))
    layer_norm(b, m["xn"], x, LN_EPS, m["norm"])
    normed = layer_norm(b, m["xn"], m["xn"], LN_EPS, m["norm"])
    l_ready = to_features(b, m["lT"], m["xn"], 2, (normed,), b.weight("lg"), b.weight("lb"))
    wql = b.weight("wql")
    qk = psum[:, 3:5, :].rearrange("p a (t c) -> p (a t) c", c=256)
    for t in range(TILES):
        pe.product(qk[:, t, :], m["lT"][:, t * P:(t + 1) * P], wql[:, 0:256], start=True, stop=True, after=(l_ready,))
    p_qk = pe.mark()
    for s in range(SEQS):
        pe.product(psum[0:64, 5 + s // 4, (s % 4) * P:(s % 4 + 1) * P], m["lT"][:, s * S:(s + 1) * S], wql[:, 256:384],
                   start=True, stop=True)
    p_v = pe.mark()
    qk_done = act.do(nc.scalar.copy, m["qk"][:], qk, after=(p_qk,))
    vl_done = act.do(nc.scalar.copy, m["vl"][:].rearrange("p s d -> p (s d)"),
                     psum[0:64, 5:7, :].rearrange("p a b -> p (a b)"), after=(p_v,))
    kv = psum[:, 3:7, :].rearrange("p a (s c) -> p (a s) c", c=256)
    for s in range(SEQS):
        pe.product(kv[:, s, :], m["cT"][:, s * SC:(s + 1) * SC], b.weight("wkv"), start=True, stop=True,
                   after=(c_ready, qk_done, vl_done))
    kv_done = act.do(nc.scalar.copy, m["kv"][:], kv, after=(pe.mark(),))
    squares = pool.do(nc.gpsimd.tensor_tensor, m["sq"][:, 0:TILES, :], m["qk"][:], m["qk"][:], ALU.mult, after=(qk_done,))
    dve.do(nc.vector.tensor_reduce, m["ss"][:], m["sq"][:, 0:TILES, :].rearrange("p t (h d) -> p (t h) d", h=4), AX,
           ALU.add, after=(squares,))
    scaled = inverse_root(b, m["ss"][:], m["ss"][:], 1.0 / width, 1e-16, ALU.max)
    view = m["qk"][:].rearrange("p t (h d) -> p (t h) d", h=4)
    qk_normed = dve.do(tt, view, view, bcast(m["ss"][:], 2, width), ALU.mult, after=(scaled,))
    csq = m["sq"][:].rearrange("p t (a c) -> p (t a) c", a=2)
    squares = pool.do(nc.gpsimd.tensor_tensor, csq, m["kv"][:, :, 0:P], m["kv"][:, :, 0:P], ALU.mult,
                      after=(kv_done, qk_normed))
    dve.do(nc.vector.tensor_reduce, m["css"][:], csq.rearrange("p s (h d) -> p s h d", h=heads), AX, ALU.add,
           after=(squares,))
    scaled = inverse_root(b, m["css"][:].rearrange("p s h -> p (s h)"), m["css"][:].rearrange("p s h -> p (s h)"),
                          1.0 / width, 1e-16, ALU.max)
    kview = m["kv"][:, :, 0:P].rearrange("p s (h d) -> p s h d", h=heads)
    k_normed = dve.do(tt, kview, kview, bcast(m["css"][:], 3, width), ALU.mult, after=(scaled,))
    q_ready = to_features(b, m["qT"], m["qk"][:, :, 0:P], 0, (qk_normed,), b.weight("qg"), 0.0)
    kl_ready = to_features(b, m["klT"], m["qk"][:, :, P:256], 1, (), b.weight("kg"), 0.0)
    kc_ready = to_features(b, m["kcT"], m["kv"][:, :, 0:P], 3, (k_normed, kv_done), b.weight("kg"), 0.0)
    for s in range(SEQS):
        t, r = s // 2, s % 2
        for h in range(heads):
            f = slice(width * h, width * h + width)
            out = psum[64 * r:64 * r + 64, 2 * h + t // 2, (t % 2) * keys:(t % 2) * keys + keys]
            pe.product(out[:, 0:SC], m["qT"][f, s * S:(s + 1) * S], m["kcT"][f, s * SC:(s + 1) * SC], start=True,
                       stop=True, after=(q_ready, kl_ready, kc_ready))
            pe.product(out[:, SC:keys], m["qT"][f, s * S:(s + 1) * S], m["klT"][f, s * S:(s + 1) * S], start=True,
                       stop=True)
    p_s = pe.mark()
    dve.do(nc.vector.tensor_scalar, m["mb"][:], m["mask"][:, bass.ts(i, TILES), :].bitcast(U8), 1.0, 3.0e38, ALU.subtract, ALU.mult)
    mb = m["mb"][:].rearrange("p (a t) k -> p a t k", a=2)
    for h in range(heads):
        src = psum[:, 2 * h:2 * h + 2, 0:2 * keys].rearrange("p a (t k) -> p a t k", k=keys)
        dst = m["p"][:, h, :, :].rearrange("p (a t) k -> p a t k", a=2)
        added = dve.do(tt, dst[:, :, :, 0:SC], src[:, :, :, 0:SC], mb, ALU.add, after=(p_s,))
        copied = act.do(nc.scalar.copy, dst[:, :, :, SC:keys], src[:, :, :, SC:keys], after=(added,))
    prob = m["p"][:].rearrange("p h t k -> p (h t) k")
    dve.do(nc.vector.tensor_reduce, m["mx"][:], prob, AX, ALU.max, after=(copied,))
    lowered = dve.do(tt, prob, prob, bcast(m["mx"][:], 2, keys), ALU.subtract)
    grown = act.do(nc.scalar.activation, prob, prob, ACT.Exp, scale=width ** -0.5, after=(lowered,))
    dve.do(nc.vector.tensor_reduce, m["mx"][:], prob, AX, ALU.add, after=(grown,))
    dve.do(nc.vector.reciprocal, m["mx"][:], m["mx"][:])
    p_done = dve.do(tt, prob, prob, bcast(m["mx"][:], 2, keys), ALU.mult)
    for n in range(heads * TILES):
        pe.do(nc.tensor.transpose, psum[:, 4 + n // 4, (n % 4) * P:(n % 4 + 1) * P], prob[:, n, 0:SC], c["ident"],
              after=(p_done,))
    p_c = pe.mark()
    for n in range(heads * TILES):
        pe.do(nc.tensor.transpose, psum[0:64, 6 + n // 4, (n % 4) * P:(n % 4 + 1) * P], prob[:, n, SC:keys], c["ident"])
    p_l = pe.mark()
    pc_done = act.do(nc.scalar.copy, m["pcT"][:], psum[:, 4:6, :].rearrange("p a b -> p (a b)"), after=(p_c,))
    pl_done = dve.do(nc.vector.tensor_copy, m["plT"][:], psum[0:64, 6:8, :].rearrange("p a b -> p (a b)"), after=(p_l,))
    for s in range(SEQS):
        t, r = s // 2, s % 2
        for h in range(heads):
            f = slice(width * h, width * h + width)
            q = slice((h * TILES + t) * P + 64 * r, (h * TILES + t) * P + 64 * r + 64)
            pe.product(psum[f, 0, s * S:(s + 1) * S], m["kv"][:, s, P + width * h:P + width * h + width],
                       m["pcT"][:, q], start=True, stop=False, skip_group_check=True, after=(pc_done, pl_done))
            pe.product(psum[f, 0, s * S:(s + 1) * S], m["vl"][:, s, f], m["plT"][:, q], start=False, stop=True,
                       skip_group_check=True)
    o_done = act.do(nc.scalar.copy, m["oT"][:], psum[:, 0, :], after=(pe.mark(),))
    project_out(b, x, m["oT"], b.weight("wo"), b.weight("bo"), 1, (o_done,))


def project_out(b, x, inT, w, bias, bank, after):
    nc = b.nc
    if bias is not None:
        b.dve.do(nc.vector.tensor_tensor, x, x, bcast(bias, 1, TILES), ALU.add)
    for t in range(TILES):
        b.pe.product(b.core.psum[:, bank, t * P:(t + 1) * P], inT[:, t * P:(t + 1) * P], w, start=True, stop=True,
                     after=after)
    return b.dve.do(nc.vector.tensor_tensor, x, x, b.core.psum[:, bank, :].rearrange("p (t d) -> p t d", t=TILES), ALU.add,
                    after=(b.pe.mark(),))


def room_L1x(nc, ctx):
    sb = lambda n, *shape: ctx.enter_context(nc.sbuf_tensor(f"L1x_{n}", list(shape), F32))
    return {"norm": norm_room(nc, ctx, TILES, "L1x_norm"), "norm8": norm_room(nc, ctx, SEQS, "L1x_norm8"),
            "ctx": ctx.enter_context(nc.sbuf_tensor("L1x_ctx", [P, ROUND["n_seq"], CX], F32)),
            "mask": ctx.enter_context(nc.sbuf_tensor("L1x_mask", [P, ROUND["n_seq"] // 2, SC // 4], I32)),
            "cn": sb("cn", P, SEQS, CX), "cT": sb("cT", CX, CTOK), "xn": sb("xn", P, TILES, D), "lT": sb("lT", P, TOK),
            "qk": sb("qk", P, TILES, 256), "vl": sb("vl", 64, SEQS, P), "kv": sb("kv", P, SEQS, 256),
            "sq": sb("sq", P, TILES, 256), "ss": sb("ss", P, 4 * TILES), "css": sb("css", P, SEQS, 2),
            "qT": sb("qT", P, TOK), "klT": sb("klT", P, TOK), "kcT": sb("kcT", P, CTOK), "mb": sb("mb", P, TILES, SC),
            "p": sb("p", P, 2, TILES, SC + S), "mx": sb("mx", P, 2 * TILES), "pcT": sb("pcT", P, CTOK),
            "plT": sb("plT", 64, CTOK), "oT": sb("oT", P, TOK)}


def once_L1x(b, m):
    nc = b.nc
    arrived = nc.alloc_semaphore("L1x_inputs")
    nc.sync.dma_start(m["ctx"][:], b.core.ctx_tok).then_inc(arrived, 16)
    pairs = b.core.mask.rearrange("(t r) k -> r t k", r=2)
    for r in range(2):
        nc.sync.dma_start(m["mask"][64 * r:64 * r + 64, :, :], pairs[r].unsqueeze(0).to_broadcast(
            [64, ROUND["n_seq"] // 2, SC // 4])).then_inc(arrived, 16)
    nc.vector.wait_ge(arrived, 48)



HEADS, WIDTH, QUAD = 16, 8, 4


def split_heads(b, kx, kT, ready):
    nc, c = b.nc, b.core.c
    for j in range(QUAD):
        done = b.dve.do(nc.vector.tensor_scalar, kx[:, j, :], kT[:], c["lane4"][:, j:j + 1], None, ALU.mult, after=ready)
    return done


def attention_waves(b, m, keys, scale, clip, ready):
    nc, psum, c = b.nc, b.core.psum, b.core.c
    dve, act, pe = b.dve, b.act, b.pe
    tiles = P // keys
    waves = TILES // tiles
    per_block = P // keys
    n_rows = QUAD * tiles * QUAD
    lowered, turned_free = {}, None

    def scores(w):
        free = (lowered[w - 1],) if w else ()
        for u in range(tiles):
            for r in range(2):
                s = 2 * (w * tiles + u) + r
                for g in range(QUAD):
                    f = slice(32 * g, 32 * g + 32)
                    out = psum[64 * r:64 * r + 64, g, u * QUAD * keys:(u + 1) * QUAD * keys]
                    pe.product(out.rearrange("p (j k) -> p j k", j=QUAD), m["qT"][f, s * S:(s + 1) * S],
                               m["kx"][f, :, s * keys:(s + 1) * keys], start=True, stop=True, after=(*ready, *free))
        return pe.mark()

    def soften(w, p_s):
        p = m["p"][:, w % 2, :].rearrange("p (n k) -> p n k", k=keys)
        s = psum[:, 0:4, :].rearrange("p a (n k) -> p (a n) k", k=keys)
        if clip is not None:
            lowered[w] = dve.do(nc.vector.tensor_scalar, p, s, clip / scale, -clip / scale, ALU.min, ALU.max,
                                after=(p_s,))
            s = p
        dve.do(nc.vector.tensor_reduce, m["mx"][:, 0:n_rows], s, AX, ALU.max, after=(p_s,))
        low = dve.do(nc.vector.tensor_tensor, p, s, bcast(m["mx"][:, 0:n_rows], 2, keys), ALU.subtract)
        if clip is None:
            lowered[w] = low
        return act.do(nc.scalar.activation, p, p, ACT.Exp, scale=scale, after=(low,))

    def apply(w, grown, free):
        p = m["p"][:, w % 2, :]
        for n in range(16):
            pe.do(nc.tensor.transpose, psum[:, 4 + n // 4, (n % 4) * P:(n % 4 + 1) * P], p[:, n * P:(n + 1) * P],
                  c["ident"], after=(grown, *free))
        turned = pe.mark()
        pT = m["pT"][:].rearrange("p (a b) -> p a b", a=4)
        e0 = act.do(nc.scalar.copy, pT[:, 0:2, :], psum[:, 4:6, :], after=(turned,))
        e1 = dve.do(nc.vector.tensor_copy, pT[:, 2:4, :], psum[:, 6:8, :], after=(turned,))
        one = WIDTH + 1
        for u in range(tiles):
            for r in range(2):
                s = 2 * (w * tiles + u) + r
                for g in range(QUAD):
                    for k in range(QUAD // per_block):
                        n = (g * tiles + u) * (QUAD // per_block) + k
                        h = QUAD * g + per_block * k
                        pe.product(psum[64 * r:64 * r + 64, 4, (u * HEADS + h) * one:(u * HEADS + h + per_block) * one],
                                   m["pT"][:, n * P + 64 * r:n * P + 64 * r + 64],
                                   m["va"][:, s, h * one:(h + per_block) * one], start=True, stop=True, after=(e0, e1))
        p_o = pe.mark()
        out = psum[:, 4, 0:tiles * HEADS * one].rearrange("p (u h e) -> p u h e", u=tiles, h=HEADS)
        z = m["z"][:, 0:tiles, :]
        dve.do(nc.vector.reciprocal, z, out[:, :, :, WIDTH], after=(p_o,))
        att = m["att"][:, w * tiles:(w + 1) * tiles, :].rearrange("p u (h d) -> p u h d", h=HEADS)
        return dve.do(nc.vector.tensor_tensor, att, out[:, :, :, 0:WIDTH], bcast(z, 3, WIDTH), ALU.mult)

    grown = soften(0, scores(0))
    done = ()
    for w in range(waves):
        nxt = soften(w + 1, scores(w + 1)) if w + 1 < waves else None
        done = (apply(w, grown, done),)
        grown = nxt
    return done[0]


def room_attention(sb, keys):
    return {"xn": sb("xn", P, TILES, D), "xT": sb("xT", P, TOK), "qT": sb("qT", P, TOK), "kT": sb("kT", P, SEQS * keys),
            "kx": sb("kx", P, QUAD, SEQS * keys), "va": sb("va", P, SEQS, HEADS * (WIDTH + 1)), "p": sb("p", P, 2, 2048),
            "pT": sb("pT", P, 2048), "mx": sb("mx", P, 32), "z": sb("z", P, 2, HEADS), "att": sb("att", P, TILES, D)}


def rotate(b, out, src, partner, cos, sin, twin, after):
    nc = b.nc
    seqs = lambda ap: ap.rearrange("p (s k) -> p s k", k=S)
    b.dve.do(nc.vector.tensor_tensor, seqs(out), seqs(src), bcast(cos, 1, SEQS), ALU.mult, after=after)
    both = b.dve.do(nc.vector.tensor_tensor, seqs(twin), seqs(partner), bcast(sin, 1, SEQS), ALU.mult)
    return b.pool.do(nc.gpsimd.tensor_tensor, out, out, twin, ALU.add, after=(both,))


def block_L1a(b, i, m):
    nc, psum, c = b.nc, b.core.psum, b.core.c
    x = b.core.x[:, bass.ts(i, TILES), :]
    normed = layer_norm(b, m["xn"], x, LN_EPS, m["norm"])
    ready = to_features(b, m["xT"], m["xn"], 7, (normed,))
    for n, w in enumerate(("wk", "wkp", "wq", "wqp")):
        b.pe.product(psum[:, n, :], b.weight(w), m["xT"][:], start=True, stop=True, after=(ready,))
    pq = b.pe.mark()
    twice = b.pool.do(nc.gpsimd.tensor_copy, m["x2"][:], bcast(m["xT"][:].rearrange("p (s k) -> p s k", k=S), 2, 2),
                      after=(ready,), alone=True)
    for s in range(SEQS):
        b.pe.product(psum[:, 4 + s // 4, (s % 4) * P:(s % 4 + 1) * P], m["x2"][:, s, :, :].rearrange("p a k -> p (a k)"),
                     b.weight("wv"), start=True, stop=True, after=(twice,))
    pv = b.pe.mark()
    k_ready = rotate(b, m["kT"][:], psum[:, 0, :], psum[:, 1, :], c["cos8"], c["sin8"], m["twin"][:], (pq,))
    q_ready = rotate(b, m["qT"][:], psum[:, 2, :], psum[:, 3, :], c["cos8"], c["sin8"], m["twin2"][:], ())
    va = m["va"][:].rearrange("p s (h e) -> p s h e", h=HEADS)
    v_ready = b.dve.do(nc.vector.tensor_tensor, va[:, :, :, 0:WIDTH].rearrange("p s h d -> p (s h) d"),
                       psum[:, 4:6, :].rearrange("p a (n d) -> p (a n) d", d=WIDTH),
                       bcast(m["par"][:], 2, WIDTH), ALU.mult, after=(pv,))
    split = split_heads(b, m["kx"], m["kT"], (k_ready,))
    done = attention_waves(b, m, S, WIDTH ** -0.5, None, (split, q_ready, v_ready))
    turned = to_features(b, m["xT"], m["att"], 5, (done,))
    project_out(b, x, m["xT"], b.weight("wo"), b.weight("bo"), 6, (turned,))


def room_L1a(nc, ctx):
    sb = lambda n, *shape: ctx.enter_context(nc.sbuf_tensor(f"L1a_{n}", list(shape), F32))
    return {"norm": norm_room(nc, ctx, TILES, "L1a_norm"), **room_attention(sb, S), "twin": sb("twin", P, TOK),
            "x2": sb("x2", P, SEQS, 2, S), "twin2": sb("twin2", P, TOK), "par": sb("par", P, SEQS * HEADS)}


def once_L1a(b, m):
    nc, parity = b.nc, b.core.c["parity"]
    ones = m["va"][:].rearrange("p s (h e) -> p s h e", h=HEADS)[:, :, :, WIDTH]
    nc.vector.tensor_copy(ones, bcast(parity, 1, SEQS))
    nc.vector.tensor_copy(m["par"][:].rearrange("p (s h) -> p s h", s=SEQS), bcast(parity, 1, SEQS))


def context_attention(b, i, m, clip):
    nc, psum = b.nc, b.core.psum
    x = b.core.x[:, bass.ts(i, TILES), :]
    got = b.pool.do(nc.gpsimd.tensor_copy, m["ctxT"][:], b.core.ctxT[:, bass.ts(i, CTOK)], alone=True)
    normed = layer_norm(b, m["xn"], x, LN_EPS, m["norm"])
    for h in range(2):
        b.pe.product(psum[:, h, :], b.weight("wk"), m["ctxT"][:, h * BANK:(h + 1) * BANK], start=True, stop=True,
                     after=(got,))
    pk = b.pe.mark()
    for s in range(SEQS):
        b.pe.product(psum[:, 2 + s // 4, (s % 4) * P:(s % 4 + 1) * P], m["ctxT"][:, s * SC:(s + 1) * SC],
                     b.weight("wv"), start=True, stop=True)
    pv = b.pe.mark()
    k_ready = b.act.do(nc.scalar.activation, m["kT"][:].rearrange("p (a b) -> p a b", a=2), psum[:, 0:2, :], ACT.Identity,
                       bias=b.weight("bk"), scale=1.0, after=(pk,))
    ready = to_features(b, m["xT"], m["xn"], 7, (normed,))
    b.pe.product(psum[:, 6, :], b.weight("wq"), m["xT"][:], start=True, stop=True, after=(ready,))
    q_ready = b.act.do(nc.scalar.activation, m["qT"][:], psum[:, 6, :], ACT.Identity, bias=b.weight("bq"), scale=1.0,
                       after=(b.pe.mark(),))
    va = m["va"][:].rearrange("p s (h e) -> p s h e", h=HEADS)
    v_ready = b.dve.do(nc.vector.tensor_tensor, va[:, :, :, 0:WIDTH],
                       psum[:, 2:4, :].rearrange("p a (s h d) -> p (a s) h d", h=HEADS, d=WIDTH),
                       bcast(b.weight("bv").rearrange("p (h d) -> p h d", h=HEADS), 1, SEQS), ALU.add, after=(pv,))
    split = split_heads(b, m["kx"], m["kT"], (k_ready,))
    return attention_waves(b, m, SC, WIDTH ** -0.5, clip, (split, q_ready, v_ready))


def block_L2x(b, i, m):
    done = context_attention(b, i, m, 10000.0)
    turned = to_features(b, m["xT"], m["att"], 5, (done,))
    project_out(b, b.core.x[:, bass.ts(i, TILES), :], m["xT"], b.weight("wo"), b.weight("bo"), 6, (turned,))


def room_L2x(nc, ctx, name="L2x"):
    sb = lambda n, *shape: ctx.enter_context(nc.sbuf_tensor(f"{name}_{n}", list(shape), F32))
    return {"norm": norm_room(nc, ctx, TILES, name + "_norm"), **room_attention(sb, SC), "ctxT": sb("ctxT", CX, CTOK)}


def once_value_ones(b, m):
    ones = m["va"][:].rearrange("p s (h e) -> p s h e", h=HEADS)[:, :, :, WIDTH]
    b.nc.vector.memset(ones, 1.0)


def block_L3x(b, i, m):
    nc, psum = b.nc, b.core.psum
    x = b.core.x[:, bass.ts(i, TILES), :]
    done = context_attention(b, i, m, None)
    turned = to_features(b, m["xT"], m["att"], 5, (done,))
    b.dve.do(nc.vector.tensor_tensor, x, x, bcast(b.weight("b2"), 1, TILES), ALU.add)
    for f in range(2):
        b.pe.product(psum[:, f, :], b.weight("w1")[:, f * P:(f + 1) * P], m["xT"][:], start=True, stop=True,
                     after=(turned,))
        grown = b.act.do(nc.scalar.activation, m["hT"][:, f, :], psum[:, f, :], ACT.Relu, bias=b.weight("b1")[:, f:f + 1],
                         scale=1.0, after=(b.pe.mark(),))
    down = down_project(b, psum[:, 2, :], m["hT"], b.weight("w2"), (grown,))
    b.dve.do(nc.vector.tensor_tensor, x, x, psum[:, 2, :].rearrange("p (t d) -> p t d", t=TILES), ALU.add, after=(down,))


def room_L3x(nc, ctx):
    m = room_L2x(nc, ctx, "L3x")
    m["hT"] = ctx.enter_context(nc.sbuf_tensor("L3x_hT", [P, 2, TOK], F32))
    return m


def softmax_rows(b, e, logits, bias, best, after):
    nc, dve, n = b.nc, b.dve, e.shape[2]
    dve.do(nc.vector.tensor_tensor, e, logits, bcast(bias, 1, TILES), ALU.add, after=after)
    dve.do(nc.vector.tensor_reduce, best, e, AX, ALU.max)
    low = dve.do(nc.vector.tensor_tensor, e, e, bcast(best, 2, n), ALU.subtract)
    grown = b.act.do(nc.scalar.activation, e, e, ACT.Exp, after=(low,))
    dve.do(nc.vector.tensor_reduce, best, e, AX, ALU.add, after=(grown,))
    dve.do(nc.vector.reciprocal, best, best)
    return dve.do(nc.vector.tensor_tensor, e, e, bcast(best, 2, n), ALU.mult)


def block_L1f(b, i, m):
    nc, psum, c = b.nc, b.core.psum, b.core.c
    dve, act, pe, pool = b.dve, b.act, b.pe, b.pool
    tt = nc.vector.tensor_tensor
    x = b.core.x[:, bass.ts(i, TILES), :]
    normed = layer_norm(b, m["xn"], x, LN_EPS, m["norm"])
    ready = to_features(b, m["xT"], m["xn"], 0, (normed,))
    logits, pl = logits_of(b, m["xT"], b.weight("gate"), EXPERTS1, 7, (ready,))
    pe.product(psum[:, 1, :], b.weight("la"), m["xT"][:], start=True, stop=True)
    a_done = act.do(nc.scalar.copy, m["aT"][:], psum[:, 1, :], after=(pe.mark(),))
    softmax_rows(b, m["e"][:], logits, b.weight("gb"), m["best"][:], (pl,))
    dve.do(nc.vector.tensor_copy, m["v"][:], m["e"][:])
    picks = [m["pick"][:, r, :, :] for r in range(2)]
    picked = pick_largest(b, picks, m["v"][:], m["best"], m["w"][:], c["first"], 2)
    for r in range(2):
        turned = turn_combine(b, m, picks[r], EXPERTS1, 7, (picked,), m["pickT"][:, r, :], (a_done,) if r == 0 else (turned,))
    for r in range(2):
        pe.product(psum[:, 2 + r, :], c["spread1"], m["pickT"][:, r, :], start=True, stop=True, after=(turned,))
    spread = pe.mark()
    for r in range(2):
        low = dve.do(tt, m["low"][:, r, :], m["aT"][:], psum[:, 2 + r, :], ALU.mult, after=(spread, a_done))
    dve.do(tt, m["w"][:], picks[0], picks[1], ALU.add)
    dve.do(tt, m["w"][:], m["w"][:], m["e"][:], ALU.mult)
    dve.do(nc.vector.tensor_reduce, m["best"][:], m["w"][:], AX, ALU.add)
    freed = []
    for f in range(4):
        cols = slice(f * P, (f + 1) * P)
        base = 1 if f % 2 == 0 else 3
        free = freed[f - 2] if f >= 2 else ()
        for r in range(2):
            pe.product(psum[:, base + r, :], b.weight("wi")[:, cols], m["xT"][:], start=True, stop=False,
                       after=(low, *free))
            pe.product(psum[:, base + r, :], b.weight("lb")[:, cols], m["low"][:, r, :], start=False, stop=True)
            if r == 0:
                p0 = pe.mark()
        p1 = pe.mark()
        bias = b.weight("bi")[:, f:f + 1]
        r0 = act.do(nc.scalar.activation, m["r0"][:, f % 2, :], psum[:, base, :], ACT.Relu, bias=bias, scale=1.0, after=(p0,))
        r1 = dve.do(nc.vector.tensor_scalar, m["hT"][:, f, :], psum[:, base + 1, :], bias, 0.0, ALU.add, ALU.max,
                    after=(p1,))
        h_done = pool.do(nc.gpsimd.tensor_tensor, m["hT"][:, f, :], m["hT"][:, f, :], m["r0"][:, f % 2, :], ALU.add,
                         after=(r0, r1))
        if f < 2:
            freed.append((r0, r1))
        if f == 1:
            act.wait(h_done)
    down = down_project(b, psum[:, 0, :], m["hT"], b.weight("wo"), (h_done,))
    y = m["xn"][:]
    dve.do(nc.vector.scalar_tensor_tensor, y, bcast(b.weight("bo"), 1, TILES), 2.0,
           psum[:, 0, :].rearrange("p (t d) -> p t d", t=TILES), ALU.mult, ALU.add, after=(down,))
    dve.do(tt, y, y, bcast(m["best"][:], 2, D), ALU.mult)
    dve.do(tt, x, x, y, ALU.add)


def room_L1f(nc, ctx):
    sb = lambda n, *shape: ctx.enter_context(nc.sbuf_tensor(f"L1f_{n}", list(shape), F32))
    return {"norm": norm_room(nc, ctx, TILES, "L1f_norm"), "xn": sb("xn", P, TILES, D), "xT": sb("xT", P, TOK), "aT": sb("aT", P, TOK),
            "e": sb("e", P, TILES, 8), "v": sb("v", P, TILES, 8), "w": sb("w", P, TILES, 8), "best": sb("best", P, TILES),
            "pick": sb("pick", P, 2, TILES, 8), "pickT": sb("pickT", 8, 2, TOK), "low": sb("low", P, 2, TOK),
            "r0": sb("r0", P, 2, TOK), "hT": sb("hT", P, 4, TOK)}


def block_L2a(b, i, m):
    x = b.core.x[:, bass.ts(i, TILES), :]
    normed = layer_norm(b, m["x2"], x, LN_EPS, m["norm"])
    ready = to_features(b, m["xT"], m["x2"], 7, (normed,))
    done = linear_attention(b, m, m["xT"], ready, b.core.c["same8"], b.core.c["head8"], 16, 1e-6)
    turned = to_features(b, m["xT"], m["msg"], 7, (done,))
    project_out(b, x, m["xT"], b.weight("wo"), None, 0, (turned,))


def room_L2a(nc, ctx):
    sb = lambda n, *shape: ctx.enter_context(nc.sbuf_tensor(f"L2a_{n}", list(shape), F32))
    return {"norm": norm_room(nc, ctx, TILES, "L2a_norm"), "x2": sb("x2", P, TILES, D), "xT": sb("xT", P, TOK), **room_linear(sb, 16)}


def rms_norm(b, out, x, square, ss, eps, after=()):
    nc, dve = b.nc, b.dve
    squares = b.pool.do(nc.gpsimd.tensor_tensor, square, x, x, ALU.mult, after=(dve.now(), *after))
    dve.do(nc.vector.tensor_reduce, ss, square, AX, ALU.add, after=(squares,))
    scaled = inverse_root(b, ss, ss, 1.0 / x.shape[2], eps)
    return dve.do(nc.vector.tensor_tensor, out, x, bcast(ss, 2, x.shape[2]), ALU.mult, after=(scaled,))


def block_L2f(b, i, m):
    nc, psum, c = b.nc, b.core.psum, b.core.c
    dve, act, pe, pool = b.dve, b.act, b.pe, b.pool
    tt = nc.vector.tensor_tensor
    x = b.core.x[:, bass.ts(i, TILES), :]
    layer_norm(b, m["x0"], x, LN_EPS, m["norm"])
    normed = rms_norm(b, m["xn"][:], m["x0"][:], m["sq"][:], m["ss"][:], 1e-5)
    ready = to_features(b, m["xT"], m["xn"], 0, (normed,), b.weight("g1"), 0.0)
    pe.product(psum[0:16, 1, :], b.weight("wkl"), m["xT"][:], start=True, stop=True, after=(ready,))
    p_lat = pe.mark()
    latent = act.do(nc.scalar.copy, m["latT"][:], psum[0:16, 1, :], after=(p_lat,))
    latent = act.do(nc.scalar.copy, m["lat2"][:], bcast(psum[0:16, 1, :].rearrange("p (s k) -> p s k", k=S), 2, 2))
    pe.product(psum[:, 2, :], b.weight("wkr"), m["xT"][:], start=True, stop=True)
    pe.product(psum[:, 3, :], b.weight("wkp"), m["xT"][:], start=True, stop=True)
    kr_ready = rotate(b, m["krT"][:], psum[:, 2, :], psum[:, 3, :], c["cos32"], c["sin32"], m["twin"][:, 0, :],
                      (pe.mark(),))
    for n in range(4):
        pe.product(psum[:, 4 + n, :], b.weight("wkvb")[:, n * P:(n + 1) * P], m["latT"][:], start=True, stop=True,
                   after=(latent,))
    kv_ready = act.do(nc.scalar.copy, m["kvT"][:], psum[:, 4:8, :], after=(pe.mark(),))
    freed = []
    for n in range(4):
        cols = slice(n * P, (n + 1) * P)
        base = 1 if n % 2 == 0 else 4
        free = freed[n - 2] if n >= 2 else (kr_ready, kv_ready, latent)
        pe.product(psum[:, base, :], b.weight("wqn")[:, cols], m["xT"][:], start=True, stop=True, after=free)
        pn = pe.mark()
        pe.product(psum[:, base + 1, :], b.weight("wqr")[:, cols], m["xT"][:], start=True, stop=True)
        pe.product(psum[:, base + 2, :], b.weight("wqp")[:, cols], m["xT"][:], start=True, stop=True)
        pr = pe.mark()
        nope = act.do(nc.scalar.copy, m["qnT"][:, n, :], psum[:, base, :], after=(pn,))
        q_ready = rotate(b, m["qrT"][:, n, :], psum[:, base + 1, :], psum[:, base + 2, :], c["cos32"], c["sin32"],
                         m["twin"][:, n % 2, :], (pr,))
        if n == 1:
            dve.wait(q_ready)
        freed.append((nope, q_ready))
    va = m["va"][:].rearrange("p s (j c e) -> p s c j e", j=4, c=4)
    reads = []
    for s in range(SEQS):
        free = (reads[s - 2],) if s >= 2 else (q_ready, nope)
        pe.product(psum[:, 1 + s % 2, :], m["lat2"][:, s, :, :].rearrange("p a k -> p (a k)"), b.weight("wkvb"),
                   start=True, stop=True, after=free)
        own = bcast(bcast(c["parity"][:, 0:4], 2, 4), 3, 32)
        reads.append(dve.do(tt, va[:, s, :, :, 0:32], psum[:, 1 + s % 2, :].rearrange("p (c j d) -> p c j d", c=4, j=4),
                            own, ALU.mult, after=(pe.mark(),)))
    freed = (reads[-1], q_ready, nope, kr_ready, kv_ready)
    for w in range(2):
        for u in range(2):
            for r in range(2):
                s = 2 * (2 * w + u) + r
                q = slice(s * S, (s + 1) * S)
                for n in range(4):
                    for j in range(4):
                        f = slice(32 * j, 32 * j + 32)
                        out = psum[64 * r:64 * r + 64, j, (4 * u + n) * S:(4 * u + n + 1) * S]
                        pe.product(out, m["qnT"][f, n, q], m["kvT"][f, n, q], start=True, stop=False,
                                   skip_group_check=True, after=freed)
                        pe.product(out, m["qrT"][f, n, q], m["krT"][f, q], start=False, stop=True,
                                   skip_group_check=True)
        p = m["p"][:].rearrange("p (n k) -> p n k", k=S)
        read = dve.do(tt, p, psum[:, 0:4, :].rearrange("p a (n k) -> p (a n) k", k=S), bcast(c["causal"], 1, 32), ALU.add,
                      after=(pe.mark(),))
        dve.do(nc.vector.tensor_reduce, m["mx"][:], p, AX, ALU.max)
        low = dve.do(tt, p, p, bcast(m["mx"][:], 2, S), ALU.subtract)
        grown = act.do(nc.scalar.activation, p, p, ACT.Exp, scale=0.125, after=(low,))
        for n in range(16):
            pe.do(nc.tensor.transpose, psum[:, 4 + n // 4, (n % 4) * P:(n % 4 + 1) * P], m["p"][:, n * P:(n + 1) * P],
                  c["ident"], after=(grown,))
        turned = pe.mark()
        e0 = act.do(nc.scalar.copy, m["pT"][:, 0:2, :], psum[:, 4:6, :], after=(turned,))
        e1 = dve.do(nc.vector.tensor_copy, m["pT"][:, 2:4, :], psum[:, 6:8, :], after=(turned,))
        pT = m["pT"][:].rearrange("p a b -> p (a b)")
        for u in range(2):
            for r in range(2):
                s = 2 * (2 * w + u) + r
                for j in range(4):
                    for k in range(2):
                        n = (j * 2 + u) * 2 + k
                        at = ((j % 2) * 2 + k) * 66
                        pe.product(psum[64 * r:64 * r + 64, 4 + 2 * u + j // 2, at:at + 66],
                                   pT[:, n * P + 64 * r:n * P + 64 * r + 64], m["va"][:, s, (2 * j + k) * 66:(2 * j + k + 1) * 66],
                                   start=True, stop=True, after=(e0, e1))
        p_o = pe.mark()
        for u in range(2):
            for jh in range(2):
                out = psum[:, 4 + 2 * u + jh, 0:264].rearrange("p (j c e) -> p j c e", j=2, c=4)
                z = m["z"][:]
                dve.do(nc.vector.reciprocal, z, out[:, :, :, 32], after=(p_o,))
                y = m["y"][:, 2 * w + u, :].rearrange("p (c j d) -> p j c d", c=4, j=4)[:, 2 * jh:2 * jh + 2, :, :]
                freed_o = dve.do(tt, y, out[:, :, :, 0:32], bcast(z, 3, 32), ALU.mult)
        freed = (freed_o, read)
    for n in range(4):
        y_ready = to_features(b, m["qnT"][:, n, :], m["y"][:, :, n * P:(n + 1) * P], n, (freed_o,))
    down = down_project(b, psum[:, 4, :], m["qnT"], b.weight("wo"), (y_ready,))
    dve.do(tt, m["x0"][:], m["x0"][:], psum[:, 4, :].rearrange("p (t d) -> p t d", t=TILES), ALU.add, after=(down,))
    normed = rms_norm(b, m["xn"][:], m["x0"][:], m["sq"][:], m["ss"][:], 1e-5)
    ready = to_features(b, m["xT"], m["xn"], 0, (normed,), b.weight("g2"), 0.0)
    logits, pl = logits_of(b, m["xT"], b.weight("router"), EXPERTS2, 7, (ready,))
    softmax_rows(b, m["e"][:], logits, b.weight("rbias"), m["best"][:], (pl,))
    dve.do(nc.vector.tensor_copy, m["v"][:], m["e"][:])
    picks = [m["pick"][:, r, :, :] for r in range(2)]
    pick_largest(b, picks, m["v"][:], m["best"], m["w"][:], c["first"], 2)
    combined = weigh_picks(b, m, picks)
    comb_ready = turn_combine(b, m, m["comb"], EXPERTS2 + 1, 7, (combined,))
    done = experts(b, m, m["xT"], m["combT"][:], c["spread2"], (EXPERTS2 + 1) * HID2, 0, (comb_ready,))
    dve.do(tt, x, x, m["x0"][:], ALU.add)
    dve.do(tt, x, x, psum[:, 0, :].rearrange("p (t d) -> p t d", t=TILES), ALU.add, after=(done,))


def weigh_picks(b, m, picks):
    nc, dve = b.nc, b.dve
    tt = nc.vector.tensor_tensor
    dve.do(tt, m["w"][:], picks[0], picks[1], ALU.add)
    dve.do(tt, m["w"][:], m["w"][:], m["e"][:], ALU.mult)
    dve.do(nc.vector.tensor_reduce, m["best"][:], m["w"][:], AX, ALU.add)
    dve.do(nc.vector.reciprocal, m["best"][:], m["best"][:])
    return dve.do(tt, m["comb"][:, :, 0:8], m["w"][:], bcast(m["best"][:], 2, 8), ALU.mult)


def room_routed(sb):
    return {"e": sb("e", P, TILES, 8), "v": sb("v", P, TILES, 8), "w": sb("w", P, TILES, 8), "best": sb("best", P, TILES),
            "pick": sb("pick", P, 2, TILES, 8), "comb": sb("comb", P, TILES, 9), "combT": sb("combT", 9, TOK),
            "h": sb("h", P, 2, TOK)}


def room_L2f(nc, ctx):
    sb = lambda n, *shape: ctx.enter_context(nc.sbuf_tensor(f"L2f_{n}", list(shape), F32))
    return {"norm": norm_room(nc, ctx, TILES, "L2f_norm"), "x0": sb("x0", P, TILES, D), "xn": sb("xn", P, TILES, D),
            "sq": sb("sq", P, TILES, D), "ss": sb("ss", P, TILES), "xT": sb("xT", P, TOK), "latT": sb("latT", 16, TOK),
            "lat2": sb("lat2", 16, SEQS, 2, S),
            "krT": sb("krT", P, TOK), "twin": sb("twin", P, 2, TOK), "kvT": sb("kvT", P, 4, TOK),
            "qnT": sb("qnT", P, 4, TOK), "qrT": sb("qrT", P, 4, TOK), "va": sb("va", P, SEQS, 16 * 33),
            "p": sb("p", P, 2048), "pT": sb("pT", P, 4, 512), "mx": sb("mx", P, 32), "z": sb("z", P, 2, 4),
            "y": sb("y", P, TILES, 512), **room_routed(sb)}


def once_L2f(b, m):
    nc, parity = b.nc, b.core.c["parity"]
    ones = m["va"][:].rearrange("p s (j c e) -> p s j c e", j=4, c=4)
    for s in range(SEQS):
        nc.vector.tensor_copy(ones[:, s, :, :, 32], bcast(parity[:, 0:4], 1, 4))
    nc.vector.memset(m["comb"][:, :, 8:9], 1.0)


def block_L3a(b, i, m):
    nc, psum, c = b.nc, b.core.psum, b.core.c
    dve, act, pe, pool = b.dve, b.act, b.pe, b.pool
    tt = nc.vector.tensor_tensor
    x = b.core.x[:, bass.ts(i, TILES), :]
    tiles = lambda ap: ap.rearrange("p (t d) -> p t d", t=TILES)
    layer_norm(b, m["x0"], x, LN_EPS, m["norm"])
    normed = layer_norm(b, m["xn"], m["x0"], LN_EPS, m["norm"])
    ready = to_features(b, m["xT"], m["xn"], 0, (normed,), b.weight("g1"), b.weight("be1"))
    pe.product(psum[0:16, 3, :], b.weight("gk1"), m["xT"][:], start=True, stop=True, after=(ready,))
    gk_done = act.do(nc.scalar.copy, m["gkT"][:], psum[0:16, 3, :], after=(pe.mark(),))
    pe.product(psum[:, 1, :], b.weight("wq"), m["xT"][:], start=True, stop=True)
    pe.product(psum[:, 2, :], b.weight("wk"), m["xT"][:], start=True, stop=True)
    for t in range(TILES):
        pe.product(psum[:, 6, t * P:(t + 1) * P], m["gkT"][:, t * P:(t + 1) * P], b.weight("gk2"), start=True, stop=True,
                   after=(gk_done,))
    pz = pe.mark()
    for t in range(TILES):
        pe.product(psum[:, 4, t * P:(t + 1) * P], m["xT"][:, t * P:(t + 1) * P], b.weight("wv"), start=True, stop=True)
        pe.product(psum[:, 5, t * P:(t + 1) * P], m["xT"][:, t * P:(t + 1) * P], b.weight("wg"), start=True, stop=True)
    pvg = pe.mark()
    dve.do(tt, m["lz"][:], tiles(psum[:, 6, :]), bcast(b.weight("bgk"), 1, TILES), ALU.add, after=(pz,))
    size = dve.do(nc.vector.scalar_tensor_tensor, m["la"][:], m["lz"][:], -1.0, m["lz"][:], ALU.mult, ALU.max)
    act.do(nc.scalar.activation, m["la"][:], m["la"][:], ACT.Exp, scale=-1.0, after=(size,))
    log = act.do(nc.scalar.activation, m["la"][:], m["la"][:], ACT.Ln, bias=1.0)
    decays = dve.do(nc.vector.scalar_tensor_tensor, m["lz"][:], m["lz"][:], 0.0, m["la"][:], ALU.min, ALU.subtract,
                    after=(log,))
    for t in range(TILES):
        pe.product(psum[:, 7, t * P:(t + 1) * P], m["lz"][:, t, :], c["decay"], start=True, stop=True, after=(decays,))
    pg = pe.mark()
    up = act.do(nc.scalar.activation, m["eq"][:], psum[:, 7, :], ACT.Exp, after=(pg,))
    down = act.do(nc.scalar.activation, m["ek"][:], psum[:, 7, :], ACT.Exp, scale=-1.0)
    v_done = act.do(nc.scalar.copy, m["v"][:], tiles(psum[:, 4, :]), after=(pvg,))
    g_done = act.do(nc.scalar.activation, m["g"][:], tiles(psum[:, 5, :]), ACT.Silu)
    dve.do(nc.vector.scalar_tensor_tensor, m["eq"][:], psum[:, 1, :], 32 ** -0.5, m["eq"][:], ALU.mult, ALU.mult,
           after=(up,))
    decayed = dve.do(tt, m["ek"][:], m["ek"][:], psum[:, 2, :], ALU.mult, after=(down,))
    for s in range(SEQS):
        t, r = s // 2, s % 2
        q = slice(s * S, (s + 1) * S)
        for h in range(4):
            f = slice(32 * h, 32 * h + 32)
            pe.product(psum[64 * r:64 * r + 64, h, t * S:(t + 1) * S], m["ek"][f, q], m["eq"][f, q], start=True,
                       stop=True, after=(decayed,))
    masked = dve.do(tt, m["a"][:], psum[:, 0:4, 0:TILES * S].rearrange("p h (t q) -> p h t q", q=S),
                    bcast(bcast(c["past"], 1, TILES), 1, 4), ALU.mult, after=(pe.mark(),))
    for s in range(SEQS):
        t, r = s // 2, s % 2
        q = slice(64 * r, 64 * r + 64)
        for h in range(4):
            f = slice(32 * h, 32 * h + 32)
            pe.product(psum[q, 4 + r, t * P + 32 * h:t * P + 32 * h + 32], m["a"][q, h, t, :], m["v"][q, t, f], start=True,
                       stop=True, after=(masked, v_done, g_done))
    po = pe.mark()
    for r in range(2):
        q = slice(64 * r, 64 * r + 64)
        copied = act.do(nc.scalar.copy, m["o"][q, :, :], tiles(psum[q, 4 + r, :]), after=(po,))
    heads = lambda ap: ap.rearrange("p t (h d) -> p (t h) d", h=4)
    rms_norm(b, heads(m["o"][:]), heads(m["o"][:]), heads(m["xn"][:]), m["ss"][:], 1e-5, (copied,))
    gated = dve.do(tt, m["o"][:], m["o"][:], m["g"][:], ALU.mult)
    o_ready = to_features(b, m["xT"], m["o"], 6, (gated,), b.weight("rms"), 0.0)
    project_out(b, m["x0"][:], m["xT"], b.weight("wo"), None, 7, (o_ready,))
    normed = layer_norm(b, m["xn"], m["x0"], LN_EPS, m["norm"])
    ready = to_features(b, m["xT"], m["xn"], 0, (normed,), b.weight("g2"), b.weight("be2"))
    dve.do(tt, m["x0"][:], m["x0"][:], bcast(b.weight("b2"), 1, TILES), ALU.add)
    dve.do(tt, x, x, m["x0"][:], ALU.add)
    for f in range(3):
        pe.product(psum[:, 1 + f, :], b.weight("w1")[:, f * P:(f + 1) * P], m["xT"][:], start=True, stop=True,
                   after=(ready,))
        biased = act.do(nc.scalar.activation, m["hT"][:, f, :], psum[:, 1 + f, :], ACT.Identity,
                        bias=b.weight("b1")[:, f:f + 1], scale=1.0, after=(pe.mark(),))
        h = m["hT"][:, f, :]
        leaky = dve.do(nc.vector.scalar_tensor_tensor, h, h, 0.01, h, ALU.mult, ALU.max, after=(biased,))
        squared = pool.do(nc.gpsimd.tensor_tensor, h, h, h, ALU.mult, after=(leaky,))
    done = down_project(b, psum[:, 4, :], m["hT"], b.weight("w2"), (squared,))
    dve.do(tt, x, x, tiles(psum[:, 4, :]), ALU.add, after=(done,))


def room_L3a(nc, ctx):
    sb = lambda n, *shape: ctx.enter_context(nc.sbuf_tensor(f"L3a_{n}", list(shape), F32))
    tile = ("x0", "xn", "lz", "la", "v", "g", "o")
    return {"norm": norm_room(nc, ctx, TILES, "L3a_norm"), **{n: sb(n, P, TILES, D) for n in tile}, "xT": sb("xT", P, TOK),
            "gkT": sb("gkT", 16, TOK), "eq": sb("eq", P, TOK), "ek": sb("ek", P, TOK), "a": sb("a", P, 4, TILES, S),
            "ss": sb("ss", P, 4 * TILES), "hT": sb("hT", P, 3, TOK)}


def block_L3f(b, i, m):
    nc, psum, c = b.nc, b.core.psum, b.core.c
    dve = b.dve
    tt = nc.vector.tensor_tensor
    x = b.core.x[:, bass.ts(i, TILES), :]
    normed = layer_norm(b, m["xn"], x, LN_EPS, m["norm"])
    ready = to_features(b, m["xT"], m["xn"], 0, (normed,))
    logits, pl = logits_of(b, m["xT"], b.weight("router"), EXPERTS3, 7, (ready,))
    dve.do(nc.vector.tensor_reduce, m["best"][:], logits, AX, ALU.max, after=(pl,))
    dve.do(nc.vector.tensor_copy, m["v"][:], logits)
    low = dve.do(tt, m["e"][:], logits, bcast(m["best"][:], 2, EXPERTS3), ALU.subtract)
    grown = b.act.do(nc.scalar.activation, m["e"][:], m["e"][:], ACT.Exp, after=(low,))
    picks = [m["pick"][:, r, :, :] for r in range(2)]
    pick_largest(b, picks, m["v"][:], m["best"], m["w"][:], c["first"], 2)
    dve.wait(grown)
    combined = weigh_picks(b, m, picks)
    comb_ready = turn_combine(b, m, m["comb"], EXPERTS3 + 1, 7, (combined,))
    done = experts(b, m, m["xT"], m["combT"][:], c["spread3"], (EXPERTS3 + 1) * HID3, 0, (comb_ready,))
    dve.do(tt, x, x, psum[:, 0, :].rearrange("p (t d) -> p t d", t=TILES), ALU.add, after=(done,))


def room_L3f(nc, ctx):
    sb = lambda n, *shape: ctx.enter_context(nc.sbuf_tensor(f"L3f_{n}", list(shape), F32))
    return {"norm": norm_room(nc, ctx, TILES, "L3f_norm"), "xn": sb("xn", P, TILES, D), "xT": sb("xT", P, TOK), **room_routed(sb)}


def once_L3f(b, m):
    b.nc.vector.memset(m["comb"][:, :, 8:9], 1.0)


ROUND = {}
ROOMS = {"L0x": room_L0x, "L0a": room_L0a, "L0f": room_L0f, "L1x": room_L1x, "L1a": room_L1a, "L1f": room_L1f,
         "L2x": room_L2x, "L2a": room_L2a, "L2f": room_L2f, "L3x": room_L3x, "L3a": room_L3a, "L3f": room_L3f}
BODIES = {"L0x": block_L0x, "L0a": block_L0a, "L0f": block_L0f, "L1x": block_L1x, "L1a": block_L1a, "L1f": block_L1f,
          "L2x": block_L2x, "L2a": block_L2a, "L2f": block_L2f, "L3x": block_L3x, "L3a": block_L3a, "L3f": block_L3f}
ONCE = {"L0a": once_ones, "L1x": once_L1x, "L1a": once_L1a, "L2x": once_value_ones, "L2a": once_ones, "L2f": once_L2f,
        "L3x": once_value_ones, "L3f": once_L3f}



def build(nc, n_seq, weights, constants, x, ctxT, ctx_tok, mask, out, plan, blocks):
    table = weight_table()
    places, _ = weight_places(table)
    n_groups = n_seq // SEQS
    ROUND["n_seq"] = n_seq
    core = Core()
    core.nc, core.places = nc, places
    ctx = ExitStack()
    sb = lambda n, *shape: ctx.enter_context(nc.sbuf_tensor(n, list(shape), F32))
    core.x = sb("x_held", P, n_seq // 2, D)
    core.ctxT = sb("ctxT_held", CX, n_seq * SC)
    core.ctx_tok = ctx_tok
    core.mask = mask
    core.psum = ctx.enter_context(nc.psum_tensor("psum", [P, 8, BANK], F32))
    const_tile = sb("constants_held", P, constants.shape[1])
    core.c, at = {}, 0
    for name, value in constant_table().items():
        core.c[name] = const_tile[0:value.shape[0], at:at + value.shape[1]]
        at += value.shape[1]
    widest = [max(places[n][1] for n in blocks[k::2]) if blocks[k::2] else 1 for k in range(2)]
    rooms = [sb(f"weights{k}", P, widest[k]) for k in range(2)]
    core.weight_room = {n: rooms[k % 2] for k, n in enumerate(blocks)}
    core.idle = {k: nc.alloc_semaphore(f"idle_{k}") for k in ("pe", "dve", "act", "pool")}
    loaded = nc.alloc_semaphore("loaded")
    n_loaded = 0

    def load(dst, src):
        nc.sync.dma_start(dst, src).then_inc(loaded, 16)

    def load_weights(name):
        first, n, _ = places[name]
        load(core.weight_room[name][:, 0:n], weights[:, first:first + n])

    load_weights(blocks[0])
    load(const_tile[:], constants)
    x_tiles = "(n p) d -> p n d"
    load(core.x[:], x.rearrange(x_tiles, p=P))
    load(core.ctxT[:], ctxT)
    n_loaded = 4
    for k, name in enumerate(blocks):
        with ExitStack() as own:
            m = ROOMS[name](nc, own)
            for engine in (nc.tensor, nc.vector, nc.scalar, nc.gpsimd):
                engine.wait_ge(loaded, 16 * n_loaded)
            b = Block(core, name, plan)
            b.n_groups = n_groups
            if name in ONCE:
                ONCE[name](b, m)
            nc.all_engine_barrier()
            if k + 1 < len(blocks):
                load_weights(blocks[k + 1])
                n_loaded += 1
            with nc.Fori(0, n_groups) as i:
                b.start_round(i)
                BODIES[name](b, i, m)
                b.end_round()
            nc.all_engine_barrier()
    stored = nc.alloc_semaphore("stored")
    nc.sync.dma_start(out.rearrange(x_tiles, p=P), core.x[:]).then_inc(stored, 16)
    nc.sync.wait_ge(stored, 16)
    ctx.close()


BLOCKS = ["L0x", "L0a", "L0f", "L1x", "L1a", "L1f", "L2x", "L2a", "L2f", "L3x", "L3a", "L3f"]


def program(nc, n_seq, n_weights, n_constants, plan, blocks=BLOCKS):
    dram = lambda n, shape, dt=F32, kind="ExternalInput": nc.dram_tensor(n, shape, dt, kind=kind).ap()
    build(nc, n_seq, dram("weights", (P, n_weights)), dram("constants", (P, n_constants)), dram("x", (n_seq * S, D)),
          dram("ctxT", (CX, n_seq * SC)), dram("ctx", (P, n_seq, CX)), dram("mask", (n_seq, SC // 4), I32),
          dram("out", (n_seq * S, D), kind="ExternalOutput"), plan, blocks)


def kernel(**inputs):
    import concourse.bacc as bacc
    from concourse.bass_utils import run_bass_kernel_spmd
    a = {k: np.asarray(v) for k, v in inputs.items()}
    x, context, mask = a["x"], a["ctx_768"], a["mask_BxS2_bk0"]
    n_seq = x.shape[0]
    packed = []
    for entries in weight_table().values():
        for name, rows, cols, layout in entries:
            w = layout(a)
            assert w.shape == (rows, cols), (name, w.shape)
            packed.append(pad_rows(w, P))
    weights = np.ascontiguousarray(np.concatenate(packed, 1))
    constants = np.ascontiguousarray(np.concatenate([pad_rows(v, P) for v in constant_table().values()], 1))
    arrays = {
        "weights": weights, "constants": constants, "x": np.ascontiguousarray(x.reshape(-1, D)),
        "ctxT": np.ascontiguousarray(context.transpose(2, 0, 1).reshape(CX, -1)),
        "ctx": np.ascontiguousarray(context.transpose(1, 0, 2)), "mask": np.ascontiguousarray(mask).view(np.int32)}
    plan = {}
    for _ in range(2):
        nc = bacc.Bacc("TRN2", target_bir_lowering=False, num_devices=1)
        program(nc, n_seq, weights.shape[1], constants.shape[1], plan)
    r = run_bass_kernel_spmd(nc, [arrays], core_ids=[0])
    return r.results[0]["out"].reshape(x.shape)
```

```python
from contextlib import ExitStack

import numpy as np
import concourse.bass as bass
from concourse import mybir

F32 = mybir.dt.float32
BF16 = mybir.dt.bfloat16
U8 = mybir.dt.uint8
I32 = mybir.dt.int32
ALU = mybir.AluOpType
ACT = mybir.ActivationFunctionType
AX = mybir.AxisListType.X

P = 128
S = 64
D = 128
CX = 96
SC = 128
BANK = 512
CONTEXTS = 2
CONTEXT_BANKS = 4
NEG = -1.0e30
LN_EPS = 1e-5



def chunks(w, rows=P):
    k = w.shape[0] // rows
    return w.reshape(k, rows, w.shape[1]).transpose(1, 0, 2).reshape(rows, k * w.shape[1])


def col(v):
    return v.reshape(-1, P).T if v.size >= P else v.reshape(-1, 1)


def row(v):
    return np.broadcast_to(v.reshape(1, -1), (P, v.size))


def rope_partner(n_heads, width):
    f = np.arange(n_heads * width)
    return f - f % width + (f % width + width // 2) % width


EXPERTS0, HID0 = 16, 64
EXPERTS1, RANK1, FF1 = 8, 16, 512
EXPERTS2, HID2 = 8, 64
EXPERTS3, HID3 = 8, 192


def pad_rows(w, rows):
    return np.concatenate([w, np.zeros((rows - w.shape[0], w.shape[1]), w.dtype)], 0)


def spaced(v):
    z = np.zeros_like(v)
    return np.stack([np.concatenate([v, z]), np.concatenate([z, v])], 1)


def placed(v, column):
    out = np.zeros((P, 4), v.dtype)
    out[np.arange(P), column] = v
    return out


def by_quad(v):
    return placed(v, np.arange(P) // 32)


def by_lane(v):
    return placed(v, np.arange(P) % 32 // 8)


def weight_table():
    t = {}
    t["L0x"] = [
        ("wv", P, 64, lambda a: a["L0_xattn_Wv"].T), ("wt", CX, 64, lambda a: a["L0_xattn_Wt"].T),
        ("bv", 64, 1, lambda a: col(a["L0_xattn_bv"])), ("bt", 64, 1, lambda a: col(a["L0_xattn_bt"]))]
    t["L0a"] = [
        ("wq", P, P, lambda a: a["L0_attn_wq"].T),
        ("wk", P, P, lambda a: a["L0_attn_wk"].T), ("wv", P, P, lambda a: a["L0_attn_wv"].T),
        ("w1", P, 512, lambda a: a["L0_attn_w1"].T), ("w2", P, 512, lambda a: chunks(a["L0_attn_w2"].T)),
        ("b1", P, 4, lambda a: col(a["L0_attn_b1"])), ("b2", P, P, lambda a: row(a["L0_attn_b2"])),
        ("g1", P, 1, lambda a: col(a["L0_attn_g1"])), ("be1", P, 1, lambda a: col(a["L0_attn_be1"])),
        ("g2", P, 1, lambda a: col(a["L0_attn_g2"])), ("be2", P, 1, lambda a: col(a["L0_attn_be2"]))]
    t["L0f"] = [
        ("router", P, 16, lambda a: a["L0_ffn_router_weight"].T),
        ("rbias", P, 16, lambda a: row(a["L0_ffn_router_bias"])),
        ("gate", P, 1024, lambda a: a["L0_ffn_w_gate"].reshape(-1, D).T),
        ("up", P, 1024, lambda a: a["L0_ffn_w_up"].reshape(-1, D).T),
        ("down", P, 1024, lambda a: chunks(a["L0_ffn_w_down"].transpose(0, 2, 1).reshape(-1, D)))]
    t["L1x"] = [
        ("wql", P, 384, lambda a: np.concatenate([a["L1_xattn_Wq"].T, a["L1_xattn_Wlkv"].T], 1)),
        ("wkv", CX, 256, lambda a: a["L1_xattn_Wkv"].T), ("wo", P, P, lambda a: a["L1_xattn_Wo"].T),
        ("bo", P, P, lambda a: row(a["L1_xattn_bo"])),
        ("xg", CX, 1, lambda a: col(a["L1_xattn_ln_x_g"])), ("xb", CX, 1, lambda a: col(a["L1_xattn_ln_x_b"])),
        ("lg", P, 1, lambda a: col(a["L1_xattn_ln_l_g"])), ("lb", P, 1, lambda a: col(a["L1_xattn_ln_l_b"])),
        ("qg", P, 2, lambda a: spaced(a["L1_xattn_qn_g"])),
        ("kg", P, 1, lambda a: col(np.tile(a["L1_xattn_kn_g"], 2)))]
    perm8 = rope_partner(16, 8)
    t["L1a"] = [
        ("wq", P, P, lambda a: a["L1_attn_w_qkv"][:D].T), ("wqp", P, P, lambda a: a["L1_attn_w_qkv"][:D][perm8].T),
        ("wk", P, P, lambda a: a["L1_attn_w_qkv"][D:2 * D].T),
        ("wkp", P, P, lambda a: a["L1_attn_w_qkv"][D:2 * D][perm8].T),
        ("wv", P, P, lambda a: a["L1_attn_w_qkv"][2 * D:].T), ("wo", P, P, lambda a: a["L1_attn_w_out"].T),
        ("bo", P, P, lambda a: row(a["L1_attn_b_out"]))]
    t["L1f"] = [
        ("gate", P, 8, lambda a: a["L1_ffn_gate_w"].T), ("gb", P, 8, lambda a: row(a["L1_ffn_gate_b"])),
        ("wi", P, 512, lambda a: a["L1_ffn_wi"].T), ("bi", P, 4, lambda a: col(a["L1_ffn_bi"])),
        ("wo", P, 512, lambda a: chunks(a["L1_ffn_wo"].T)), ("bo", P, P, lambda a: row(a["L1_ffn_bo"])),
        ("la", P, P, lambda a: a["L1_ffn_lora_A"].reshape(-1, D).T),
        ("lb", P, 512, lambda a: a["L1_ffn_lora_B"].transpose(0, 2, 1).reshape(P, 512))]
    t["L2x"] = [
        ("wq", P, P, lambda a: a["L2_xattn_Wq"]), ("wk", CX, P, lambda a: a["L2_xattn_Wk"]),
        ("wv", CX, P, lambda a: a["L2_xattn_Wv"]), ("wo", P, P, lambda a: a["L2_xattn_Wo"]),
        ("bq", P, 4, lambda a: by_quad(a["L2_xattn_bq"])), ("bk", P, 4, lambda a: by_lane(a["L2_xattn_bk"])),
        ("bv", P, P, lambda a: row(a["L2_xattn_bv"])), ("bo", P, P, lambda a: row(a["L2_xattn_bo"]))]
    t["L2a"] = [
        ("wq", P, P, lambda a: a["L2_attn_Wq"]), ("wk", P, P, lambda a: a["L2_attn_Wk"]),
        ("wv", P, P, lambda a: a["L2_attn_Wv"]), ("wo", P, P, lambda a: a["L2_attn_Wo"])]
    pair = np.arange(32) ^ 1
    t["L2f"] = [
        ("g1", P, 1, lambda a: col(a["L2_ffn_w_ln1"])), ("g2", P, 1, lambda a: col(a["L2_ffn_w_ln2"])),
        ("wqn", P, 512, lambda a: a["L2_ffn_Wq"].reshape(D, 16, 64)[:, :, :32].reshape(D, 512)),
        ("wqr", P, 512, lambda a: a["L2_ffn_Wq"].reshape(D, 16, 64)[:, :, 32:].reshape(D, 512)),
        ("wqp", P, 512, lambda a: a["L2_ffn_Wq"].reshape(D, 16, 64)[:, :, 32:][:, :, pair].reshape(D, 512)),
        ("wkl", P, 16, lambda a: a["L2_ffn_Wkva"][:, :16]),
        ("wkr", P, P, lambda a: np.tile(a["L2_ffn_Wkva"][:, 16:], (1, 4))),
        ("wkp", P, P, lambda a: np.tile(a["L2_ffn_Wkva"][:, 16:][:, pair], (1, 4))),
        ("wkvb", P, 512, lambda a: pad_rows(a["L2_ffn_Wkvb"], P)),
        ("wo", P, 512, lambda a: chunks(a["L2_ffn_Wo"].reshape(16, 64, D)[:, :32].reshape(512, D))),
        ("router", P, 8, lambda a: a["L2_ffn_Wgate"]), ("rbias", P, 8, lambda a: row(a["L2_ffn_expert_bias"])),
        ("gate", P, 576, lambda a: np.concatenate([a["L2_ffn_Wg"], a["L2_ffn_sWg"]]).transpose(1, 0, 2).reshape(D, 576)),
        ("up", P, 576, lambda a: np.concatenate([a["L2_ffn_Wu"], a["L2_ffn_sWu"]]).transpose(1, 0, 2).reshape(D, 576)),
        ("down", P, 640, lambda a: chunks(pad_rows(np.concatenate([a["L2_ffn_Wd"], a["L2_ffn_sWd"]]).reshape(576, D), 640)))]
    t["L3x"] = [
        ("wq", P, P, lambda a: a["L3_xattn_Wq"]), ("wk", CX, P, lambda a: a["L3_xattn_Wk"]),
        ("wv", CX, P, lambda a: a["L3_xattn_Wv"]), ("bq", P, 4, lambda a: by_quad(a["L3_xattn_bq"])),
        ("bk", P, 4, lambda a: by_lane(a["L3_xattn_bk"])), ("bv", P, P, lambda a: row(a["L3_xattn_bv"])),
        ("w1", P, 256, lambda a: a["L3_xattn_W1"]), ("b1", P, 2, lambda a: col(a["L3_xattn_b1"])),
        ("w2", P, 256, lambda a: chunks(a["L3_xattn_W2"])), ("b2", P, P, lambda a: row(a["L3_xattn_b2"]))]
    t["L3a"] = [
        ("g1", P, 1, lambda a: col(a["L3_attn_ln1_w"])), ("be1", P, 1, lambda a: col(a["L3_attn_ln1_b"])),
        ("g2", P, 1, lambda a: col(a["L3_attn_ln2_w"])), ("be2", P, 1, lambda a: col(a["L3_attn_ln2_b"])),
        ("rms", P, 1, lambda a: col(np.tile(a["L3_attn_rms_w"], 4))),
        ("wq", P, P, lambda a: a["L3_attn_Wq"]), ("wk", P, P, lambda a: a["L3_attn_Wk"]),
        ("wv", P, P, lambda a: a["L3_attn_Wv"]), ("wg", P, P, lambda a: a["L3_attn_Wg"]),
        ("gk1", P, 16, lambda a: a["L3_attn_Wgk1"]), ("gk2", 16, P, lambda a: a["L3_attn_Wgk2"]),
        ("bgk", P, P, lambda a: row(a["L3_attn_bgk2"])), ("wo", P, P, lambda a: a["L3_attn_Wo"]),
        ("w1", P, 384, lambda a: a["L3_attn_W1"]), ("b1", P, 3, lambda a: col(a["L3_attn_b1"])),
        ("w2", P, 384, lambda a: chunks(a["L3_attn_W2"])), ("b2", P, P, lambda a: row(a["L3_attn_b2"]))]
    half = HID3
    t["L3f"] = [
        ("router", P, 8, lambda a: a["L3_ffn_gate_w"].T),
        ("gate", P, 1728, lambda a: np.concatenate([a["L3_ffn_w_up"][:, :half].reshape(-1, D), a["L3_ffn_sg_gate"]]).T),
        ("up", P, 1728, lambda a: np.concatenate([a["L3_ffn_w_up"][:, half:].reshape(-1, D), a["L3_ffn_sg_up"]]).T),
        ("down", P, 1792, lambda a: chunks(pad_rows(np.concatenate(
            [a["L3_ffn_w_down"].transpose(0, 2, 1).reshape(-1, D), a["L3_ffn_sg_down"].T]), 1792)))]
    return t


def weight_places(table):
    places, at = {}, 0
    for block, entries in table.items():
        inside, n = {}, 0
        for name, rows, cols, _ in entries:
            inside[name] = (n, rows, cols)
            n += cols
        places[block] = (at, n, inside)
        at += n
    return places, at


def expert_spread(hidden, experts, total):
    e = np.minimum(np.arange(total) // hidden, experts)
    return (np.arange(experts + 1)[:, None] == e[None, :]).astype(np.float32)


def constant_table():
    p = np.arange(P)
    c = {"ident": np.eye(P), "ones": np.ones((P, P)), "halves": np.full((P, 32), -0.5)}
    c["same16"] = p[:, None] // 16 == p[None, :] // 16
    c["head16"] = p[:, None] // 16 == np.arange(8)[None, :]
    c["same8"] = p[:, None] // 8 == p[None, :] // 8
    c["head8"] = p[:, None] // 8 == np.arange(16)[None, :]
    c["lane4"] = (p[:, None] % 32) // 8 == np.arange(4)[None, :]
    c["quad"] = p[:, None] // 32 == np.arange(4)[None, :]
    c["parity"] = p[:, None] // 64 == np.arange(16)[None, :] % 2
    c["first"] = np.broadcast_to(16.0 - np.arange(16), (P, 16))
    pos = np.arange(S, dtype=np.float32)
    inv = (1.0 / np.float32(10000.0) ** (np.arange(0, 8, 2, dtype=np.float32) / np.float32(8))).astype(np.float32)
    ang = (pos[None, :] * inv[p % 4][:, None]).astype(np.float32)
    c["cos8"] = np.cos(ang)
    c["sin8"] = np.sin(ang) * np.where(p % 8 < 4, -1.0, 1.0)[:, None]
    inv = (1.0 / np.float32(100000.0) ** (np.arange(0, 32, 2, dtype=np.float32) / np.float32(32))).astype(np.float32)
    ang = (pos[None, :] * inv[(p % 32) // 2][:, None]).astype(np.float32)
    c["cos32"] = np.cos(ang)
    c["sin32"] = np.sin(ang) * np.where(p % 2 == 0, -1.0, 1.0)[:, None]
    c["causal"] = np.where(np.arange(S)[None, :] <= (p % S)[:, None], 0.0, NEG)
    same = p[:, None] // S == p[None, :] // S
    upto = (p[:, None] <= p[None, :]).astype(np.float64)
    c["decay"] = same * (upto - (p % S < S // 2)[:, None]) / 16.0
    c["past"] = (p % S)[:, None] <= np.arange(S)[None, :]
    return {k: np.asarray(v, np.float32) for k, v in c.items()}


def half_table():
    t = {"ident": np.eye(P)}
    for name, spread in (("spread0", expert_spread(HID0, EXPERTS0, EXPERTS0 * HID0)[:EXPERTS0]),
                         ("spread2", expert_spread(HID2, EXPERTS2, 5 * P)), ("spread3", expert_spread(HID3, EXPERTS3, 14 * P))):
        t[name] = pad_rows(np.tile(spread, (3, 1)), P)
    spread = expert_spread(RANK1, EXPERTS1, P)[:EXPERTS1]
    t["pick0"] = pad_rows(spread, P)
    t["pick1"] = pad_rows(np.concatenate([0 * spread, spread]), P)
    return t


def half_words(table):
    one = np.uint16(0x3F80)
    return np.ascontiguousarray(np.concatenate(list(table.values()), 1).astype(np.uint16) * one).view(np.float32)



class Step:

    def __init__(self, queue, instruction, args, kwargs, after, alone):
        self.queue, self.instruction, self.args, self.kwargs = queue, instruction, args, kwargs
        self.after, self.alone = after, alone
        self.counted = False
        self.number = None


class Queue:

    def __init__(self, context, lane):
        self.context, self.lane, self.last, self.pending = context, lane, None, ()

    def wait(self, token):
        self.pending += (token,)

    def product(self, out, stationary, moving, after=(), **kwargs):
        small = stationary.shape[0] <= 64 and int(np.prod(stationary.shape[1:])) <= 64
        return self.do(self.lane.engine.matmul, out, stationary, moving, after=after, alone=small, **kwargs)

    def do(self, instruction, *args, after=(), alone=False, **kwargs):
        after = (*self.pending, *after)
        if self.last is None:
            after = (*self.context.round_before(self.lane), *after)
        elif self.lane.chained:
            after = (*after, self.last)
        self.pending = ()
        self.last = Step(self, instruction, args, kwargs, after, alone)
        self.context.steps.append(self.last)
        return self.mark() if self.lane.chained else None

    def mark(self):
        self.last.counted = True
        return self.last

    def now(self):
        return self.last


class Lane:

    def __init__(self, nc, engine, name, per_round, chained, idle, step=1):
        self.engine, self.name, self.per_round, self.chained, self.step = engine, name, per_round, chained, step
        self.sem = nc.alloc_semaphore(name)
        self.idle = idle
        self.count, self.reached = 0, {}
        if per_round:
            engine.sem_inc(self.sem, per_round * step)

    def emit(self, step, i):
        waits = 0
        latest = {}
        for token in step.after:
            if token.queue.lane not in latest or latest[token.queue.lane].number < token.number:
                latest[token.queue.lane] = token
        for lane, token in latest.items():
            if self.reached.get(lane.name, -lane.per_round - 1) < token.number:
                self.reached[lane.name] = token.number
                self.engine.wait_ge(lane.sem, i * (lane.per_round * lane.step) + (lane.per_round + token.number) * lane.step)
                waits += 1
                if self.step > 1:
                    self.engine.sem_inc(self.idle, 1)
        if step.alone and waits:
            self.engine.sem_inc(self.idle, 1)
        placed = step.instruction(*step.args, **step.kwargs)
        if step.counted:
            placed.then_inc(self.sem, self.step)


class Context:

    def __init__(self, block, number, tiles):
        self.block, self.nc, self.core, self.number = block, block.nc, block.core, number
        self.tiles, self.seqs, self.tok, self.ctok = tiles, 2 * tiles, tiles * P, 2 * tiles * SC
        self.tag = f"c{number}_"
        self.psum = block.core.psum[:, CONTEXT_BANKS * number:CONTEXT_BANKS * (number + 1), :]

    def weight(self, name):
        return self.block.weight(name)

    def begin(self):
        self.steps = []
        self.queues = {key: Queue(self, lane) for key, lane in self.block.lanes.items()
                       if not key.startswith("load") or key == f"load{self.number}"}
        self.pe, self.dve, self.act, self.pool = (self.queues[k] for k in ("pe", "dve", "act", "pool"))
        self.load = self.queues[f"load{self.number}"]

    def round_before(self, own_lane):
        tokens = []
        for key, lane in self.block.lanes.items():
            last = self.block.plan.get((self.block.name, key, self.number))
            if last is not None and (lane is not own_lane or lane.chained):
                token = Step(self.queues[key], None, (), {}, (), False)
                token.number = last - lane.per_round
                tokens.append(token)
        return tokens


class Block:

    def __init__(self, core, name, plan):
        self.core, self.nc, self.name, self.plan = core, core.nc, name, plan
        nc = core.nc
        self.lanes = {}
        for key, engine, chained, step in (("pe", nc.tensor, False, 1), ("dve", nc.vector, True, 1),
                                           ("act", nc.scalar, True, 1), ("pool", nc.gpsimd, True, 1),
                                           ("load0", nc.sync, True, 16), ("load1", nc.sync, True, 16)):
            self.lanes[key] = Lane(nc, engine, f"{name}_{key}", plan.get((name, key), 1), chained,
                                   core.idle[key], step)

    def weight(self, name):
        at, rows, cols = self.core.places[self.name][2][name]
        return self.core.weight_room[self.name][0:rows, at:at + cols]

    def iteration(self, i, body, contexts, rooms):
        turns = []
        for context, room in zip(contexts, rooms):
            context.begin()
            body(context, i * len(contexts) + context.number, room)
            mine = []
            for step in context.steps:
                if mine and step.queue is context.pe and mine[-1][-1].queue is context.pe and not mine[-1][-1].counted:
                    mine[-1].append(step)
                else:
                    mine.append([step])
            turns.append(mine)
        order = []
        for k in range(max(len(mine) for mine in turns)):
            for mine in turns:
                order += mine[k] if k < len(mine) else []
        for lane in self.lanes.values():
            lane.count, lane.reached = 0, {}
        for step in order:
            if step.counted:
                step.queue.lane.count += 1
                step.number = step.queue.lane.count
        for step in order:
            step.queue.lane.emit(step, i)
        for key, lane in self.lanes.items():
            self.plan[(self.name, key)] = lane.count
            for context in contexts:
                counted = [s.number for s in context.steps if s.queue.lane is lane and s.counted]
                if counted:
                    self.plan[(self.name, key, context.number)] = counted[-1]


class Core:
    pass


def bcast(ap, axis, n):
    return ap.unsqueeze(axis).to_broadcast([*ap.shape[:axis], n, *ap.shape[axis:]])


def layer_norm(b, out, x, eps, scratch, after=()):
    stats, moments, rstd = scratch
    n = x.shape[1]
    for t in range(n):
        b.dve.do(b.nc.vector.bn_stats, stats[:, t, :], x[:, t, :], after=after)
    for t in range(n):
        b.dve.do(b.nc.vector.bn_aggr, moments[:, t, :], stats[:, t, :], alone=True)
    scaled = inverse_root(b, rstd[:, 0:n], moments[:, 0:n, 1], 1.0, eps)
    for t in range(n):
        token = b.dve.do(b.nc.vector.tensor_scalar, out[:, t, :], x[:, t, :], moments[:, t, 0:1], rstd[:, t:t + 1],
                         ALU.subtract, ALU.mult, after=(scaled,))
    return token


def inverse_root(b, out, x, scale, eps, guard=ALU.add):
    summed = b.dve.do(b.nc.vector.tensor_scalar, out, x, scale, eps, ALU.mult, guard)
    return b.pool.do(b.nc.gpsimd.tensor_tensor, out, out, b.core.c["halves"][:, 0:out.shape[1]], ALU.pow,
                     after=(summed,))


def norm_room(nc, ctx, n, name):
    return (ctx.enter_context(nc.sbuf_tensor(f"{name}_stats", [P, n, 6], F32)),
            ctx.enter_context(nc.sbuf_tensor(f"{name}_moments", [P, n, 2], F32)),
            ctx.enter_context(nc.sbuf_tensor(f"{name}_rstd", [P, n], F32)))


def to_features(b, outT, x, bank, after, scale=None, bias=None):
    nc, width = b.nc, x.shape[2]
    done = None
    for first in range(0, x.shape[1], 4):
        n = min(4, x.shape[1] - first)
        room = b.psum[:, bank + first // 4, :]
        for t in range(n):
            b.pe.do(nc.tensor.transpose, room[0:width, t * P:(t + 1) * P], x[:, first + t, :], b.core.c["ident"],
                    after=after)
        turned = b.pe.mark()
        src = room[0:width, 0:n * P]
        dst = outT[0:width, first * P:(first + n) * P]
        if scale is None:
            done = b.act.do(nc.scalar.copy, dst, src, after=(turned,))
        else:
            done = b.act.do(nc.scalar.activation, dst, src, ACT.Identity, bias=bias, scale=scale, after=(turned,))
    return done


def down_project(b, out, hT, w, after, rows_of=None):
    n = hT.shape[1]
    for f in range(n):
        rows = P if rows_of is None else rows_of(f)
        for t in range(b.tiles):
            b.pe.product(out[:, t * P:(t + 1) * P], hT[0:rows, f, t * P:(t + 1) * P],
                    w[0:rows, f * P:(f + 1) * P], start=(f == 0 and t == 0), stop=(f == n - 1),
                    skip_group_check=True, after=after)
    return b.pe.mark()


def pick_largest(b, picked, value, best, weight, first, n_picks, after=()):
    T, E = value.shape[1], value.shape[2]
    nc, dve = b.nc, b.dve
    order = bcast(first[:, 0:E], 1, T)
    token = None
    for r in range(n_picks):
        top = best[:, 0:T]
        dve.do(nc.vector.tensor_reduce, top, value, AX, ALU.max, after=after)
        dve.do(nc.vector.tensor_tensor, weight, value, bcast(top, 2, E), ALU.is_equal)
        dve.do(nc.vector.tensor_tensor, weight, weight, order, ALU.mult)
        dve.do(nc.vector.tensor_reduce, top, weight, AX, ALU.max)
        token = dve.do(nc.vector.tensor_tensor, picked[r], weight, bcast(top, 2, E), ALU.is_equal)
        if r < n_picks - 1:
            dve.do(nc.vector.scalar_tensor_tensor, value, picked[r], NEG, value, ALU.mult, ALU.add)
    return token


def block_L0x(b, i, m):
    nc, psum, c = b.nc, b.psum, b.core.c
    x = b.core.x[:, bass.ts(i, b.tiles), :]
    got_ctx = b.load.do(nc.sync.dma_start, m["ctxT"][:], b.core.ctxT[:, bass.ts(i, b.ctok)])
    normed = layer_norm(b, m["xn"], x, LN_EPS, m["norm"])
    turned = to_features(b, m["xT"], m["xn"], 0, (normed,))
    for h in range(2):
        b.pe.product(psum[0:64, 2 + h, :], b.weight("wt"), m["ctxT"][:, h * BANK:(h + 1) * BANK],
                start=True, stop=True, after=(got_ctx,))
    pt = b.pe.mark()
    b.pe.product(psum[0:64, 1, :], b.weight("wv"), m["xT"][:], start=True, stop=True, after=(turned,))
    pv = b.pe.mark()
    t_done = b.act.do(nc.scalar.activation, m["tT"][0:64, :], psum[0:64, 2:4, :].rearrange("p a b -> p (a b)"), ACT.Identity,
                      bias=b.weight("bt"), scale=1.0, after=(pt,))
    v_done = b.act.do(nc.scalar.activation, m["vT"][0:64, :], psum[0:64, 1, :], ACT.Identity, bias=b.weight("bv"), scale=1.0,
                      after=(pv,))
    t_sq = b.pool.do(nc.gpsimd.tensor_tensor, m["t2"][:], m["tT"][:], m["tT"][:], ALU.mult, after=(t_done,))
    v_sq = b.pool.do(nc.gpsimd.tensor_tensor, m["v2"][:], m["vT"][:], m["vT"][:], ALU.mult, after=(v_done,))
    for s in range(b.seqs):
        q = slice(64 * (s % 2), 64 * (s % 2) + 64)
        b.pe.product(psum[q, 0, (s // 2) * P:(s // 2 + 1) * P], m["vT"][:, s * S:(s + 1) * S],
                m["tT"][:, s * SC:(s + 1) * SC], start=True, stop=True, after=(v_done, t_done))
    for s in range(b.seqs):
        q = slice(64 * (s % 2), 64 * (s % 2) + 64)
        b.pe.product(psum[q, 2, (s // 2) * P:(s // 2 + 1) * P], c["ones"][:, 0:64],
                m["t2"][:, s * SC:(s + 1) * SC], start=True, stop=True, after=(t_sq, t_done))
    for t in range(b.tiles):
        b.pe.product(psum[:, 1, t:t + 1], m["v2"][:, t * P:(t + 1) * P], c["ones"][:, 0:1],
                start=True, stop=True, after=(v_sq,))
    pd = b.pe.mark()
    b.dve.do(nc.vector.tensor_copy, m["vn"][:], psum[:, 1, 0:b.tiles], after=(pd,))
    for t in range(b.tiles):
        b.dve.do(nc.vector.tensor_scalar, m["r"][:, t, :], psum[:, 2, t * P:(t + 1) * P], m["vn"][:, t:t + 1], 1e-16,
                 ALU.mult, ALU.max)
    scaled = b.act.do(nc.scalar.activation, m["r"][:], m["r"][:], ACT.Sqrt, after=(b.dve.now(),))
    b.dve.do(nc.vector.reciprocal, m["r"][:], m["r"][:], after=(scaled,))
    b.dve.do(nc.vector.tensor_tensor, m["r"][:], m["r"][:], psum[:, 0, :].rearrange("p (t d) -> p t d", t=b.tiles),
             ALU.mult)
    b.dve.do(nc.vector.tensor_tensor, x, x, m["r"][:], ALU.add)


def room_L0x(nc, ctx, g):
    sb = lambda n, *shape, dt=F32: ctx.enter_context(nc.sbuf_tensor(f"{g.tag}L0x_{n}", list(shape), dt))
    return {"norm": norm_room(nc, ctx, g.tiles, g.tag + "L0x_norm"), "xn": sb("xn", P, g.tiles, D), "xT": sb("xT", P, g.tok),
            "ctxT": sb("ctxT", CX, g.ctok), "tT": sb("tT", P, g.ctok), "vT": sb("vT", P, g.tok), "t2": sb("t2", P, g.ctok),
            "v2": sb("v2", P, g.tok), "vn": sb("vn", P, g.tiles), "r": sb("r", P, g.tiles, D)}


def once_L0x(b, m):
    for name in ("tT", "vT"):
        b.nc.vector.memset(m[name][64:P], 0.0)


def phi(b, out, src, low, after):
    nc = b.nc
    cut = b.dve.do(nc.vector.tensor_scalar, low, src, 0.0, None, ALU.min, after=after)
    grown = b.act.do(nc.scalar.activation, low, low, ACT.Exp, after=(cut,))
    return b.dve.do(nc.vector.scalar_tensor_tensor, out, src, 0.0, low, ALU.max, ALU.add, after=(grown,))


def linear_attention(b, m, xT, ready, same, head, heads, eps):
    nc, psum = b.nc, b.psum
    b.pe.product(psum[:, 0, :], b.weight("wq"), xT[:], start=True, stop=True, after=(ready,))
    pq = b.pe.mark()
    kv = psum[:, 1:3, :].rearrange("p a (t c) -> p (a t) c", c=256)
    for t in range(b.tiles):
        b.pe.product(kv[:, t, 0:P], xT[:, t * P:(t + 1) * P], b.weight("wk"), start=True, stop=True)
        b.pe.product(kv[:, t, P:256], xT[:, t * P:(t + 1) * P], b.weight("wv"), start=True, stop=True)
    pkv = b.pe.mark()
    for r in range(2):
        v_done = b.act.do(nc.scalar.activation, m["va"][:, :, r, 0:P], kv[:, :, P:256], ACT.Copy,
                          scale=b.core.c["parity"][:, r:r + 1], after=(pkv,))
    q_done = phi(b, m["qT"][:], psum[:, 0, :], m["qlow"][:], (pq,))
    k_done = phi(b, m["k"][:], kv[:, :, 0:P], m["klow"][:], (v_done,))
    for t in range(b.tiles):
        b.pe.product(psum[:, t, 0:2 * (P + 1)], m["k"][:, t, :], m["va"][:, t, :, :].rearrange("p r d -> p (r d)"),
                     start=True, stop=True, after=(v_done, k_done, q_done))
    cross = psum[:, :, 0:2 * (P + 1)].rearrange("p t (r d) -> p t r d", r=2)
    kv_pair = m["kv"][:].rearrange("p (t r) d -> p t r d", r=2)
    pc = b.pe.mark()
    for r in range(2):
        b.dve.do(nc.vector.tensor_tensor, kv_pair[:, :, r, 0:P], cross[:, :, r, 0:P], bcast(same, 1, b.tiles), ALU.mult,
                 after=(pc,))
        kv_done = b.dve.do(nc.vector.tensor_tensor, kv_pair[:, :, r, P:P + heads],
                           cross[:, :, r, P:P + 1].to_broadcast([P, b.tiles, heads]), bcast(head, 1, b.tiles), ALU.mult)
    out = psum[:, 0:2, :].rearrange("p a (t c) -> p (a t) c", c=256)
    for t in range(b.tiles):
        for r in range(2):
            q = slice(64 * r, 64 * r + 64)
            b.pe.product(out[q, t, 0:P + heads], m["qT"][:, t * P + 64 * r:t * P + 64 * r + 64],
                    m["kv"][:, 2 * t + r, :], start=True, stop=True, after=(kv_done,))
    po = b.pe.mark()
    b.dve.do(nc.vector.tensor_scalar, m["z"][:], out[:, :, P:P + heads], eps, None, ALU.add, after=(po,))
    b.dve.do(nc.vector.reciprocal, m["z"][:], m["z"][:])
    msg = m["msg"][:].rearrange("p t (h d) -> p t h d", h=heads)
    return b.dve.do(nc.vector.tensor_tensor, msg, out[:, :, 0:P].rearrange("p t (h d) -> p t h d", h=heads),
                    bcast(m["z"][:], 3, P // heads), ALU.mult)


def room_linear(sb, g, heads):
    return {"qT": sb("qT", P, g.tok), "qlow": sb("qlow", P, g.tok), "k": sb("k", P, g.tiles, D), "klow": sb("klow", P, g.tiles, D),
            "va": sb("va", P, g.tiles, 2, D + 1), "kv": sb("kv", P, g.seqs, D + heads), "z": sb("z", P, g.tiles, heads),
            "msg": sb("msg", P, g.tiles, D)}


def block_L0a(b, i, m):
    nc, psum, c = b.nc, b.psum, b.core.c
    x = b.core.x[:, bass.ts(i, b.tiles), :]
    layer_norm(b, m["xin"], x, LN_EPS, m["norm"])
    normed = layer_norm(b, m["x2"], m["xin"], LN_EPS, m["norm"])
    ready = to_features(b, m["xT"], m["x2"], 3, (normed,), b.weight("g1"), b.weight("be1"))
    linear_attention(b, m, m["xT"], ready, c["same16"], c["head16"], 8, 1e-6)
    b.dve.do(nc.vector.tensor_tensor, m["xin"][:], m["xin"][:], m["msg"][:], ALU.add)
    normed = layer_norm(b, m["x2"], m["xin"], LN_EPS, m["norm"])
    ready = to_features(b, m["xT"], m["x2"], 3, (normed,), b.weight("g2"), b.weight("be2"))
    biased = b.pool.do(nc.gpsimd.tensor_tensor, m["xin"][:], m["xin"][:], bcast(b.weight("b2"), 1, b.tiles), ALU.add,
                       after=(normed,))
    for f in range(4):
        b.pe.product(psum[:, f, :], b.weight("w1")[:, f * P:(f + 1) * P], m["xT"][:], start=True,
                stop=True, after=(ready,))
        grown = b.act.do(nc.scalar.activation, m["hT"][:, f, :], psum[:, f, :], ACT.Gelu, bias=b.weight("b1")[:, f:f + 1],
                         scale=1.0, after=(b.pe.mark(),))
    down = down_project(b, psum[:, 0, :], m["hT"], b.weight("w2"), (grown,))
    b.dve.do(nc.vector.tensor_tensor, m["xin"][:], m["xin"][:], psum[:, 0, :].rearrange("p (t d) -> p t d", t=b.tiles),
             ALU.add, after=(down, biased))
    b.dve.do(nc.vector.tensor_tensor, x, x, m["xin"][:], ALU.add)


def room_L0a(nc, ctx, g):
    sb = lambda n, *shape, dt=F32: ctx.enter_context(nc.sbuf_tensor(f"{g.tag}L0a_{n}", list(shape), dt))
    m = {"norm": norm_room(nc, ctx, g.tiles, g.tag + "L0a_norm"), "xin": sb("xin", P, g.tiles, D), "x2": sb("x2", P, g.tiles, D),
         "xT": sb("xT", P, g.tok), "hT": sb("hT", P, 4, g.tok)}
    m.update(room_linear(sb, g, 8))
    return m


def once_ones(b, m):
    b.nc.vector.tensor_copy(m["va"][:, :, :, D], bcast(b.core.c["parity"][:, 0:2], 1, b.tiles))


def experts(b, m, xT, spread, hidden, after):
    nc, psum = b.nc, b.psum
    n = -(-hidden // P)
    free, finished, down = (None, None, None), [], []
    for f in range(n):
        rows = min(P, hidden - f * P)
        cols = slice(f * P, f * P + rows)
        waits = [(x,) if x is not None else () for x in free]
        b.pe.product(psum[0:rows, 1, 0:b.tok], b.weight("gate")[:, cols], xT[:], start=True, stop=True, after=(*after, *waits[0]))
        pg = b.pe.mark()
        b.pe.product(psum[0:rows, 2, 0:b.tok], b.weight("up")[:, cols], xT[:], start=True, stop=True, after=waits[1])
        pu = b.pe.mark()
        b.pe.product(psum[0:rows, 3, 0:b.tok], spread[:, cols], m["combT"][:], start=True, stop=True, after=waits[2])
        pc = b.pe.mark()
        if f >= 2:
            b.act.wait(down[f - 2])
        h = m["h"][0:rows, f % 2, :]
        s_done = b.act.do(nc.scalar.activation, h, psum[0:rows, 1, 0:b.tok], ACT.Silu, after=(pg,))
        gated = b.dve.do(nc.vector.tensor_tensor, h, h, psum[0:rows, 2, 0:b.tok], ALU.mult, after=(s_done, pu))
        finished.append(b.dve.do(nc.vector.tensor_tensor, h, h, psum[0:rows, 3, 0:b.tok], ALU.mult, after=(pc,)))
        free = (s_done, gated, finished[f])
        if f >= 1:
            down.append(expert_down(b, m, f - 1, n, hidden, finished[f - 1]))
    down.append(expert_down(b, m, n - 1, n, hidden, finished[n - 1]))
    return down[-1]


def expert_down(b, m, f, n, hidden, ready):
    rows = min(P, hidden - f * P)
    for t in range(b.tiles):
        b.pe.product(b.psum[:, 0, t * P:(t + 1) * P], m["h"][0:rows, f % 2, t * P:(t + 1) * P],
                b.weight("down")[0:rows, f * P:(f + 1) * P], start=(f == 0 and t == 0), stop=(f == n - 1),
                skip_group_check=True, after=(ready,))
    return b.pe.mark()


def turn_combine(b, m, comb, n, bank, after):
    nc, dve = b.nc, b.dve
    part, rest, comb = m["parts"][:], m["rest"][:], comb[:]
    dve.do(nc.vector.tensor_copy, part[:, :, 0:n], comb, after=after)
    dve.do(nc.vector.tensor_tensor, rest, comb, part[:, :, 0:n], ALU.subtract)
    dve.do(nc.vector.tensor_copy, part[:, :, n:2 * n], rest)
    dve.do(nc.vector.tensor_tensor, rest, rest, part[:, :, n:2 * n], ALU.subtract)
    split = dve.do(nc.vector.tensor_copy, part[:, :, 2 * n:3 * n], rest)
    return turn_parts(b, m["combT"][0:3 * n, :], part, 3 * n, bank, (split,))


def once_combine(b, m):
    b.nc.vector.memset(m["combT"][:], 0.0)


def turn_parts(b, out, part, n, bank, after):
    for t in range(b.tiles):
        b.pe.product(b.psum[0:n, bank, t * P:(t + 1) * P], part[:, t, 0:n], b.core.half["ident"], start=True, stop=True,
                     after=after)
    return b.act.do(b.nc.scalar.copy, out, b.psum[0:n, bank, 0:b.tok], after=(b.pe.mark(),))


def logits_of(b, xT, w, n, bank, after):
    out = b.psum[:, bank, 0:b.tiles * n].rearrange("p (t e) -> p t e", t=b.tiles)
    for t in range(b.tiles):
        b.pe.product(out[:, t, :], xT[:, t * P:(t + 1) * P], w, start=True, stop=True, after=after)
    return out, b.pe.mark()


def block_L0f(b, i, m):
    nc, psum, c = b.nc, b.psum, b.core.c
    x = b.core.x[:, bass.ts(i, b.tiles), :]
    normed = layer_norm(b, m["xn"], x, LN_EPS, m["norm"])
    ready = to_features(b, m["xT"], m["xn"], 0, (normed,))
    logits, pl = logits_of(b, m["xT"], b.weight("router"), EXPERTS0, 3, (ready,))
    scored = b.act.do(nc.scalar.activation, m["score"][:], logits, ACT.Sigmoid, after=(pl,))
    dve, tt = b.dve, nc.vector.tensor_tensor
    dve.do(tt, m["choice"][:], m["score"][:], bcast(b.weight("rbias"), 1, b.tiles), ALU.add, after=(scored,))
    pair = m["choice"][:].rearrange("p t (g a c) -> p (t g) a c", g=4, a=2)
    hi, lo, a1, a2, gs = (m[k][:] for k in ("hi", "lo", "a1", "a2", "gs"))
    dve.do(tt, hi, pair[:, :, :, 0], pair[:, :, :, 1], ALU.max)
    dve.do(tt, lo, pair[:, :, :, 0], pair[:, :, :, 1], ALU.min)
    dve.do(tt, a1, hi[:, :, 0], hi[:, :, 1], ALU.max)
    dve.do(tt, a2, hi[:, :, 0], hi[:, :, 1], ALU.min)
    dve.do(tt, gs, lo[:, :, 0], lo[:, :, 1], ALU.max)
    dve.do(tt, gs, gs, a2, ALU.max)
    dve.do(tt, gs, gs, a1, ALU.add)
    groups = [m["pick"][:, r, :, 0:4] for r in range(2)]
    pick_largest(b, groups, gs.rearrange("p (t g) -> p t g", g=4), m["best"], m["w"][:, :, 0:4], c["first"], 2)
    dve.do(tt, groups[0], groups[0], groups[1], ALU.add)
    gmask = m["gmask"][:]
    dve.do(nc.vector.tensor_copy, gmask.rearrange("p t (g e) -> p t g e", g=4), bcast(groups[0], 3, 4))
    dve.do(tt, m["choice"][:], m["choice"][:], gmask, ALU.mult)
    dve.do(nc.vector.tensor_scalar, gmask, gmask, 1.0, 1e9, ALU.subtract, ALU.mult)
    dve.do(tt, m["choice"][:], m["choice"][:], gmask, ALU.add)
    picks = [m["pick"][:, r, :, :] for r in range(4)]
    pick_largest(b, picks, m["choice"][:], m["best"], m["w"][:], c["first"], 4)
    for r in range(1, 4):
        dve.do(tt, picks[0], picks[0], picks[r], ALU.add)
    dve.do(tt, m["w"][:], picks[0], m["score"][:], ALU.mult)
    dve.do(nc.vector.tensor_reduce, m["best"][:], m["w"][:], AX, ALU.add)
    dve.do(nc.vector.tensor_scalar, m["best"][:], m["best"][:], 1e-20, None, ALU.add)
    dve.do(nc.vector.reciprocal, m["best"][:], m["best"][:])
    combined = dve.do(nc.vector.scalar_tensor_tensor, m["w"][:], m["w"][:], 2.5, bcast(m["best"][:], 2, EXPERTS0),
                      ALU.mult, ALU.mult)
    comb_ready = turn_combine(b, m, m["w"], EXPERTS0, 3, (combined,))
    done = experts(b, m, m["xT"], b.core.half["spread0"], EXPERTS0 * HID0, (comb_ready,))
    dve.do(tt, x, x, psum[:, 0, :].rearrange("p (t d) -> p t d", t=b.tiles), ALU.add, after=(done,))


def room_L0f(nc, ctx, g):
    sb = lambda n, *shape, dt=F32: ctx.enter_context(nc.sbuf_tensor(f"{g.tag}L0f_{n}", list(shape), dt))
    return {"norm": norm_room(nc, ctx, g.tiles, g.tag + "L0f_norm"), "xn": sb("xn", P, g.tiles, D), "xT": sb("xT", P, g.tok),
            "score": sb("score", P, g.tiles, 16), "choice": sb("choice", P, g.tiles, 16), "gmask": sb("gmask", P, g.tiles, 16),
            "hi": sb("hi", P, 4 * g.tiles, 2), "lo": sb("lo", P, 4 * g.tiles, 2), "a1": sb("a1", P, 4 * g.tiles),
            "a2": sb("a2", P, 4 * g.tiles), "gs": sb("gs", P, 4 * g.tiles), "pick": sb("pick", P, 4, g.tiles, 16),
            "best": sb("best", P, g.tiles), "w": sb("w", P, g.tiles, 16), "combT": sb("combT", P, g.tok, dt=BF16),
            "parts": sb("parts", P, g.tiles, 48, dt=BF16), "rest": sb("rest", P, g.tiles, 16),
            "h": sb("h", P, 2, g.tok)}


def block_L1x(b, i, m):
    nc, psum, c = b.nc, b.psum, b.core.c
    dve, act, pool, pe = b.dve, b.act, b.pool, b.pe
    tt = nc.vector.tensor_tensor
    x = b.core.x[:, bass.ts(i, b.tiles), :]
    heads, width, keys = 2, 64, SC + S
    got = b.load.do(nc.sync.dma_start, m["ctx"][:], b.core.ctx_tok[:, bass.ts(i, b.seqs), :])
    pairs = b.core.mask[:, bass.ts(i, b.tiles), :]
    for r in range(2):
        got_mask = b.load.do(nc.sync.dma_start, m["mask"][64 * r:64 * r + 64, :, :],
                             pairs[r:r + 1, :, :].to_broadcast([64, b.tiles, SC // 4]))
    normed = layer_norm(b, m["cn"], m["ctx"][:], LN_EPS, m["norm8"], (got,))
    c_ready = to_features(b, m["cT"], m["cn"], 0, (normed,), b.weight("xg"), b.weight("xb"))
    layer_norm(b, m["xn"], x, LN_EPS, m["norm"])
    normed = layer_norm(b, m["xn"], m["xn"], LN_EPS, m["norm"])
    l_ready = to_features(b, m["lT"], m["xn"], 1, (normed,), b.weight("lg"), b.weight("lb"))
    wql = b.weight("wql")
    qk = psum[:, 2, :].rearrange("p (t c) -> p t c", c=256)
    for t in range(b.tiles):
        pe.product(qk[:, t, :], m["lT"][:, t * P:(t + 1) * P], wql[:, 0:256], start=True, stop=True, after=(l_ready,))
    p_qk = pe.mark()
    for s in range(b.seqs):
        pe.product(psum[0:64, 3, s * P:(s + 1) * P], m["lT"][:, s * S:(s + 1) * S], wql[:, 256:384],
                   start=True, stop=True)
    p_v = pe.mark()
    qk_done = act.do(nc.scalar.copy, m["qk"][:], qk, after=(p_qk,))
    vl_done = act.do(nc.scalar.copy, m["vl"][0:64, :, :], psum[0:64, 3, :].rearrange("p (s d) -> p s d", d=P), after=(p_v,))
    kv = psum[:, 0:2, :].rearrange("p a (s c) -> p (a s) c", c=256)
    for s in range(b.seqs):
        pe.product(kv[:, s, :], m["cT"][:, s * SC:(s + 1) * SC], b.weight("wkv"), start=True, stop=True,
                   after=(c_ready, l_ready))
    kv_done = act.do(nc.scalar.copy, m["kv"][:], kv, after=(pe.mark(),))
    squares = pool.do(nc.gpsimd.tensor_tensor, m["sq"][:, 0:b.tiles, :], m["qk"][:], m["qk"][:], ALU.mult, after=(qk_done,))
    dve.do(nc.vector.tensor_reduce, m["ss"][:], m["sq"][:, 0:b.tiles, :].rearrange("p t (h d) -> p (t h) d", h=4), AX,
           ALU.add, after=(squares,))
    scaled = inverse_root(b, m["ss"][:], m["ss"][:], 1.0 / width, 1e-16, ALU.max)
    view = m["qk"][:].rearrange("p t (h d) -> p (t h) d", h=4)
    qk_normed = dve.do(tt, view, view, bcast(m["ss"][:], 2, width), ALU.mult, after=(scaled,))
    csq = m["sq"][:].rearrange("p t (a c) -> p (t a) c", a=2)
    squares = pool.do(nc.gpsimd.tensor_tensor, csq, m["kv"][:, :, 0:P], m["kv"][:, :, 0:P], ALU.mult,
                      after=(kv_done, qk_normed))
    dve.do(nc.vector.tensor_reduce, m["css"][:], csq.rearrange("p s (h d) -> p s h d", h=heads), AX, ALU.add,
           after=(squares,))
    scaled = inverse_root(b, m["css"][:].rearrange("p s h -> p (s h)"), m["css"][:].rearrange("p s h -> p (s h)"),
                          1.0 / width, 1e-16, ALU.max)
    kview = m["kv"][:, :, 0:P].rearrange("p s (h d) -> p s h d", h=heads)
    k_normed = dve.do(tt, kview, kview, bcast(m["css"][:], 3, width), ALU.mult, after=(scaled,))
    for h in range(heads):
        q_ready = to_features(b, m["qT"][:, h, :], m["qk"][:, :, 0:P], 2, (qk_normed,) if h == 0 else (q_ready,),
                              b.weight("qg")[:, h:h + 1], 0.0)
    kl_ready = to_features(b, m["klT"], m["qk"][:, :, P:256], 3, (vl_done,), b.weight("kg"), 0.0)
    kc_ready = to_features(b, m["kcT"], m["kv"][:, :, 0:P], 0, (k_normed, kv_done), b.weight("kg"), 0.0)
    for t in range(b.tiles):
        for h in range(heads):
            for first, n, kT in ((0, SC, m["kcT"]), (SC, S, m["klT"])):
                for r in range(2):
                    s = 2 * t + r
                    pe.product(psum[64 * r:64 * r + 64, h, t * keys + first:t * keys + first + n],
                               m["qT"][:, h, s * S:(s + 1) * S], kT[:, s * n:(s + 1) * n], start=True, stop=True,
                               after=(q_ready, kl_ready, kc_ready))
    p_s = pe.mark()
    dve.do(nc.vector.tensor_scalar, m["mb"][:], m["mask"][:].bitcast(U8), 1.0, 3.0e38, ALU.subtract, ALU.mult,
           after=(got_mask,))
    for h in range(heads):
        src = psum[:, h, 0:b.tiles * keys].rearrange("p (t k) -> p t k", k=keys)
        dst = m["p"][:, h, :, :]
        added = dve.do(tt, dst[:, :, 0:SC], src[:, :, 0:SC], m["mb"][:], ALU.add, after=(p_s,))
        copied = act.do(nc.scalar.copy, dst[:, :, SC:keys], src[:, :, SC:keys], after=(added,))
    prob = m["p"][:].rearrange("p h t k -> p (h t) k")
    dve.do(nc.vector.tensor_reduce, m["mx"][:], prob, AX, ALU.max, after=(copied,))
    lowered = dve.do(tt, prob, prob, bcast(m["mx"][:], 2, keys), ALU.subtract)
    grown = act.do(nc.scalar.activation, prob, prob, ACT.Exp, scale=width ** -0.5, after=(lowered,))
    dve.do(nc.vector.tensor_reduce, m["mx"][:], prob, AX, ALU.add, after=(grown,))
    dve.do(nc.vector.reciprocal, m["mx"][:], m["mx"][:])
    p_done = dve.do(tt, prob, prob, bcast(m["mx"][:], 2, keys), ALU.mult)
    for n in range(heads * b.tiles):
        pe.do(nc.tensor.transpose, psum[:, 2, n * P:(n + 1) * P], prob[:, n, 0:SC], c["ident"], after=(p_done,))
    p_c = pe.mark()
    for n in range(heads * b.tiles):
        pe.do(nc.tensor.transpose, psum[0:64, 3, n * P:(n + 1) * P], prob[:, n, SC:keys], c["ident"])
    p_l = pe.mark()
    pc_done = act.do(nc.scalar.copy, m["pcT"][:], psum[:, 2, :], after=(p_c,))
    pl_done = dve.do(nc.vector.tensor_copy, m["plT"][0:64, :], psum[0:64, 3, :], after=(p_l,))
    for s in range(b.seqs):
        t, r = s // 2, s % 2
        for h in range(heads):
            f = slice(width * h, width * h + width)
            q = slice((h * b.tiles + t) * P + 64 * r, (h * b.tiles + t) * P + 64 * r + 64)
            pe.product(psum[f, 0, s * S:(s + 1) * S], m["kv"][:, s, P + width * h:P + width * h + width],
                       m["pcT"][:, q], start=True, stop=False, skip_group_check=True, after=(pc_done, pl_done))
            pe.product(psum[f, 0, s * S:(s + 1) * S], m["vl"][:, s, f], m["plT"][:, q], start=False, stop=True,
                       skip_group_check=True)
    o_done = act.do(nc.scalar.copy, m["oT"][:], psum[:, 0, 0:b.tok], after=(pe.mark(),))
    project_out(b, x, m["oT"], b.weight("wo"), b.weight("bo"), 1, (o_done,))


def project_out(b, x, inT, w, bias, bank, after):
    nc = b.nc
    if bias is not None:
        b.dve.do(nc.vector.tensor_tensor, x, x, bcast(bias, 1, b.tiles), ALU.add)
    for t in range(b.tiles):
        b.pe.product(b.psum[:, bank, t * P:(t + 1) * P], inT[:, t * P:(t + 1) * P], w, start=True, stop=True,
                     after=after)
    return b.dve.do(nc.vector.tensor_tensor, x, x, b.psum[:, bank, 0:b.tok].rearrange("p (t d) -> p t d", t=b.tiles),
                    ALU.add, after=(b.pe.mark(),))


def room_L1x(nc, ctx, g):
    sb = lambda n, *shape, dt=F32: ctx.enter_context(nc.sbuf_tensor(f"{g.tag}L1x_{n}", list(shape), dt))
    return {"norm": norm_room(nc, ctx, g.tiles, g.tag + "L1x_norm"), "norm8": norm_room(nc, ctx, g.seqs, g.tag + "L1x_norm8"),
            "ctx": sb("ctx", P, g.seqs, CX), "mask": sb("mask", P, g.tiles, SC // 4, dt=I32),
            "cn": sb("cn", P, g.seqs, CX), "cT": sb("cT", CX, g.ctok), "xn": sb("xn", P, g.tiles, D), "lT": sb("lT", P, g.tok),
            "qk": sb("qk", P, g.tiles, 256), "vl": sb("vl", P, g.seqs, P), "kv": sb("kv", P, g.seqs, 256),
            "sq": sb("sq", P, g.tiles, 256), "ss": sb("ss", P, 4 * g.tiles), "css": sb("css", P, g.seqs, 2),
            "qT": sb("qT", P, 2, g.tok), "klT": sb("klT", P, g.tok), "kcT": sb("kcT", P, g.ctok), "mb": sb("mb", P, g.tiles, SC),
            "p": sb("p", P, 2, g.tiles, SC + S), "mx": sb("mx", P, 2 * g.tiles), "pcT": sb("pcT", P, g.ctok),
            "plT": sb("plT", P, g.ctok), "oT": sb("oT", P, g.tok)}


def once_L1x(b, m):
    b.nc.vector.memset(m["vl"][64:P], 0.0)
    b.nc.vector.memset(m["plT"][64:P], 0.0)



HEADS, WIDTH, QUAD = 16, 8, 4


def attention_waves(b, m, keys, scale, clip, ready):
    nc, psum, c = b.nc, b.psum, b.core.c
    dve, act, pe = b.dve, b.act, b.pe
    tiles = P // keys
    per_block = P // keys
    n_rows = QUAD * tiles * QUAD
    one = WIDTH + 1
    for w in range(b.tiles // tiles):
        for u in range(tiles):
            for g in range(QUAD):
                for r in range(2):
                    s = 2 * (w * tiles + u) + r
                    out = psum[64 * r:64 * r + 64, g, u * QUAD * keys:(u + 1) * QUAD * keys]
                    pe.product(out.rearrange("p (j k) -> p j k", j=QUAD), m["qx"][:, g, s * S:(s + 1) * S],
                               m["kx"][:, :, s * keys:(s + 1) * keys], start=True, stop=True, after=ready)
        p_s = pe.mark()
        p = m["p"][:].rearrange("p (n k) -> p n k", k=keys)
        s = psum[:, 0:4, :].rearrange("p a (n k) -> p (a n) k", k=keys)
        if clip is not None:
            dve.do(nc.vector.tensor_scalar, p, s, clip / scale, -clip / scale, ALU.min, ALU.max, after=(p_s,))
            s = p
        dve.do(nc.vector.tensor_reduce, m["mx"][:, 0:n_rows], s, AX, ALU.max, after=(p_s,))
        low = dve.do(nc.vector.tensor_tensor, p, s, bcast(m["mx"][:, 0:n_rows], 2, keys), ALU.subtract)
        grown = act.do(nc.scalar.activation, p, p, ACT.Exp, scale=scale, after=(low,))
        for n in range(16):
            pe.do(nc.tensor.transpose, psum[:, n // 4, (n % 4) * P:(n % 4 + 1) * P], m["p"][:, n * P:(n + 1) * P],
                  c["ident"], after=(grown,))
            if n == 7:
                half = pe.mark()
        turned = pe.mark()
        pT = m["pT"][:].rearrange("p (a b) -> p a b", a=4)
        e0 = act.do(nc.scalar.copy, pT[:, 0:2, :], psum[:, 0:2, :], after=(half,))
        e1 = dve.do(nc.vector.tensor_copy, pT[:, 2:4, :], psum[:, 2:4, :], after=(turned,))
        for u in range(tiles):
            for g in range(QUAD):
                for k in range(QUAD // per_block):
                    n = (g * tiles + u) * (QUAD // per_block) + k
                    h = QUAD * g + per_block * k
                    pe.product(psum[:, u, h * 2 * one:(h + per_block) * 2 * one], m["pT"][:, n * P:(n + 1) * P],
                               m["va"][:, w * tiles + u, h:h + per_block, :, :].rearrange("p h r e -> p (h r e)"),
                               start=True, stop=True, after=(e0, e1))
        p_o = pe.mark()
        out = psum[:, 0:tiles, 0:2 * HEADS * one].rearrange("p u (h r e) -> p u h r e", h=HEADS, r=2)
        att = m["att"][:, w * tiles:(w + 1) * tiles, :].rearrange("p u (h d) -> p u h d", h=HEADS)
        for r in range(2):
            q = slice(64 * r, 64 * r + 64)
            z = m["z"][q, 0:tiles, :]
            dve.do(nc.vector.reciprocal, z, out[q, :, :, r, WIDTH], after=(p_o,))
            done = dve.do(nc.vector.tensor_tensor, att[q], out[q, :, :, r, 0:WIDTH], bcast(z, 3, WIDTH), ALU.mult)
        ready = (done,)
    return done


def room_attention(sb, g, keys):
    return {"xn": sb("xn", P, g.tiles, D), "xT": sb("xT", P, g.tok), "qx": sb("qx", P, QUAD, g.tok),
            "kx": sb("kx", P, QUAD, g.seqs * keys), "va": sb("va", P, g.tiles, HEADS, 2, WIDTH + 1), "p": sb("p", P, 2048),
            "pT": sb("pT", P, 2048), "mx": sb("mx", P, 32), "z": sb("z", P, 2, HEADS), "att": sb("att", P, g.tiles, D)}


def rotate(b, out, src, partner, cos, sin, twin, after):
    nc = b.nc
    seqs = lambda ap: ap.rearrange("p (s k) -> p s k", k=S)
    b.dve.do(nc.vector.tensor_tensor, seqs(out), seqs(src), bcast(cos, 1, b.seqs), ALU.mult, after=after)
    both = b.dve.do(nc.vector.tensor_tensor, seqs(twin), seqs(partner), bcast(sin, 1, b.seqs), ALU.mult)
    return b.pool.do(nc.gpsimd.tensor_tensor, out, out, twin, ALU.add, after=(both,))


def block_L1a(b, i, m):
    nc, psum, c = b.nc, b.psum, b.core.c
    x = b.core.x[:, bass.ts(i, b.tiles), :]
    normed = layer_norm(b, m["xn"], x, LN_EPS, m["norm"])
    ready = to_features(b, m["xT"], m["xn"], 3, (normed,))
    for n, w in enumerate(("wk", "wkp", "wq", "wqp")):
        b.pe.product(psum[:, n, :], b.weight(w), m["xT"][:], start=True, stop=True, after=(ready,))
        if n == 1:
            pk = b.pe.mark()
    pq = b.pe.mark()
    twice = b.pool.do(nc.gpsimd.tensor_copy, m["x2"][:], bcast(m["xT"][:].rearrange("p (s k) -> p s k", k=S), 2, 2),
                      after=(ready,), alone=True)
    k_ready = rotate(b, m["kT"][:], psum[:, 0, :], psum[:, 1, :], c["cos8"], c["sin8"], m["twin"][:], (pk,))
    for s in range(b.seqs):
        b.pe.product(psum[:, s // 4, (s % 4) * P:(s % 4 + 1) * P], m["x2"][:, s, :, :].rearrange("p a k -> p (a k)"),
                     b.weight("wv"), start=True, stop=True, after=(twice, k_ready))
    pv = b.pe.mark()
    q_ready = rotate(b, m["qT"][:], psum[:, 2, :], psum[:, 3, :], c["cos8"], c["sin8"], m["twin2"][:], (pq,))
    values = psum[:, 0:2, :].rearrange("p a (t r h d) -> p (a t) h r d", r=2, h=HEADS, d=WIDTH)
    for r in range(2):
        v_ready = b.dve.do(nc.vector.tensor_tensor, m["va"][:, :, :, r, 0:WIDTH], values[:, :, :, r, :],
                           bcast(bcast(c["parity"], 1, b.tiles), 3, WIDTH), ALU.mult, after=(pv,))
    for j in range(QUAD):
        k_kept = b.dve.do(nc.vector.tensor_scalar, m["kx"][:, j, :], m["kT"][:], c["lane4"][:, j:j + 1], None, ALU.mult,
                          after=(k_ready,))
    for g in range(QUAD):
        q_kept = b.act.do(nc.scalar.activation, m["qx"][:, g, :], m["qT"][:], ACT.Copy, scale=c["quad"][:, g:g + 1],
                          after=(q_ready,))
    done = attention_waves(b, m, S, WIDTH ** -0.5, None, (k_kept, q_kept, v_ready))
    turned = to_features(b, m["xT"], m["att"], 2, (done,))
    project_out(b, x, m["xT"], b.weight("wo"), b.weight("bo"), 3, (turned,))


def room_L1a(nc, ctx, g):
    sb = lambda n, *shape, dt=F32: ctx.enter_context(nc.sbuf_tensor(f"{g.tag}L1a_{n}", list(shape), dt))
    return {"norm": norm_room(nc, ctx, g.tiles, g.tag + "L1a_norm"), **room_attention(sb, g, S), "twin": sb("twin", P, g.tok),
            "qT": sb("qT", P, g.tok), "kT": sb("kT", P, g.tok), "x2": sb("x2", P, g.seqs, 2, S), "twin2": sb("twin2", P, g.tok)}


def once_L1a(b, m):
    nc, parity = b.nc, b.core.c["parity"]
    for r in range(2):
        nc.vector.tensor_copy(m["va"][:, :, :, r, WIDTH], bcast(parity, 1, b.tiles))


def context_attention(b, i, m, clip):
    nc, psum, c = b.nc, b.psum, b.core.c
    x = b.core.x[:, bass.ts(i, b.tiles), :]
    got = b.load.do(nc.sync.dma_start, m["ctxT"][:], b.core.ctxT[:, bass.ts(i, b.ctok)])
    normed = layer_norm(b, m["xn"], x, LN_EPS, m["norm"])
    for h in range(2):
        b.pe.product(psum[:, h, :], b.weight("wk"), m["ctxT"][:, h * BANK:(h + 1) * BANK], start=True, stop=True,
                     after=(got,))
    pk = b.pe.mark()
    for s in range(b.seqs):
        b.pe.product(psum[:, 2 + s // 4, (s % 4) * P:(s % 4 + 1) * P], m["ctxT"][:, s * SC:(s + 1) * SC],
                     b.weight("wv"), start=True, stop=True)
    pv = b.pe.mark()
    for j in range(QUAD):
        k_ready = b.act.do(nc.scalar.activation, m["kx"][:, j, :].rearrange("p (a b) -> p a b", a=2), psum[:, 0:2, :],
                           ACT.Identity, bias=b.weight("bk")[:, j:j + 1], scale=c["lane4"][:, j:j + 1], after=(pk,))
    values = psum[:, 2:4, :].rearrange("p a (t r h d) -> p (a t) h r d", r=2, h=HEADS, d=WIDTH)
    for r in range(2):
        v_ready = b.dve.do(nc.vector.tensor_tensor, m["va"][:, :, :, r, 0:WIDTH], values[:, :, :, r, :],
                           bcast(b.weight("bv").rearrange("p (h d) -> p h d", h=HEADS), 1, b.tiles), ALU.add, after=(pv,))
    ready = to_features(b, m["xT"], m["xn"], 0, (normed, k_ready))
    b.pe.product(psum[:, 1, :], b.weight("wq"), m["xT"][:], start=True, stop=True, after=(ready,))
    pq = b.pe.mark()
    for g in range(QUAD):
        q_ready = b.act.do(nc.scalar.activation, m["qx"][:, g, :], psum[:, 1, :], ACT.Identity,
                           bias=b.weight("bq")[:, g:g + 1], scale=c["quad"][:, g:g + 1], after=(pq,))
    return attention_waves(b, m, SC, WIDTH ** -0.5, clip, (q_ready, v_ready))


def block_L2x(b, i, m):
    done = context_attention(b, i, m, 10000.0)
    turned = to_features(b, m["xT"], m["att"], 3, (done,))
    project_out(b, b.core.x[:, bass.ts(i, b.tiles), :], m["xT"], b.weight("wo"), b.weight("bo"), 2, (turned,))


def room_L2x(nc, ctx, g, name="L2x"):
    sb = lambda n, *shape, dt=F32: ctx.enter_context(nc.sbuf_tensor(f"{g.tag}{name}_{n}", list(shape), dt))
    return {"norm": norm_room(nc, ctx, g.tiles, g.tag + name + "_norm"), **room_attention(sb, g, SC), "ctxT": sb("ctxT", CX, g.ctok)}


def once_value_ones(b, m):
    b.nc.vector.memset(m["va"][:, :, :, :, WIDTH], 1.0)


def block_L3x(b, i, m):
    nc, psum = b.nc, b.psum
    x = b.core.x[:, bass.ts(i, b.tiles), :]
    done = context_attention(b, i, m, None)
    turned = to_features(b, m["xT"], m["att"], 3, (done,))
    b.dve.do(nc.vector.tensor_tensor, x, x, bcast(b.weight("b2"), 1, b.tiles), ALU.add)
    for f in range(2):
        b.pe.product(psum[:, f, :], b.weight("w1")[:, f * P:(f + 1) * P], m["xT"][:], start=True, stop=True,
                     after=(turned,))
        grown = b.act.do(nc.scalar.activation, m["hT"][:, f, :], psum[:, f, :], ACT.Relu, bias=b.weight("b1")[:, f:f + 1],
                         scale=1.0, after=(b.pe.mark(),))
    down = down_project(b, psum[:, 2, :], m["hT"], b.weight("w2"), (grown,))
    b.dve.do(nc.vector.tensor_tensor, x, x, psum[:, 2, :].rearrange("p (t d) -> p t d", t=b.tiles), ALU.add, after=(down,))


def room_L3x(nc, ctx, g):
    m = room_L2x(nc, ctx, g, "L3x")
    m["hT"] = ctx.enter_context(nc.sbuf_tensor(f"{g.tag}L3x_hT", [P, 2, g.tok], F32))
    return m


def softmax_rows(b, e, logits, bias, best, after):
    nc, dve, n = b.nc, b.dve, e.shape[2]
    dve.do(nc.vector.tensor_tensor, e, logits, bcast(bias, 1, b.tiles), ALU.add, after=after)
    dve.do(nc.vector.tensor_reduce, best, e, AX, ALU.max)
    low = dve.do(nc.vector.tensor_tensor, e, e, bcast(best, 2, n), ALU.subtract)
    grown = b.act.do(nc.scalar.activation, e, e, ACT.Exp, after=(low,))
    dve.do(nc.vector.tensor_reduce, best, e, AX, ALU.add, after=(grown,))
    dve.do(nc.vector.reciprocal, best, best)
    return dve.do(nc.vector.tensor_tensor, e, e, bcast(best, 2, n), ALU.mult)


def block_L1f(b, i, m):
    nc, psum, c = b.nc, b.psum, b.core.c
    dve, act, pe, pool = b.dve, b.act, b.pe, b.pool
    tt = nc.vector.tensor_tensor
    x = b.core.x[:, bass.ts(i, b.tiles), :]
    normed = layer_norm(b, m["xn"], x, LN_EPS, m["norm"])
    ready = to_features(b, m["xT"], m["xn"], 0, (normed,))
    logits, pl = logits_of(b, m["xT"], b.weight("gate"), EXPERTS1, 3, (ready,))
    pe.product(psum[:, 1, :], b.weight("la"), m["xT"][:], start=True, stop=True)
    a_done = act.do(nc.scalar.copy, m["aT"][:], psum[:, 1, :], after=(pe.mark(),))
    softmax_rows(b, m["e"][:], logits, b.weight("gb"), m["best"][:], (pl,))
    dve.do(nc.vector.tensor_copy, m["v"][:], m["e"][:])
    picks = [m["pick"][:, :, r, :] for r in range(2)]
    picked = pick_largest(b, picks, m["v"][:], m["best"], m["w"][:], c["first"], 2)
    both = dve.do(nc.vector.tensor_copy, m["pick16"][:], m["pick"][:].rearrange("p t r e -> p t (r e)"), after=(picked,))
    turned = turn_parts(b, m["pickT"][0:2 * EXPERTS1, :], m["pick16"][:], 2 * EXPERTS1, 3, (both,))
    for r in range(2):
        pe.product(psum[:, 2 + r, :], b.core.half[f"pick{r}"], m["pickT"][:], start=True, stop=True, after=(turned,))
        low = dve.do(tt, m["low"][:, r, :], m["aT"][:], psum[:, 2 + r, :], ALU.mult, after=(pe.mark(), a_done))
    dve.do(tt, m["w"][:], picks[0], picks[1], ALU.add)
    dve.do(tt, m["w"][:], m["w"][:], m["e"][:], ALU.mult)
    dve.do(nc.vector.tensor_reduce, m["best"][:], m["w"][:], AX, ALU.add)
    readers = [a_done, low, low]
    for f in range(4):
        cols = slice(f * P, (f + 1) * P)
        bias = b.weight("bi")[:, f:f + 1]
        for r in range(2):
            bank = 1 + (2 * f + r) % 3
            pe.product(psum[:, bank, :], b.weight("wi")[:, cols], m["xT"][:], start=True, stop=False,
                       after=(low, readers[2 * f + r]))
            pe.product(psum[:, bank, :], b.weight("lb")[:, cols], m["low"][:, r, :], start=False, stop=True)
            done = pe.mark()
            if r == 0:
                readers.append(act.do(nc.scalar.activation, m["r0"][:, f % 2, :], psum[:, bank, :], ACT.Relu, bias=bias,
                                      scale=1.0, after=(done,)))
            else:
                readers.append(dve.do(nc.vector.tensor_scalar, m["hT"][:, f, :], psum[:, bank, :], bias, 0.0, ALU.add,
                                      ALU.max, after=(done,)))
        h_done = pool.do(nc.gpsimd.tensor_tensor, m["hT"][:, f, :], m["hT"][:, f, :], m["r0"][:, f % 2, :], ALU.add,
                         after=readers[-2:])
        if f == 1:
            act.wait(h_done)
    down = down_project(b, psum[:, 0, :], m["hT"], b.weight("wo"), (h_done,))
    y = m["xn"][:]
    dve.do(nc.vector.scalar_tensor_tensor, y, bcast(b.weight("bo"), 1, b.tiles), 2.0,
           psum[:, 0, :].rearrange("p (t d) -> p t d", t=b.tiles), ALU.mult, ALU.add, after=(down,))
    dve.do(tt, y, y, bcast(m["best"][:], 2, D), ALU.mult)
    dve.do(tt, x, x, y, ALU.add)


def room_L1f(nc, ctx, g):
    sb = lambda n, *shape, dt=F32: ctx.enter_context(nc.sbuf_tensor(f"{g.tag}L1f_{n}", list(shape), dt))
    return {"norm": norm_room(nc, ctx, g.tiles, g.tag + "L1f_norm"), "xn": sb("xn", P, g.tiles, D), "xT": sb("xT", P, g.tok), "aT": sb("aT", P, g.tok),
            "e": sb("e", P, g.tiles, 8), "v": sb("v", P, g.tiles, 8), "w": sb("w", P, g.tiles, 8), "best": sb("best", P, g.tiles),
            "pick": sb("pick", P, g.tiles, 2, 8), "pick16": sb("pick16", P, g.tiles, 16, dt=BF16),
            "pickT": sb("pickT", P, g.tok, dt=BF16), "low": sb("low", P, 2, g.tok),
            "r0": sb("r0", P, 2, g.tok), "hT": sb("hT", P, 4, g.tok)}


def once_L1f(b, m):
    b.nc.vector.memset(m["pickT"][:], 0.0)


def block_L2a(b, i, m):
    x = b.core.x[:, bass.ts(i, b.tiles), :]
    normed = layer_norm(b, m["x2"], x, LN_EPS, m["norm"])
    ready = to_features(b, m["xT"], m["x2"], 3, (normed,))
    done = linear_attention(b, m, m["xT"], ready, b.core.c["same8"], b.core.c["head8"], 16, 1e-6)
    turned = to_features(b, m["xT"], m["msg"], 2, (done,))
    project_out(b, x, m["xT"], b.weight("wo"), None, 3, (turned,))


def room_L2a(nc, ctx, g):
    sb = lambda n, *shape, dt=F32: ctx.enter_context(nc.sbuf_tensor(f"{g.tag}L2a_{n}", list(shape), dt))
    return {"norm": norm_room(nc, ctx, g.tiles, g.tag + "L2a_norm"), "x2": sb("x2", P, g.tiles, D), "xT": sb("xT", P, g.tok), **room_linear(sb, g, 16)}


def rms_norm(b, out, x, square, ss, eps, after=()):
    nc, dve = b.nc, b.dve
    squares = b.pool.do(nc.gpsimd.tensor_tensor, square, x, x, ALU.mult, after=(dve.now(), *after))
    dve.do(nc.vector.tensor_reduce, ss, square, AX, ALU.add, after=(squares,))
    scaled = inverse_root(b, ss, ss, 1.0 / x.shape[2], eps)
    return dve.do(nc.vector.tensor_tensor, out, x, bcast(ss, 2, x.shape[2]), ALU.mult, after=(scaled,))


def block_L2f(b, i, m):
    nc, psum, c = b.nc, b.psum, b.core.c
    dve, act, pe, pool = b.dve, b.act, b.pe, b.pool
    tt = nc.vector.tensor_tensor
    x = b.core.x[:, bass.ts(i, b.tiles), :]
    layer_norm(b, m["x0"], x, LN_EPS, m["norm"])
    normed = rms_norm(b, m["xn"][:], m["x0"][:], m["sq"][:], m["ss"][:], 1e-5)
    ready = to_features(b, m["xT"], m["xn"], 0, (normed,), b.weight("g1"), 0.0)
    pe.product(psum[0:16, 1, 0:b.tok], b.weight("wkl"), m["xT"][:], start=True, stop=True, after=(ready,))
    p_lat = pe.mark()
    latent = act.do(nc.scalar.copy, m["latT"][0:16, :], psum[0:16, 1, 0:b.tok], after=(p_lat,))
    latent2 = act.do(nc.scalar.copy, m["lat2"][0:16], bcast(psum[0:16, 1, 0:b.tok].rearrange("p (s k) -> p s k", k=S), 2, 2))
    pe.product(psum[:, 0, 0:b.tok], b.weight("wkr"), m["xT"][:], start=True, stop=True)
    pe.product(psum[:, 0, b.tok:2 * b.tok], b.weight("wkp"), m["xT"][:], start=True, stop=True)
    kr_ready = rotate(b, m["krT"][:], psum[:, 0, 0:b.tok], psum[:, 0, b.tok:2 * b.tok], c["cos32"], c["sin32"],
                      m["twin"][:, 0, :], (pe.mark(),))
    chunk = lambda bank, n: psum[:, bank + n // 2, (n % 2) * b.tok:(n % 2 + 1) * b.tok]
    for n in range(4):
        pe.product(chunk(2, n), b.weight("wkvb")[:, n * P:(n + 1) * P], m["latT"][:], start=True, stop=True,
                   after=(latent,))
    p_kv = pe.mark()
    for j in range(4):
        kr_kept = act.do(nc.scalar.activation, m["krx"][:, j, :], m["krT"][:], ACT.Copy, scale=c["quad"][:, j:j + 1],
                         after=(kr_ready,))
    for j in range(4):
        kv_kept = act.do(nc.scalar.activation, m["knx"][:, :, j, :],
                         psum[:, 2:4, :].rearrange("p a (n k) -> p (a n) k", n=2), ACT.Copy, scale=c["quad"][:, j:j + 1],
                         after=(p_kv,))
    freed = []
    for n in range(4):
        cols = slice(n * P, (n + 1) * P)
        base = 2 * (n % 2)
        free = freed[n - 2] if n >= 2 else (kr_ready, latent2) if n == 0 else (kv_kept,)
        pe.product(psum[:, base, 0:b.tok], b.weight("wqn")[:, cols], m["xT"][:], start=True, stop=True, after=free)
        pn = pe.mark()
        pe.product(psum[:, base + 1, 0:b.tok], b.weight("wqr")[:, cols], m["xT"][:], start=True, stop=True)
        pe.product(psum[:, base + 1, b.tok:2 * b.tok], b.weight("wqp")[:, cols], m["xT"][:], start=True, stop=True)
        pr = pe.mark()
        nope = act.do(nc.scalar.copy, m["qnT"][:, n, :], psum[:, base, 0:b.tok], after=(pn,))
        q_ready = rotate(b, m["qrT"][:, n, :], psum[:, base + 1, 0:b.tok], psum[:, base + 1, b.tok:2 * b.tok], c["cos32"],
                         c["sin32"], m["twin"][:, n % 2, :], (pr,))
        if n == 1:
            dve.wait(q_ready)
        freed.append((nope, q_ready))
    own = bcast(c["parity"], 2, 32)
    for s in range(b.seqs):
        free = (freed[2 + s // 2] if s % 2 == 0 else ())
        pe.product(psum[:, s, :], m["lat2"][:, s, :, :].rearrange("p a k -> p (a k)"), b.weight("wkvb"),
                   start=True, stop=True, after=(latent2, *free))
        read = dve.do(tt, m["va"][:, s, :, 0:32], psum[:, s, :].rearrange("p (h d) -> p h d", h=16), own, ALU.mult,
                      after=(pe.mark(),))
    for u in range(b.tiles):
        for n in range(4):
            for q_, k_, first in ((m["qnT"], m["knx"][:, n, :, :], True), (m["qrT"], m["krx"], False)):
                for r in range(2):
                    q = slice((2 * u + r) * S, (2 * u + r + 1) * S)
                    out = psum[64 * r:64 * r + 64, 2 * u + n // 2, (n % 2) * 4 * S:(n % 2 + 1) * 4 * S]
                    pe.product(out.rearrange("p (j k) -> p j k", j=4), q_[:, n, q], k_[:, :, q], start=first,
                               stop=not first, skip_group_check=True, after=(read, q_ready, nope, kr_kept, kv_kept))
    p = m["p"][:].rearrange("p (n k) -> p n k", k=S)
    p_s = pe.mark()
    dve.do(tt, p, psum[:, 0:4, :].rearrange("p a (n k) -> p (a n) k", k=S), bcast(c["causal"], 1, 32), ALU.add,
           after=(p_s,))
    dve.do(nc.vector.tensor_reduce, m["mx"][:], p, AX, ALU.max)
    low = dve.do(tt, p, p, bcast(m["mx"][:], 2, S), ALU.subtract)
    grown = act.do(nc.scalar.activation, p, p, ACT.Exp, scale=0.125, after=(low,))
    for n in range(16):
        pe.do(nc.tensor.transpose, psum[:, n // 4, (n % 4) * P:(n % 4 + 1) * P], m["p"][:, n * P:(n + 1) * P],
              c["ident"], after=(grown,))
        if n == 7:
            half = pe.mark()
    turned = pe.mark()
    pT = m["pT"].rearrange("p (a b) -> p a b", a=4)
    e0 = act.do(nc.scalar.copy, pT[:, 0:2, :], psum[:, 0:2, :], after=(half,))
    e1 = dve.do(nc.vector.tensor_copy, pT[:, 2:4, :], psum[:, 2:4, :], after=(turned,))
    for u in range(b.tiles):
        for k in range(8):
            for r in range(2):
                n = 8 * u + k
                pe.product(psum[64 * r:64 * r + 64, 2 * u + k // 4, (k % 4) * 66:(k % 4 + 1) * 66],
                           m["pT"][:, n * P + 64 * r:n * P + 64 * r + 64],
                           m["va"][:, 2 * u + r, 2 * k:2 * k + 2, :].rearrange("p h e -> p (h e)"),
                           start=True, stop=True, after=(e0, e1))
    out = psum[:, 0:4, 0:264].rearrange("p a (h e) -> p a h e", h=8)
    dve.do(nc.vector.reciprocal, m["z"][:], out[:, :, :, 32], after=(pe.mark(),))
    y = m["y"].rearrange("p t (a h d) -> p (t a) h d", a=2, h=8)
    y_done = dve.do(tt, y, out[:, :, :, 0:32], bcast(m["z"][:], 3, 32), ALU.mult)
    for n in range(4):
        y_ready = to_features(b, m["qnT"][:, n, :], m["y"][:, :, n * P:(n + 1) * P], n, (y_done,))
    down = down_project(b, psum[:, 0, :], m["qnT"], b.weight("wo"), (y_ready,))
    dve.do(tt, m["x0"][:], m["x0"][:], psum[:, 0, 0:b.tok].rearrange("p (t d) -> p t d", t=b.tiles), ALU.add, after=(down,))
    normed = rms_norm(b, m["xn"][:], m["x0"][:], m["sq"][:], m["ss"][:], 1e-5)
    ready = to_features(b, m["xT"], m["xn"], 1, (normed,), b.weight("g2"), 0.0)
    logits, pl = logits_of(b, m["xT"], b.weight("router"), EXPERTS2, 3, (ready,))
    softmax_rows(b, m["e"][:], logits, b.weight("rbias"), m["best"][:], (pl,))
    dve.do(nc.vector.tensor_copy, m["v"][:], m["e"][:])
    picks = [m["pick"][:, r, :, :] for r in range(2)]
    pick_largest(b, picks, m["v"][:], m["best"], m["w"][:], c["first"], 2)
    combined = weigh_picks(b, m, picks)
    comb_ready = turn_combine(b, m, m["comb"], EXPERTS2 + 1, 3, (combined,))
    done = experts(b, m, m["xT"], b.core.half["spread2"], (EXPERTS2 + 1) * HID2, (comb_ready,))
    dve.do(tt, x, x, m["x0"][:], ALU.add)
    dve.do(tt, x, x, psum[:, 0, 0:b.tok].rearrange("p (t d) -> p t d", t=b.tiles), ALU.add, after=(done,))


def weigh_picks(b, m, picks):
    nc, dve = b.nc, b.dve
    tt = nc.vector.tensor_tensor
    dve.do(tt, m["w"][:], picks[0], picks[1], ALU.add)
    dve.do(tt, m["w"][:], m["w"][:], m["e"][:], ALU.mult)
    dve.do(nc.vector.tensor_reduce, m["best"][:], m["w"][:], AX, ALU.add)
    dve.do(nc.vector.reciprocal, m["best"][:], m["best"][:])
    return dve.do(tt, m["comb"][:, :, 0:8], m["w"][:], bcast(m["best"][:], 2, 8), ALU.mult)


def room_routed(sb, g):
    return {"e": sb("e", P, g.tiles, 8), "v": sb("v", P, g.tiles, 8), "w": sb("w", P, g.tiles, 8), "best": sb("best", P, g.tiles),
            "pick": sb("pick", P, 2, g.tiles, 8), "comb": sb("comb", P, g.tiles, 9), "combT": sb("combT", P, g.tok, dt=BF16),
            "parts": sb("parts", P, g.tiles, 27, dt=BF16), "rest": sb("rest", P, g.tiles, 9),
            "h": sb("h", P, 2, g.tok)}


def room_L2f(nc, ctx, g):
    sb = lambda n, *shape, dt=F32: ctx.enter_context(nc.sbuf_tensor(f"{g.tag}L2f_{n}", list(shape), dt))
    m = {"norm": norm_room(nc, ctx, g.tiles, g.tag + "L2f_norm"), "x0": sb("x0", P, g.tiles, D), "xn": sb("xn", P, g.tiles, D),
         "sq": sb("sq", P, g.tiles, D), "ss": sb("ss", P, g.tiles), "xT": sb("xT", P, g.tok), "latT": sb("latT", P, g.tok),
         "lat2": sb("lat2", P, g.seqs, 2, S), "krT": sb("krT", P, g.tok), "krx": sb("krx", P, 4, g.tok),
         "twin": sb("twin", P, 2, g.tok), "knx": sb("knx", P, 4, 4, g.tok), "qnT": sb("qnT", P, 4, g.tok),
         "qrT": sb("qrT", P, 4, g.tok), "va": sb("va", P, g.seqs, 16, 33), "p": sb("p", P, 2048), "mx": sb("mx", P, 32),
         "z": sb("z", P, 4, 8), **room_routed(sb, g)}
    spent = m["knx"][:].rearrange("p n j k -> p (n j k)")
    m["pT"], m["y"] = spent[:, 0:2048], spent[:, 2048:2048 + 512 * g.tiles].rearrange("p (t f) -> p t f", t=g.tiles)
    return m


def once_L2f(b, m):
    nc, parity = b.nc, b.core.c["parity"]
    nc.vector.tensor_copy(m["va"][:, :, :, 32], bcast(parity, 1, b.seqs))
    nc.vector.memset(m["latT"][:], 0.0)
    nc.vector.memset(m["lat2"][:], 0.0)
    once_shared(b, m)


def once_shared(b, m):
    b.nc.vector.memset(m["comb"][:, :, 8:9], 1.0)
    once_combine(b, m)


def block_L3a(b, i, m):
    nc, psum, c = b.nc, b.psum, b.core.c
    dve, act, pe, pool = b.dve, b.act, b.pe, b.pool
    tt = nc.vector.tensor_tensor
    x = b.core.x[:, bass.ts(i, b.tiles), :]
    tiles = lambda ap: ap.rearrange("p (t d) -> p t d", t=b.tiles)
    layer_norm(b, m["x0"], x, LN_EPS, m["norm"])
    normed = layer_norm(b, m["xn"], m["x0"], LN_EPS, m["norm"])
    ready = to_features(b, m["xT"], m["xn"], 0, (normed,), b.weight("g1"), b.weight("be1"))
    pe.product(psum[0:16, 3, :], b.weight("gk1"), m["xT"][:], start=True, stop=True, after=(ready,))
    gk_done = act.do(nc.scalar.copy, m["gkT"][:], psum[0:16, 3, :], after=(pe.mark(),))
    for bank, w in ((1, "wv"), (2, "wg")):
        for t in range(b.tiles):
            pe.product(psum[:, bank, t * P:(t + 1) * P], m["xT"][:, t * P:(t + 1) * P], b.weight(w), start=True, stop=True)
    pvg = pe.mark()
    for t in range(b.tiles):
        pe.product(psum[:, 0, t * P:(t + 1) * P], m["gkT"][:, t * P:(t + 1) * P], b.weight("gk2"), start=True, stop=True,
                   after=(gk_done,))
    pz = pe.mark()
    v_done = act.do(nc.scalar.copy, m["v"][:], tiles(psum[:, 1, :]), after=(pvg,))
    g_done = act.do(nc.scalar.activation, m["g"][:], tiles(psum[:, 2, :]), ACT.Silu)
    pe.product(psum[:, 1, :], b.weight("wq"), m["xT"][:], start=True, stop=True, after=(v_done,))
    pe.product(psum[:, 2, :], b.weight("wk"), m["xT"][:], start=True, stop=True, after=(g_done,))
    pqk = pe.mark()
    dve.do(tt, m["lz"][:], tiles(psum[:, 0, :]), bcast(b.weight("bgk"), 1, b.tiles), ALU.add, after=(pz,))
    size = dve.do(nc.vector.scalar_tensor_tensor, m["la"][:], m["lz"][:], -1.0, m["lz"][:], ALU.mult, ALU.max)
    act.do(nc.scalar.activation, m["la"][:], m["la"][:], ACT.Exp, scale=-1.0, after=(size,))
    log = act.do(nc.scalar.activation, m["la"][:], m["la"][:], ACT.Ln, bias=1.0)
    decays = dve.do(nc.vector.scalar_tensor_tensor, m["lz"][:], m["lz"][:], 0.0, m["la"][:], ALU.min, ALU.subtract,
                    after=(log,))
    for t in range(b.tiles):
        pe.product(psum[:, 3, t * P:(t + 1) * P], m["lz"][:, t, :], c["decay"], start=True, stop=True, after=(decays,))
    pg = pe.mark()
    up = act.do(nc.scalar.activation, m["eq"][:], psum[:, 3, :], ACT.Exp, after=(pg,))
    down = act.do(nc.scalar.activation, m["ek"][:], psum[:, 3, :], ACT.Exp, scale=-1.0)
    dve.do(nc.vector.scalar_tensor_tensor, m["eq"][:], psum[:, 1, :], 32 ** -0.5, m["eq"][:], ALU.mult, ALU.mult,
           after=(up, pqk))
    decayed = dve.do(tt, m["ek"][:], m["ek"][:], psum[:, 2, :], ALU.mult, after=(down,))
    for s in range(b.seqs):
        t, r = s // 2, s % 2
        q = slice(s * S, (s + 1) * S)
        for h in range(4):
            f = slice(32 * h, 32 * h + 32)
            pe.product(psum[64 * r:64 * r + 64, h, t * S:(t + 1) * S], m["ek"][f, q], m["eq"][f, q], start=True,
                       stop=True, after=(decayed,))
    masked = dve.do(tt, m["a"][:], psum[:, 0:4, 0:b.tiles * S].rearrange("p h (t q) -> p h t q", q=S),
                    bcast(bcast(c["past"], 1, b.tiles), 1, 4), ALU.mult, after=(pe.mark(),))
    for s in range(b.seqs):
        t, r = s // 2, s % 2
        q = slice(64 * r, 64 * r + 64)
        for h in range(4):
            f = slice(32 * h, 32 * h + 32)
            pe.product(psum[q, r, t * P + 32 * h:t * P + 32 * h + 32], m["a"][q, h, t, :], m["v"][q, t, f], start=True,
                       stop=True, after=(masked, v_done, g_done))
    po = pe.mark()
    for r in range(2):
        q = slice(64 * r, 64 * r + 64)
        copied = act.do(nc.scalar.copy, m["o"][q, :, :], tiles(psum[q, r, :]), after=(po,))
    heads = lambda ap: ap.rearrange("p t (h d) -> p (t h) d", h=4)
    rms_norm(b, heads(m["o"][:]), heads(m["o"][:]), heads(m["xn"][:]), m["ss"][:], 1e-5, (copied,))
    gated = dve.do(tt, m["o"][:], m["o"][:], m["g"][:], ALU.mult)
    o_ready = to_features(b, m["xT"], m["o"], 2, (gated,), b.weight("rms"), 0.0)
    project_out(b, m["x0"][:], m["xT"], b.weight("wo"), None, 3, (o_ready,))
    normed = layer_norm(b, m["xn"], m["x0"], LN_EPS, m["norm"])
    ready = to_features(b, m["xT"], m["xn"], 0, (normed,), b.weight("g2"), b.weight("be2"))
    dve.do(tt, m["x0"][:], m["x0"][:], bcast(b.weight("b2"), 1, b.tiles), ALU.add)
    dve.do(tt, x, x, m["x0"][:], ALU.add)
    for f in range(3):
        pe.product(psum[:, 1 + f, :], b.weight("w1")[:, f * P:(f + 1) * P], m["xT"][:], start=True, stop=True,
                   after=(ready,))
        biased = act.do(nc.scalar.activation, m["hT"][:, f, :], psum[:, 1 + f, :], ACT.Identity,
                        bias=b.weight("b1")[:, f:f + 1], scale=1.0, after=(pe.mark(),))
        h = m["hT"][:, f, :]
        leaky = dve.do(nc.vector.scalar_tensor_tensor, h, h, 0.01, h, ALU.mult, ALU.max, after=(biased,))
        squared = pool.do(nc.gpsimd.tensor_tensor, h, h, h, ALU.mult, after=(leaky,))
    done = down_project(b, psum[:, 0, :], m["hT"], b.weight("w2"), (squared,))
    dve.do(tt, x, x, tiles(psum[:, 0, :]), ALU.add, after=(done,))


def room_L3a(nc, ctx, g):
    sb = lambda n, *shape, dt=F32: ctx.enter_context(nc.sbuf_tensor(f"{g.tag}L3a_{n}", list(shape), dt))
    tile = ("x0", "xn", "lz", "la", "v", "g", "o")
    return {"norm": norm_room(nc, ctx, g.tiles, g.tag + "L3a_norm"), **{n: sb(n, P, g.tiles, D) for n in tile}, "xT": sb("xT", P, g.tok),
            "gkT": sb("gkT", 16, g.tok), "eq": sb("eq", P, g.tok), "ek": sb("ek", P, g.tok), "a": sb("a", P, 4, g.tiles, S),
            "ss": sb("ss", P, 4 * g.tiles), "hT": sb("hT", P, 3, g.tok)}


def block_L3f(b, i, m):
    nc, psum, c = b.nc, b.psum, b.core.c
    dve = b.dve
    tt = nc.vector.tensor_tensor
    x = b.core.x[:, bass.ts(i, b.tiles), :]
    normed = layer_norm(b, m["xn"], x, LN_EPS, m["norm"])
    ready = to_features(b, m["xT"], m["xn"], 0, (normed,))
    logits, pl = logits_of(b, m["xT"], b.weight("router"), EXPERTS3, 3, (ready,))
    dve.do(nc.vector.tensor_reduce, m["best"][:], logits, AX, ALU.max, after=(pl,))
    dve.do(nc.vector.tensor_copy, m["v"][:], logits)
    low = dve.do(tt, m["e"][:], logits, bcast(m["best"][:], 2, EXPERTS3), ALU.subtract)
    grown = b.act.do(nc.scalar.activation, m["e"][:], m["e"][:], ACT.Exp, after=(low,))
    picks = [m["pick"][:, r, :, :] for r in range(2)]
    pick_largest(b, picks, m["v"][:], m["best"], m["w"][:], c["first"], 2)
    dve.wait(grown)
    combined = weigh_picks(b, m, picks)
    comb_ready = turn_combine(b, m, m["comb"], EXPERTS3 + 1, 3, (combined,))
    done = experts(b, m, m["xT"], b.core.half["spread3"], (EXPERTS3 + 1) * HID3, (comb_ready,))
    dve.do(tt, x, x, psum[:, 0, :].rearrange("p (t d) -> p t d", t=b.tiles), ALU.add, after=(done,))


def room_L3f(nc, ctx, g):
    sb = lambda n, *shape, dt=F32: ctx.enter_context(nc.sbuf_tensor(f"{g.tag}L3f_{n}", list(shape), dt))
    return {"norm": norm_room(nc, ctx, g.tiles, g.tag + "L3f_norm"), "xn": sb("xn", P, g.tiles, D), "xT": sb("xT", P, g.tok), **room_routed(sb, g)}


TILES = {"L1x": 2, "L2f": 2}
ROOMS = {"L0x": room_L0x, "L0a": room_L0a, "L0f": room_L0f, "L1x": room_L1x, "L1a": room_L1a, "L1f": room_L1f,
         "L2x": room_L2x, "L2a": room_L2a, "L2f": room_L2f, "L3x": room_L3x, "L3a": room_L3a, "L3f": room_L3f}
BODIES = {"L0x": block_L0x, "L0a": block_L0a, "L0f": block_L0f, "L1x": block_L1x, "L1a": block_L1a, "L1f": block_L1f,
          "L2x": block_L2x, "L2a": block_L2a, "L2f": block_L2f, "L3x": block_L3x, "L3a": block_L3a, "L3f": block_L3f}
ONCE = {"L0x": once_L0x, "L0a": once_ones, "L0f": once_combine, "L1x": once_L1x, "L1a": once_L1a, "L1f": once_L1f,
        "L2x": once_value_ones, "L2a": once_ones, "L2f": once_L2f, "L3x": once_value_ones, "L3f": once_shared}



def build(nc, n_seq, weights, constants, halves, x, ctxT, ctx_tok, mask, out, plan, blocks):
    table = weight_table()
    places, _ = weight_places(table)
    core = Core()
    core.nc, core.places = nc, places
    ctx = ExitStack()
    sb = lambda n, *shape: ctx.enter_context(nc.sbuf_tensor(n, list(shape), F32))
    core.x = sb("x_held", P, n_seq // 2, D)
    core.ctxT, core.ctx_tok = ctxT, ctx_tok
    core.mask = mask.rearrange("(t r) k -> r t k", r=2)
    core.psum = ctx.enter_context(nc.psum_tensor("psum", [P, 8, BANK], F32))
    const_tile = sb("constants_held", P, constants.shape[1])
    core.c, at = {}, 0
    for name, value in constant_table().items():
        core.c[name] = const_tile[0:value.shape[0], at:at + value.shape[1]]
        at += value.shape[1]
    half_tile = sb("halves_held", P, halves.shape[1])
    core.half, at = {}, 0
    for name, value in half_table().items():
        core.half[name] = half_tile[:].bitcast(BF16)[:, at:at + value.shape[1]]
        at += value.shape[1]
    widest = [max(places[n][1] for n in blocks[k::2]) if blocks[k::2] else 1 for k in range(2)]
    weight_rooms = [sb(f"weights{k}", P, widest[k]) for k in range(2)]
    core.weight_room = {n: weight_rooms[k % 2] for k, n in enumerate(blocks)}
    core.idle = {k: nc.alloc_semaphore(f"idle_{k}") for k in ("pe", "dve", "act", "pool", "load0", "load1")}
    loaded = nc.alloc_semaphore("loaded")
    n_loaded = 0

    def load(dst, src):
        nc.sync.dma_start(dst, src).then_inc(loaded, 16)

    def load_weights(name):
        first, n, _ = places[name]
        load(core.weight_room[name][:, 0:n], weights[:, first:first + n])

    load_weights(blocks[0])
    load(const_tile[:], constants)
    x_tiles = "(n p) d -> p n d"
    load(core.x[:], x.rearrange(x_tiles, p=P))
    load(half_tile[:], halves)
    n_loaded = 4
    for k, name in enumerate(blocks):
        with ExitStack() as own:
            b = Block(core, name, plan)
            tiles = TILES.get(name, 4)
            contexts = [Context(b, k, tiles) for k in range(CONTEXTS)]
            rooms = [ROOMS[name](nc, own, g) for g in contexts]
            for engine in (nc.tensor, nc.vector, nc.scalar, nc.gpsimd):
                engine.wait_ge(loaded, 16 * n_loaded)
            if name in ONCE:
                for g, m in zip(contexts, rooms):
                    ONCE[name](g, m)
            nc.all_engine_barrier()
            if k + 1 < len(blocks):
                load_weights(blocks[k + 1])
                n_loaded += 1
            with nc.Fori(0, n_seq // (CONTEXTS * 2 * tiles)) as i:
                b.iteration(i, BODIES[name], contexts, rooms)
            nc.all_engine_barrier()
    stored = nc.alloc_semaphore("stored")
    nc.sync.dma_start(out.rearrange(x_tiles, p=P), core.x[:]).then_inc(stored, 16)
    nc.sync.wait_ge(stored, 16)
    ctx.close()


BLOCKS = ["L0x", "L0a", "L0f", "L1x", "L1a", "L1f", "L2x", "L2a", "L2f", "L3x", "L3a", "L3f"]


def program(nc, n_seq, n_weights, n_constants, n_halves, plan, blocks=BLOCKS):
    dram = lambda n, shape, dt=F32, kind="ExternalInput": nc.dram_tensor(n, shape, dt, kind=kind).ap()
    build(nc, n_seq, dram("weights", (P, n_weights)), dram("constants", (P, n_constants)), dram("halves", (P, n_halves)), dram("x", (n_seq * S, D)),
          dram("ctxT", (CX, n_seq * SC)), dram("ctx", (P, n_seq, CX)), dram("mask", (n_seq, SC // 4), I32),
          dram("out", (n_seq * S, D), kind="ExternalOutput"), plan, blocks)


def kernel(**inputs):
    import concourse.bacc as bacc
    from concourse.bass_utils import run_bass_kernel_spmd
    a = {k: np.asarray(v) for k, v in inputs.items()}
    x, context, mask = a["x"], a["ctx_768"], a["mask_BxS2_bk0"]
    n_seq = x.shape[0]
    packed = []
    for entries in weight_table().values():
        for name, rows, cols, layout in entries:
            w = layout(a)
            assert w.shape == (rows, cols), (name, w.shape)
            packed.append(pad_rows(w, P))
    weights = np.ascontiguousarray(np.concatenate(packed, 1))
    constants = np.ascontiguousarray(np.concatenate([pad_rows(v, P) for v in constant_table().values()], 1))
    halves = half_words(half_table())
    arrays = {
        "weights": weights, "constants": constants, "halves": halves, "x": np.ascontiguousarray(x.reshape(-1, D)),
        "ctxT": np.ascontiguousarray(context.transpose(2, 0, 1).reshape(CX, -1)),
        "ctx": np.ascontiguousarray(context.transpose(1, 0, 2)), "mask": np.ascontiguousarray(mask).view(np.int32)}
    plan = {}
    for _ in range(2):
        nc = bacc.Bacc("TRN2", target_bir_lowering=False, num_devices=1)
        program(nc, n_seq, weights.shape[1], constants.shape[1], halves.shape[1], plan)
    r = run_bass_kernel_spmd(nc, [arrays], core_ids=[0])
    return r.results[0]["out"].reshape(x.shape)
```

```python
from contextlib import ExitStack

import numpy as np
import concourse.bass as bass
from concourse import mybir

F32 = mybir.dt.float32
BF16 = mybir.dt.bfloat16
U8 = mybir.dt.uint8
I32 = mybir.dt.int32
ALU = mybir.AluOpType
ACT = mybir.ActivationFunctionType
AX = mybir.AxisListType.X

P = 128
S = 64
D = 128
CX = 96
SC = 128
BANK = 512
CONTEXTS = 2
CONTEXT_BANKS = 4
NEG = -1.0e30
LN_EPS = 1e-5



def chunks(w, rows=P):
    k = w.shape[0] // rows
    return w.reshape(k, rows, w.shape[1]).transpose(1, 0, 2).reshape(rows, k * w.shape[1])


def col(v):
    return v.reshape(-1, P).T if v.size >= P else v.reshape(-1, 1)


def row(v):
    return np.broadcast_to(v.reshape(1, -1), (P, v.size))


def rope_partner(n_heads, width):
    f = np.arange(n_heads * width)
    return f - f % width + (f % width + width // 2) % width


EXPERTS0, HID0 = 16, 64
EXPERTS1, RANK1, FF1 = 8, 16, 512
EXPERTS2, HID2 = 8, 64
EXPERTS3, HID3 = 8, 192


def pad_rows(w, rows):
    return np.concatenate([w, np.zeros((rows - w.shape[0], w.shape[1]), w.dtype)], 0)


def spaced(v):
    z = np.zeros_like(v)
    return np.stack([np.concatenate([v, z]), np.concatenate([z, v])], 1)


def placed(v, column):
    out = np.zeros((P, 4), v.dtype)
    out[np.arange(P), column] = v
    return out


def by_quad(v):
    return placed(v, np.arange(P) // 32)


def by_lane(v):
    return placed(v, np.arange(P) % 32 // 8)


def weight_table():
    t = {}
    t["L0x"] = [
        ("wv", P, 64, lambda a: a["L0_xattn_Wv"].T), ("wt", CX, 64, lambda a: a["L0_xattn_Wt"].T),
        ("bv", 64, 1, lambda a: col(a["L0_xattn_bv"])), ("bt", 64, 1, lambda a: col(a["L0_xattn_bt"]))]
    t["L0a"] = [
        ("wq", P, P, lambda a: a["L0_attn_wq"].T),
        ("wk", P, P, lambda a: a["L0_attn_wk"].T), ("wv", P, P, lambda a: a["L0_attn_wv"].T),
        ("w1", P, 512, lambda a: a["L0_attn_w1"].T), ("w2", P, 512, lambda a: chunks(a["L0_attn_w2"].T)),
        ("b1", P, 4, lambda a: col(a["L0_attn_b1"])), ("b2", P, P, lambda a: row(a["L0_attn_b2"])),
        ("g1", P, 1, lambda a: col(a["L0_attn_g1"])), ("be1", P, 1, lambda a: col(a["L0_attn_be1"])),
        ("g2", P, 1, lambda a: col(a["L0_attn_g2"])), ("be2", P, 1, lambda a: col(a["L0_attn_be2"]))]
    t["L0f"] = [
        ("router", P, 16, lambda a: a["L0_ffn_router_weight"].T),
        ("rbias", P, 16, lambda a: row(a["L0_ffn_router_bias"])),
        ("gate", P, 1024, lambda a: a["L0_ffn_w_gate"].reshape(-1, D).T),
        ("up", P, 1024, lambda a: a["L0_ffn_w_up"].reshape(-1, D).T),
        ("down", P, 1024, lambda a: chunks(a["L0_ffn_w_down"].transpose(0, 2, 1).reshape(-1, D)))]
    t["L1x"] = [
        ("wql", P, 384, lambda a: np.concatenate([a["L1_xattn_Wq"].T, a["L1_xattn_Wlkv"].T], 1)),
        ("wkv", CX, 256, lambda a: a["L1_xattn_Wkv"].T), ("wo", P, P, lambda a: a["L1_xattn_Wo"].T),
        ("bo", P, P, lambda a: row(a["L1_xattn_bo"])),
        ("xg", CX, 1, lambda a: col(a["L1_xattn_ln_x_g"])), ("xb", CX, 1, lambda a: col(a["L1_xattn_ln_x_b"])),
        ("lg", P, 1, lambda a: col(a["L1_xattn_ln_l_g"])), ("lb", P, 1, lambda a: col(a["L1_xattn_ln_l_b"])),
        ("qg", P, 2, lambda a: spaced(a["L1_xattn_qn_g"])),
        ("kg", P, 1, lambda a: col(np.tile(a["L1_xattn_kn_g"], 2)))]
    perm8 = rope_partner(16, 8)
    t["L1a"] = [
        ("wq", P, P, lambda a: a["L1_attn_w_qkv"][:D].T), ("wqp", P, P, lambda a: a["L1_attn_w_qkv"][:D][perm8].T),
        ("wk", P, P, lambda a: a["L1_attn_w_qkv"][D:2 * D].T),
        ("wkp", P, P, lambda a: a["L1_attn_w_qkv"][D:2 * D][perm8].T),
        ("wv", P, P, lambda a: a["L1_attn_w_qkv"][2 * D:].T), ("wo", P, P, lambda a: a["L1_attn_w_out"].T),
        ("bo", P, P, lambda a: row(a["L1_attn_b_out"]))]
    t["L1f"] = [
        ("gate", P, 8, lambda a: a["L1_ffn_gate_w"].T), ("gb", P, 8, lambda a: row(a["L1_ffn_gate_b"])),
        ("wi", P, 512, lambda a: a["L1_ffn_wi"].T), ("bi", P, 4, lambda a: col(a["L1_ffn_bi"])),
        ("wo", P, 512, lambda a: chunks(a["L1_ffn_wo"].T)), ("bo", P, P, lambda a: row(a["L1_ffn_bo"])),
        ("la", P, P, lambda a: a["L1_ffn_lora_A"].reshape(-1, D).T),
        ("lb", P, 512, lambda a: a["L1_ffn_lora_B"].transpose(0, 2, 1).reshape(P, 512))]
    t["L2x"] = [
        ("wq", P, P, lambda a: a["L2_xattn_Wq"]), ("wk", CX, P, lambda a: a["L2_xattn_Wk"]),
        ("wv", CX, P, lambda a: a["L2_xattn_Wv"]), ("wo", P, P, lambda a: a["L2_xattn_Wo"]),
        ("bq", P, 4, lambda a: by_quad(a["L2_xattn_bq"])), ("bk", P, 4, lambda a: by_lane(a["L2_xattn_bk"])),
        ("bv", P, P, lambda a: row(a["L2_xattn_bv"])), ("bo", P, P, lambda a: row(a["L2_xattn_bo"]))]
    t["L2a"] = [
        ("wq", P, P, lambda a: a["L2_attn_Wq"]), ("wk", P, P, lambda a: a["L2_attn_Wk"]),
        ("wv", P, P, lambda a: a["L2_attn_Wv"]), ("wo", P, P, lambda a: a["L2_attn_Wo"])]
    pair = np.arange(32) ^ 1
    t["L2f"] = [
        ("g1", P, 1, lambda a: col(a["L2_ffn_w_ln1"])), ("g2", P, 1, lambda a: col(a["L2_ffn_w_ln2"])),
        ("wqn", P, 512, lambda a: a["L2_ffn_Wq"].reshape(D, 16, 64)[:, :, :32].reshape(D, 512)),
        ("wqr", P, 512, lambda a: a["L2_ffn_Wq"].reshape(D, 16, 64)[:, :, 32:].reshape(D, 512)),
        ("wqp", P, 512, lambda a: a["L2_ffn_Wq"].reshape(D, 16, 64)[:, :, 32:][:, :, pair].reshape(D, 512)),
        ("wkl", P, 16, lambda a: a["L2_ffn_Wkva"][:, :16]),
        ("wkr", P, P, lambda a: np.tile(a["L2_ffn_Wkva"][:, 16:], (1, 4))),
        ("wkp", P, P, lambda a: np.tile(a["L2_ffn_Wkva"][:, 16:][:, pair], (1, 4))),
        ("wkvb", P, 512, lambda a: pad_rows(a["L2_ffn_Wkvb"], P)),
        ("wo", P, 512, lambda a: chunks(a["L2_ffn_Wo"].reshape(16, 64, D)[:, :32].reshape(512, D))),
        ("router", P, 8, lambda a: a["L2_ffn_Wgate"]), ("rbias", P, 8, lambda a: row(a["L2_ffn_expert_bias"])),
        ("gate", P, 576, lambda a: np.concatenate([a["L2_ffn_Wg"], a["L2_ffn_sWg"]]).transpose(1, 0, 2).reshape(D, 576)),
        ("up", P, 576, lambda a: np.concatenate([a["L2_ffn_Wu"], a["L2_ffn_sWu"]]).transpose(1, 0, 2).reshape(D, 576)),
        ("down", P, 640, lambda a: chunks(pad_rows(np.concatenate([a["L2_ffn_Wd"], a["L2_ffn_sWd"]]).reshape(576, D), 640)))]
    t["L3x"] = [
        ("wq", P, P, lambda a: a["L3_xattn_Wq"]), ("wk", CX, P, lambda a: a["L3_xattn_Wk"]),
        ("wv", CX, P, lambda a: a["L3_xattn_Wv"]), ("bq", P, 4, lambda a: by_quad(a["L3_xattn_bq"])),
        ("bk", P, 4, lambda a: by_lane(a["L3_xattn_bk"])), ("bv", P, P, lambda a: row(a["L3_xattn_bv"])),
        ("w1", P, 256, lambda a: a["L3_xattn_W1"]), ("b1", P, 2, lambda a: col(a["L3_xattn_b1"])),
        ("w2", P, 256, lambda a: chunks(a["L3_xattn_W2"])), ("b2", P, P, lambda a: row(a["L3_xattn_b2"]))]
    t["L3a"] = [
        ("g1", P, 1, lambda a: col(a["L3_attn_ln1_w"])), ("be1", P, 1, lambda a: col(a["L3_attn_ln1_b"])),
        ("g2", P, 1, lambda a: col(a["L3_attn_ln2_w"])), ("be2", P, 1, lambda a: col(a["L3_attn_ln2_b"])),
        ("rms", P, 1, lambda a: col(np.tile(a["L3_attn_rms_w"], 4))),
        ("wq", P, P, lambda a: a["L3_attn_Wq"]), ("wk", P, P, lambda a: a["L3_attn_Wk"]),
        ("wv", P, P, lambda a: a["L3_attn_Wv"]), ("wg", P, P, lambda a: a["L3_attn_Wg"]),
        ("gk1", P, 16, lambda a: a["L3_attn_Wgk1"]), ("gk2", 16, P, lambda a: a["L3_attn_Wgk2"]),
        ("bgk", P, P, lambda a: row(a["L3_attn_bgk2"])), ("wo", P, P, lambda a: a["L3_attn_Wo"]),
        ("w1", P, 384, lambda a: a["L3_attn_W1"]), ("b1", P, 3, lambda a: col(a["L3_attn_b1"])),
        ("w2", P, 384, lambda a: chunks(a["L3_attn_W2"])), ("b2", P, P, lambda a: row(a["L3_attn_b2"]))]
    half = HID3
    t["L3f"] = [
        ("router", P, 8, lambda a: a["L3_ffn_gate_w"].T),
        ("gate", P, 1728, lambda a: np.concatenate([a["L3_ffn_w_up"][:, :half].reshape(-1, D), a["L3_ffn_sg_gate"]]).T),
        ("up", P, 1728, lambda a: np.concatenate([a["L3_ffn_w_up"][:, half:].reshape(-1, D), a["L3_ffn_sg_up"]]).T),
        ("down", P, 1792, lambda a: chunks(pad_rows(np.concatenate(
            [a["L3_ffn_w_down"].transpose(0, 2, 1).reshape(-1, D), a["L3_ffn_sg_down"].T]), 1792)))]
    return t


def weight_places(table):
    places, at = {}, 0
    for block, entries in table.items():
        inside, n = {}, 0
        for name, rows, cols, _ in entries:
            inside[name] = (n, rows, cols)
            n += cols
        places[block] = (at, n, inside)
        at += n
    return places, at


def expert_spread(hidden, experts, total):
    e = np.minimum(np.arange(total) // hidden, experts)
    return (np.arange(experts + 1)[:, None] == e[None, :]).astype(np.float32)


def constant_table():
    p = np.arange(P)
    c = {"ident": np.eye(P), "ones": np.ones((P, P)), "halves": np.full((P, 32), -0.5)}
    c["same16"] = p[:, None] // 16 == p[None, :] // 16
    c["head16"] = p[:, None] // 16 == np.arange(8)[None, :]
    c["same8"] = p[:, None] // 8 == p[None, :] // 8
    c["head8"] = p[:, None] // 8 == np.arange(16)[None, :]
    c["lane4"] = (p[:, None] % 32) // 8 == np.arange(4)[None, :]
    c["quad"] = p[:, None] // 32 == np.arange(4)[None, :]
    c["parity"] = p[:, None] // 64 == np.arange(16)[None, :] % 2
    c["first"] = np.broadcast_to(16.0 - np.arange(16), (P, 16))
    pos = np.arange(S, dtype=np.float32)
    inv = (1.0 / np.float32(10000.0) ** (np.arange(0, 8, 2, dtype=np.float32) / np.float32(8))).astype(np.float32)
    ang = (pos[None, :] * inv[p % 4][:, None]).astype(np.float32)
    c["cos8"] = np.cos(ang)
    c["sin8"] = np.sin(ang) * np.where(p % 8 < 4, -1.0, 1.0)[:, None]
    inv = (1.0 / np.float32(100000.0) ** (np.arange(0, 32, 2, dtype=np.float32) / np.float32(32))).astype(np.float32)
    ang = (pos[None, :] * inv[(p % 32) // 2][:, None]).astype(np.float32)
    c["cos32"] = np.cos(ang)
    c["sin32"] = np.sin(ang) * np.where(p % 2 == 0, -1.0, 1.0)[:, None]
    c["causal"] = np.where(np.arange(S)[None, :] <= (p % S)[:, None], 0.0, NEG)
    same = p[:, None] // S == p[None, :] // S
    upto = (p[:, None] <= p[None, :]).astype(np.float64)
    c["decay"] = same * (upto - (p % S < S // 2)[:, None]) / 16.0
    c["past"] = (p % S)[:, None] <= np.arange(S)[None, :]
    return {k: np.asarray(v, np.float32) for k, v in c.items()}


def half_table():
    t = {"ident": np.eye(P)}
    for name, spread in (("spread0", expert_spread(HID0, EXPERTS0, EXPERTS0 * HID0)[:EXPERTS0]),
                         ("spread2", expert_spread(HID2, EXPERTS2, 5 * P)), ("spread3", expert_spread(HID3, EXPERTS3, 14 * P))):
        t[name] = pad_rows(np.tile(spread, (3, 1)), P)
    spread = expert_spread(RANK1, EXPERTS1, P)[:EXPERTS1]
    t["pick0"] = pad_rows(spread, P)
    t["pick1"] = pad_rows(np.concatenate([0 * spread, spread]), P)
    return t


def half_words(table):
    one = np.uint16(0x3F80)
    return np.ascontiguousarray(np.concatenate(list(table.values()), 1).astype(np.uint16) * one).view(np.float32)



class Step:

    def __init__(self, queue, instruction=None, args=(), kwargs=None, after=(), alone=False):
        self.queue, self.instruction, self.args, self.kwargs = queue, instruction, args, kwargs
        self.after, self.alone = after, alone
        self.counted = False
        self.number = None


class Queue:

    def __init__(self, context, lane):
        self.context, self.lane, self.last, self.pending = context, lane, None, ()
        self.key = lane.key

    def wait(self, token):
        self.pending += (token,)

    def product(self, out, stationary, moving, after=(), **kwargs):
        small = stationary.shape[0] <= 64 and int(np.prod(stationary.shape[1:])) <= 64
        return self.do(self.lane.engine.matmul, out, stationary, moving, after=after, alone=small, **kwargs)

    def do(self, instruction, *args, after=(), alone=False, **kwargs):
        after = (*self.pending, *after)
        if self.last is None:
            after = (*(t for t in self.context.before.values() if t.queue is not self or self.lane.chained), *after)
        elif self.lane.chained:
            after = (*after, self.last)
        self.pending = ()
        self.last = Step(self, instruction, args, kwargs, after, alone)
        self.context.steps.append(self.last)
        return self.mark() if self.lane.chained else None

    def mark(self):
        self.last.counted = True
        return self.last

    def now(self):
        return self.last


class Lane:

    def __init__(self, nc, engine, key, name, per_round, chained, idle, step=1):
        self.key, self.engine, self.name, self.per_round, self.chained, self.step = key, engine, name, per_round, chained, step
        self.sem = nc.alloc_semaphore(name)
        self.idle = idle
        self.count, self.reached = 0, {}

    def emit(self, step, i):
        waits = 0
        latest = {}
        for token in step.after:
            if token.number is None:
                continue
            if token.queue.lane not in latest or latest[token.queue.lane].number < token.number:
                latest[token.queue.lane] = token
        for lane, token in latest.items():
            if self.reached.get(lane.name, -lane.per_round) < token.number:
                self.reached[lane.name] = token.number
                self.engine.wait_ge(lane.sem, i * (lane.per_round * lane.step) + (lane.per_round + token.number) * lane.step)
                waits += 1
                if self.step > 1:
                    self.engine.sem_inc(self.idle, 1)
        if step.alone and waits:
            self.engine.sem_inc(self.idle, 1)
        placed = step.instruction(*step.args, **step.kwargs)
        if step.counted:
            placed.then_inc(self.sem, self.step)


class Context:

    def __init__(self, block, number, tiles):
        self.block, self.nc, self.core, self.number = block, block.nc, block.core, number
        self.tiles, self.seqs, self.tok, self.ctok = tiles, 2 * tiles, tiles * P, 2 * tiles * SC
        self.tag = f"c{number}_"
        self.psum = block.core.psum[:, CONTEXT_BANKS * number:CONTEXT_BANKS * (number + 1), :]

    def weight(self, name):
        return self.block.weight(name)

    def record(self, body, group, room):
        self.steps = []
        self.queues = {key: Queue(self, lane) for key, lane in self.block.lanes.items()
                       if not key.startswith("load") or key == f"load{self.number}"}
        self.pe, self.dve, self.act, self.pool = (self.queues[k] for k in ("pe", "dve", "act", "pool"))
        self.load = self.queues[f"load{self.number}"]
        self.before = {key: Step(queue) for key, queue in self.queues.items()}
        body(self, group, room)
        turns = []
        for step in self.steps:
            if turns and step.queue is self.pe and turns[-1][-1].queue is self.pe and not turns[-1][-1].counted:
                turns[-1].append(step)
            else:
                turns.append([step])
        return Recording(self.steps, turns, self.before)


class Recording:

    def __init__(self, steps, turns, before):
        self.steps, self.turns, self.before = steps, turns, before

    def last(self, key):
        numbers = [s.number for s in self.steps if s.queue is self.before[key].queue and s.counted]
        return numbers[-1] if numbers else None

    def follow(self, lasts):
        for key, token in self.before.items():
            token.number = lasts[key]


def estimate(step):
    out, source = step.args[0], step.args[1]
    if step.queue.key == "pe":
        columns = max(int(np.prod(out.shape[1:])), 64)
        return columns * (1.7 if source.dtype == F32 else 0.42) * (0.5 if out.shape[0] <= 64 else 1.0) + 10
    columns = max(int(np.prod(out.shape[1:])), int(np.prod(source.shape[1:])))
    fixed, each = {"dve": (60, 1.05), "act": (200, 0.9), "pool": (200, 2.2)}.get(step.queue.key, (3000, 0.0))
    return fixed + each * columns


def merge(streams):
    free, done, order, at = {}, {}, [], [0] * len(streams)
    ready = lambda step: max([done[t] + 150 for t in step.after if t in done], default=0)
    while any(k < len(s) for k, s in zip(at, streams)):
        starts = [(max([free.get(s[k][0].queue.lane, 0)] + [ready(step) for step in s[k]]), n)
                  for n, (k, s) in enumerate(zip(at, streams)) if k < len(s)]
        time, n = min(starts)
        for step in streams[n][at[n]]:
            time = max(time, ready(step)) + estimate(step)
            done[step] = time
        free[step.queue.lane] = time
        order += streams[n][at[n]]
        at[n] += 1
    return order


def split_turn(turns, share):
    times, done, free = [], {}, {}
    for turn in turns:
        time = free.get(turn[0].queue.lane, 0)
        for step in turn:
            time = max([time] + [done[t] + 150 for t in step.after if t in done]) + estimate(step)
            done[step] = time
        free[turn[0].queue.lane] = time
        times.append(time)
    return next(k for k, time in enumerate(times) if time >= share * max(times))


class Block:

    def __init__(self, core, name, plan):
        self.core, self.nc, self.name, self.plan = core, core.nc, name, plan
        nc = core.nc
        self.lanes = {}
        for key, engine, chained, step in (("pe", nc.tensor, False, 1), ("dve", nc.vector, True, 1),
                                           ("act", nc.scalar, True, 1), ("pool", nc.gpsimd, True, 1),
                                           ("load0", nc.sync, True, 16), ("load1", nc.sync, True, 16)):
            self.lanes[key] = Lane(nc, engine, key, f"{name}_{key}", plan.get((name, key), 1), chained,
                                   core.idle[key], step)

    def weight(self, name):
        at, rows, cols = self.core.places[self.name][2][name]
        return self.core.weight_room[self.name][0:rows, at:at + cols]

    def number(self, order):
        counts = {lane: 0 for lane in self.lanes.values()}
        for step in order:
            if step.counted:
                counts[step.queue.lane] += 1
                step.number = counts[step.queue.lane]
        return counts

    def emit(self, order, i):
        for lane in self.lanes.values():
            lane.reached = {}
        for step in order:
            step.queue.lane.emit(step, i)

    def run(self, body, contexts, rooms, rounds, share):
        first, second = contexts
        group = lambda i, context: i * CONTEXTS + context.number
        ahead = first.record(body, group(0, first), rooms[0])
        cut = split_turn(ahead.turns, share)
        order = [step for turn in ahead.turns[:cut] for step in turn]
        counts = self.number(order)
        ahead.follow({key: None for key in ahead.before})
        self.emit(order, -1)
        for lane in self.lanes.values():
            if lane.step > 1 and counts[lane]:
                lane.engine.wait_ge(lane.sem, counts[lane] * lane.step)
        self.nc.all_engine_barrier()
        for lane in self.lanes.values():
            if lane.per_round > counts[lane]:
                lane.engine.sem_inc(lane.sem, (lane.per_round - counts[lane]) * lane.step)
        with self.nc.Fori(0, rounds - 1) as i:
            now = first.record(body, group(i, first), rooms[0])
            nxt = first.record(body, group(i + 1, first), rooms[0])
            other = second.record(body, group(i, second), rooms[1])
            order = merge([now.turns[cut:] + nxt.turns[:cut], other.turns])
            counts = self.number(order)
            for lane, count in counts.items():
                self.plan[(self.name, lane.key)] = count
            back = lambda number, key: None if number is None else number - counts[self.lanes[key]]
            head = [back(b.number, b.queue.key) for b in nxt.steps]
            for a, number in zip(now.steps, head):
                if a.number is None:
                    a.number = number
            lasts = {key: now.last(key) for key in now.before}
            nxt.follow(lasts)
            before = [{key: back(r.last(key), key) for key in r.before} for r in (now, other)]
            now.follow(before[0])
            other.follow(before[1])
            self.emit(order, i)
        i = rounds - 1
        now = first.record(body, group(i, first), rooms[0])
        other = second.record(body, group(i, second), rooms[1])
        order = merge([now.turns[cut:], other.turns])
        self.number(order)
        for a, number in zip(now.steps, head):
            if a.number is None:
                a.number = number
        now.follow(before[0])
        other.follow(before[1])
        self.emit(order, i)


class Core:
    pass


def bcast(ap, axis, n):
    return ap.unsqueeze(axis).to_broadcast([*ap.shape[:axis], n, *ap.shape[axis:]])


def layer_norm(b, out, x, eps, scratch, after=()):
    stats, moments, rstd = scratch
    n = x.shape[1]
    for t in range(n):
        b.dve.do(b.nc.vector.bn_stats, stats[:, t, :], x[:, t, :], after=after)
    for t in range(n):
        b.dve.do(b.nc.vector.bn_aggr, moments[:, t, :], stats[:, t, :], alone=True)
    scaled = inverse_root(b, rstd[:, 0:n], moments[:, 0:n, 1], 1.0, eps)
    for t in range(n):
        token = b.dve.do(b.nc.vector.tensor_scalar, out[:, t, :], x[:, t, :], moments[:, t, 0:1], rstd[:, t:t + 1],
                         ALU.subtract, ALU.mult, after=(scaled,))
    return token


def inverse_root(b, out, x, scale, eps, guard=ALU.add):
    summed = b.dve.do(b.nc.vector.tensor_scalar, out, x, scale, eps, ALU.mult, guard)
    return b.pool.do(b.nc.gpsimd.tensor_tensor, out, out, b.core.c["halves"][:, 0:out.shape[1]], ALU.pow,
                     after=(summed,))


def norm_room(nc, ctx, n, name):
    return (ctx.enter_context(nc.sbuf_tensor(f"{name}_stats", [P, n, 6], F32)),
            ctx.enter_context(nc.sbuf_tensor(f"{name}_moments", [P, n, 2], F32)),
            ctx.enter_context(nc.sbuf_tensor(f"{name}_rstd", [P, n], F32)))


def to_features(b, outT, x, bank, after, scale=None, bias=None):
    nc, width = b.nc, x.shape[2]
    done = None
    for first in range(0, x.shape[1], 4):
        n = min(4, x.shape[1] - first)
        room = b.psum[:, bank + first // 4, :]
        for t in range(n):
            b.pe.do(nc.tensor.transpose, room[0:width, t * P:(t + 1) * P], x[:, first + t, :], b.core.c["ident"],
                    after=after)
        turned = b.pe.mark()
        src = room[0:width, 0:n * P]
        dst = outT[0:width, first * P:(first + n) * P]
        if scale is None:
            done = b.act.do(nc.scalar.copy, dst, src, after=(turned,))
        else:
            done = b.act.do(nc.scalar.activation, dst, src, ACT.Identity, bias=bias, scale=scale, after=(turned,))
    return done


def down_project(b, out, hT, w, after, rows_of=None):
    n = hT.shape[1]
    for f in range(n):
        rows = P if rows_of is None else rows_of(f)
        for t in range(b.tiles):
            b.pe.product(out[:, t * P:(t + 1) * P], hT[0:rows, f, t * P:(t + 1) * P],
                    w[0:rows, f * P:(f + 1) * P], start=(f == 0 and t == 0), stop=(f == n - 1),
                    skip_group_check=True, after=after)
    return b.pe.mark()


def pick_largest(b, picked, value, best, weight, first, n_picks, after=()):
    T, E = value.shape[1], value.shape[2]
    nc, dve = b.nc, b.dve
    order = bcast(first[:, 0:E], 1, T)
    token = None
    for r in range(n_picks):
        top = best[:, 0:T]
        dve.do(nc.vector.tensor_reduce, top, value, AX, ALU.max, after=after)
        dve.do(nc.vector.tensor_tensor, weight, value, bcast(top, 2, E), ALU.is_equal)
        dve.do(nc.vector.tensor_tensor, weight, weight, order, ALU.mult)
        dve.do(nc.vector.tensor_reduce, top, weight, AX, ALU.max)
        token = dve.do(nc.vector.tensor_tensor, picked[r], weight, bcast(top, 2, E), ALU.is_equal)
        if r < n_picks - 1:
            dve.do(nc.vector.scalar_tensor_tensor, value, picked[r], NEG, value, ALU.mult, ALU.add)
    return token


def block_L0x(b, i, m):
    nc, psum, c = b.nc, b.psum, b.core.c
    x = b.core.x[:, bass.ts(i, b.tiles), :]
    got_ctx = b.load.do(nc.sync.dma_start, m["ctxT"][:], b.core.ctxT[:, bass.ts(i, b.ctok)])
    normed = layer_norm(b, m["xn"], x, LN_EPS, m["norm"])
    turned = to_features(b, m["xT"], m["xn"], 0, (normed,))
    for h in range(2):
        b.pe.product(psum[0:64, 2 + h, :], b.weight("wt"), m["ctxT"][:, h * BANK:(h + 1) * BANK],
                start=True, stop=True, after=(got_ctx,))
    pt = b.pe.mark()
    b.pe.product(psum[0:64, 1, :], b.weight("wv"), m["xT"][:], start=True, stop=True, after=(turned,))
    pv = b.pe.mark()
    t_done = b.act.do(nc.scalar.activation, m["tT"][0:64, :], psum[0:64, 2:4, :].rearrange("p a b -> p (a b)"), ACT.Identity,
                      bias=b.weight("bt"), scale=1.0, after=(pt,))
    v_done = b.act.do(nc.scalar.activation, m["vT"][0:64, :], psum[0:64, 1, :], ACT.Identity, bias=b.weight("bv"), scale=1.0,
                      after=(pv,))
    t_sq = b.pool.do(nc.gpsimd.tensor_tensor, m["t2"][:], m["tT"][:], m["tT"][:], ALU.mult, after=(t_done,))
    v_sq = b.pool.do(nc.gpsimd.tensor_tensor, m["v2"][:], m["vT"][:], m["vT"][:], ALU.mult, after=(v_done,))
    for s in range(b.seqs):
        q = slice(64 * (s % 2), 64 * (s % 2) + 64)
        b.pe.product(psum[q, 0, (s // 2) * P:(s // 2 + 1) * P], m["vT"][:, s * S:(s + 1) * S],
                m["tT"][:, s * SC:(s + 1) * SC], start=True, stop=True, after=(v_done, t_done))
    for s in range(b.seqs):
        q = slice(64 * (s % 2), 64 * (s % 2) + 64)
        b.pe.product(psum[q, 2, (s // 2) * P:(s // 2 + 1) * P], c["ones"][:, 0:64],
                m["t2"][:, s * SC:(s + 1) * SC], start=True, stop=True, after=(t_sq, t_done))
    for t in range(b.tiles):
        b.pe.product(psum[:, 1, t:t + 1], m["v2"][:, t * P:(t + 1) * P], c["ones"][:, 0:1],
                start=True, stop=True, after=(v_sq,))
    pd = b.pe.mark()
    b.dve.do(nc.vector.tensor_copy, m["vn"][:], psum[:, 1, 0:b.tiles], after=(pd,))
    for t in range(b.tiles):
        b.dve.do(nc.vector.tensor_scalar, m["r"][:, t, :], psum[:, 2, t * P:(t + 1) * P], m["vn"][:, t:t + 1], 1e-16,
                 ALU.mult, ALU.max)
    scaled = b.act.do(nc.scalar.activation, m["r"][:], m["r"][:], ACT.Sqrt, after=(b.dve.now(),))
    b.dve.do(nc.vector.reciprocal, m["r"][:], m["r"][:], after=(scaled,))
    b.dve.do(nc.vector.tensor_tensor, m["r"][:], m["r"][:], psum[:, 0, :].rearrange("p (t d) -> p t d", t=b.tiles),
             ALU.mult)
    b.dve.do(nc.vector.tensor_tensor, x, x, m["r"][:], ALU.add)


def room_L0x(nc, ctx, g):
    sb = lambda n, *shape, dt=F32: ctx.enter_context(nc.sbuf_tensor(f"{g.tag}L0x_{n}", list(shape), dt))
    return {"norm": norm_room(nc, ctx, g.tiles, g.tag + "L0x_norm"), "xn": sb("xn", P, g.tiles, D), "xT": sb("xT", P, g.tok),
            "ctxT": sb("ctxT", CX, g.ctok), "tT": sb("tT", P, g.ctok), "vT": sb("vT", P, g.tok), "t2": sb("t2", P, g.ctok),
            "v2": sb("v2", P, g.tok), "vn": sb("vn", P, g.tiles), "r": sb("r", P, g.tiles, D)}


def once_L0x(b, m):
    for name in ("tT", "vT"):
        b.nc.vector.memset(m[name][64:P], 0.0)


def phi(b, out, src, low, after):
    nc = b.nc
    cut = b.dve.do(nc.vector.tensor_scalar, low, src, 0.0, None, ALU.min, after=after)
    grown = b.act.do(nc.scalar.activation, low, low, ACT.Exp, after=(cut,))
    return b.dve.do(nc.vector.scalar_tensor_tensor, out, src, 0.0, low, ALU.max, ALU.add, after=(grown,))


def linear_attention(b, m, xT, ready, same, head, heads, eps):
    nc, psum = b.nc, b.psum
    b.pe.product(psum[:, 0, :], b.weight("wq"), xT[:], start=True, stop=True, after=(ready,))
    pq = b.pe.mark()
    kv = psum[:, 1:3, :].rearrange("p a (t c) -> p (a t) c", c=256)
    for t in range(b.tiles):
        b.pe.product(kv[:, t, 0:P], xT[:, t * P:(t + 1) * P], b.weight("wk"), start=True, stop=True)
        b.pe.product(kv[:, t, P:256], xT[:, t * P:(t + 1) * P], b.weight("wv"), start=True, stop=True)
    pkv = b.pe.mark()
    for r in range(2):
        v_done = b.act.do(nc.scalar.activation, m["va"][:, :, r, 0:P], kv[:, :, P:256], ACT.Copy,
                          scale=b.core.c["parity"][:, r:r + 1], after=(pkv,))
    q_done = phi(b, m["qT"][:], psum[:, 0, :], m["qlow"][:], (pq,))
    k_done = phi(b, m["k"][:], kv[:, :, 0:P], m["klow"][:], (v_done,))
    for t in range(b.tiles):
        b.pe.product(psum[:, t, 0:2 * (P + 1)], m["k"][:, t, :], m["va"][:, t, :, :].rearrange("p r d -> p (r d)"),
                     start=True, stop=True, after=(v_done, k_done, q_done))
    cross = psum[:, :, 0:2 * (P + 1)].rearrange("p t (r d) -> p t r d", r=2)
    kv_pair = m["kv"][:].rearrange("p (t r) d -> p t r d", r=2)
    pc = b.pe.mark()
    for r in range(2):
        b.dve.do(nc.vector.tensor_tensor, kv_pair[:, :, r, 0:P], cross[:, :, r, 0:P], bcast(same, 1, b.tiles), ALU.mult,
                 after=(pc,))
        kv_done = b.dve.do(nc.vector.tensor_tensor, kv_pair[:, :, r, P:P + heads],
                           cross[:, :, r, P:P + 1].to_broadcast([P, b.tiles, heads]), bcast(head, 1, b.tiles), ALU.mult)
    out = psum[:, 0:2, :].rearrange("p a (t c) -> p (a t) c", c=256)
    for t in range(b.tiles):
        for r in range(2):
            q = slice(64 * r, 64 * r + 64)
            b.pe.product(out[q, t, 0:P + heads], m["qT"][:, t * P + 64 * r:t * P + 64 * r + 64],
                    m["kv"][:, 2 * t + r, :], start=True, stop=True, after=(kv_done,))
    po = b.pe.mark()
    b.dve.do(nc.vector.tensor_scalar, m["z"][:], out[:, :, P:P + heads], eps, None, ALU.add, after=(po,))
    b.dve.do(nc.vector.reciprocal, m["z"][:], m["z"][:])
    msg = m["msg"][:].rearrange("p t (h d) -> p t h d", h=heads)
    return b.dve.do(nc.vector.tensor_tensor, msg, out[:, :, 0:P].rearrange("p t (h d) -> p t h d", h=heads),
                    bcast(m["z"][:], 3, P // heads), ALU.mult)


def room_linear(sb, g, heads):
    return {"qT": sb("qT", P, g.tok), "qlow": sb("qlow", P, g.tok), "k": sb("k", P, g.tiles, D), "klow": sb("klow", P, g.tiles, D),
            "va": sb("va", P, g.tiles, 2, D + 1), "kv": sb("kv", P, g.seqs, D + heads), "z": sb("z", P, g.tiles, heads),
            "msg": sb("msg", P, g.tiles, D)}


def block_L0a(b, i, m):
    nc, psum, c = b.nc, b.psum, b.core.c
    x = b.core.x[:, bass.ts(i, b.tiles), :]
    layer_norm(b, m["xin"], x, LN_EPS, m["norm"])
    normed = layer_norm(b, m["x2"], m["xin"], LN_EPS, m["norm"])
    ready = to_features(b, m["xT"], m["x2"], 3, (normed,), b.weight("g1"), b.weight("be1"))
    linear_attention(b, m, m["xT"], ready, c["same16"], c["head16"], 8, 1e-6)
    b.dve.do(nc.vector.tensor_tensor, m["xin"][:], m["xin"][:], m["msg"][:], ALU.add)
    normed = layer_norm(b, m["x2"], m["xin"], LN_EPS, m["norm"])
    ready = to_features(b, m["xT"], m["x2"], 3, (normed,), b.weight("g2"), b.weight("be2"))
    biased = b.pool.do(nc.gpsimd.tensor_tensor, m["xin"][:], m["xin"][:], bcast(b.weight("b2"), 1, b.tiles), ALU.add,
                       after=(normed,))
    for f in range(4):
        b.pe.product(psum[:, f, :], b.weight("w1")[:, f * P:(f + 1) * P], m["xT"][:], start=True,
                stop=True, after=(ready,))
        grown = b.act.do(nc.scalar.activation, m["hT"][:, f, :], psum[:, f, :], ACT.Gelu, bias=b.weight("b1")[:, f:f + 1],
                         scale=1.0, after=(b.pe.mark(),))
    down = down_project(b, psum[:, 0, :], m["hT"], b.weight("w2"), (grown,))
    b.dve.do(nc.vector.tensor_tensor, m["xin"][:], m["xin"][:], psum[:, 0, :].rearrange("p (t d) -> p t d", t=b.tiles),
             ALU.add, after=(down, biased))
    b.dve.do(nc.vector.tensor_tensor, x, x, m["xin"][:], ALU.add)


def room_L0a(nc, ctx, g):
    sb = lambda n, *shape, dt=F32: ctx.enter_context(nc.sbuf_tensor(f"{g.tag}L0a_{n}", list(shape), dt))
    m = {"norm": norm_room(nc, ctx, g.tiles, g.tag + "L0a_norm"), "xin": sb("xin", P, g.tiles, D), "x2": sb("x2", P, g.tiles, D),
         "xT": sb("xT", P, g.tok), "hT": sb("hT", P, 4, g.tok)}
    m.update(room_linear(sb, g, 8))
    return m


def once_ones(b, m):
    b.nc.vector.tensor_copy(m["va"][:, :, :, D], bcast(b.core.c["parity"][:, 0:2], 1, b.tiles))


def experts(b, m, xT, spread, hidden, after):
    nc, psum = b.nc, b.psum
    n = -(-hidden // P)
    free, finished, down = (None, None, None), [], []
    for f in range(n):
        rows = min(P, hidden - f * P)
        cols = slice(f * P, f * P + rows)
        waits = [(x,) if x is not None else () for x in free]
        b.pe.product(psum[0:rows, 1, 0:b.tok], b.weight("gate")[:, cols], xT[:], start=True, stop=True, after=(*after, *waits[0]))
        pg = b.pe.mark()
        b.pe.product(psum[0:rows, 2, 0:b.tok], b.weight("up")[:, cols], xT[:], start=True, stop=True, after=waits[1])
        pu = b.pe.mark()
        b.pe.product(psum[0:rows, 3, 0:b.tok], spread[:, cols], m["combT"][:], start=True, stop=True, after=waits[2])
        pc = b.pe.mark()
        if f >= 2:
            b.act.wait(down[f - 2])
        h = m["h"][0:rows, f % 2, :]
        s_done = b.act.do(nc.scalar.activation, h, psum[0:rows, 1, 0:b.tok], ACT.Silu, after=(pg,))
        gated = b.dve.do(nc.vector.tensor_tensor, h, h, psum[0:rows, 2, 0:b.tok], ALU.mult, after=(s_done, pu))
        finished.append(b.dve.do(nc.vector.tensor_tensor, h, h, psum[0:rows, 3, 0:b.tok], ALU.mult, after=(pc,)))
        free = (s_done, gated, finished[f])
        if f >= 1:
            down.append(expert_down(b, m, f - 1, n, hidden, finished[f - 1]))
    down.append(expert_down(b, m, n - 1, n, hidden, finished[n - 1]))
    return down[-1]


def expert_down(b, m, f, n, hidden, ready):
    rows = min(P, hidden - f * P)
    for t in range(b.tiles):
        b.pe.product(b.psum[:, 0, t * P:(t + 1) * P], m["h"][0:rows, f % 2, t * P:(t + 1) * P],
                b.weight("down")[0:rows, f * P:(f + 1) * P], start=(f == 0 and t == 0), stop=(f == n - 1),
                skip_group_check=True, after=(ready,))
    return b.pe.mark()


def turn_combine(b, m, comb, n, bank, after):
    nc, dve = b.nc, b.dve
    part, rest, comb = m["parts"][:], m["rest"][:], comb[:]
    dve.do(nc.vector.tensor_copy, part[:, :, 0:n], comb, after=after)
    dve.do(nc.vector.tensor_tensor, rest, comb, part[:, :, 0:n], ALU.subtract)
    dve.do(nc.vector.tensor_copy, part[:, :, n:2 * n], rest)
    dve.do(nc.vector.tensor_tensor, rest, rest, part[:, :, n:2 * n], ALU.subtract)
    split = dve.do(nc.vector.tensor_copy, part[:, :, 2 * n:3 * n], rest)
    return turn_parts(b, m["combT"][0:3 * n, :], part, 3 * n, bank, (split,))


def once_combine(b, m):
    b.nc.vector.memset(m["combT"][:], 0.0)


def turn_parts(b, out, part, n, bank, after):
    for t in range(b.tiles):
        b.pe.product(b.psum[0:n, bank, t * P:(t + 1) * P], part[:, t, 0:n], b.core.half["ident"], start=True, stop=True,
                     after=after)
    return b.act.do(b.nc.scalar.copy, out, b.psum[0:n, bank, 0:b.tok], after=(b.pe.mark(),))


def logits_of(b, xT, w, n, bank, after):
    out = b.psum[:, bank, 0:b.tiles * n].rearrange("p (t e) -> p t e", t=b.tiles)
    for t in range(b.tiles):
        b.pe.product(out[:, t, :], xT[:, t * P:(t + 1) * P], w, start=True, stop=True, after=after)
    return out, b.pe.mark()


def block_L0f(b, i, m):
    nc, psum, c = b.nc, b.psum, b.core.c
    x = b.core.x[:, bass.ts(i, b.tiles), :]
    normed = layer_norm(b, m["xn"], x, LN_EPS, m["norm"])
    ready = to_features(b, m["xT"], m["xn"], 0, (normed,))
    logits, pl = logits_of(b, m["xT"], b.weight("router"), EXPERTS0, 3, (ready,))
    scored = b.act.do(nc.scalar.activation, m["score"][:], logits, ACT.Sigmoid, after=(pl,))
    dve, tt = b.dve, nc.vector.tensor_tensor
    dve.do(tt, m["choice"][:], m["score"][:], bcast(b.weight("rbias"), 1, b.tiles), ALU.add, after=(scored,))
    pair = m["choice"][:].rearrange("p t (g a c) -> p (t g) a c", g=4, a=2)
    hi, lo, a1, a2, gs = (m[k][:] for k in ("hi", "lo", "a1", "a2", "gs"))
    dve.do(tt, hi, pair[:, :, :, 0], pair[:, :, :, 1], ALU.max)
    dve.do(tt, lo, pair[:, :, :, 0], pair[:, :, :, 1], ALU.min)
    dve.do(tt, a1, hi[:, :, 0], hi[:, :, 1], ALU.max)
    dve.do(tt, a2, hi[:, :, 0], hi[:, :, 1], ALU.min)
    dve.do(tt, gs, lo[:, :, 0], lo[:, :, 1], ALU.max)
    dve.do(tt, gs, gs, a2, ALU.max)
    dve.do(tt, gs, gs, a1, ALU.add)
    groups = [m["pick"][:, r, :, 0:4] for r in range(2)]
    pick_largest(b, groups, gs.rearrange("p (t g) -> p t g", g=4), m["best"], m["w"][:, :, 0:4], c["first"], 2)
    dve.do(tt, groups[0], groups[0], groups[1], ALU.add)
    gmask = m["gmask"][:]
    dve.do(nc.vector.tensor_copy, gmask.rearrange("p t (g e) -> p t g e", g=4), bcast(groups[0], 3, 4))
    dve.do(tt, m["choice"][:], m["choice"][:], gmask, ALU.mult)
    dve.do(nc.vector.tensor_scalar, gmask, gmask, 1.0, 1e9, ALU.subtract, ALU.mult)
    dve.do(tt, m["choice"][:], m["choice"][:], gmask, ALU.add)
    picks = [m["pick"][:, r, :, :] for r in range(4)]
    pick_largest(b, picks, m["choice"][:], m["best"], m["w"][:], c["first"], 4)
    for r in range(1, 4):
        dve.do(tt, picks[0], picks[0], picks[r], ALU.add)
    dve.do(tt, m["w"][:], picks[0], m["score"][:], ALU.mult)
    dve.do(nc.vector.tensor_reduce, m["best"][:], m["w"][:], AX, ALU.add)
    dve.do(nc.vector.tensor_scalar, m["best"][:], m["best"][:], 1e-20, None, ALU.add)
    dve.do(nc.vector.reciprocal, m["best"][:], m["best"][:])
    combined = dve.do(nc.vector.scalar_tensor_tensor, m["w"][:], m["w"][:], 2.5, bcast(m["best"][:], 2, EXPERTS0),
                      ALU.mult, ALU.mult)
    comb_ready = turn_combine(b, m, m["w"], EXPERTS0, 3, (combined,))
    done = experts(b, m, m["xT"], b.core.half["spread0"], EXPERTS0 * HID0, (comb_ready,))
    dve.do(tt, x, x, psum[:, 0, :].rearrange("p (t d) -> p t d", t=b.tiles), ALU.add, after=(done,))


def room_L0f(nc, ctx, g):
    sb = lambda n, *shape, dt=F32: ctx.enter_context(nc.sbuf_tensor(f"{g.tag}L0f_{n}", list(shape), dt))
    return {"norm": norm_room(nc, ctx, g.tiles, g.tag + "L0f_norm"), "xn": sb("xn", P, g.tiles, D), "xT": sb("xT", P, g.tok),
            "score": sb("score", P, g.tiles, 16), "choice": sb("choice", P, g.tiles, 16), "gmask": sb("gmask", P, g.tiles, 16),
            "hi": sb("hi", P, 4 * g.tiles, 2), "lo": sb("lo", P, 4 * g.tiles, 2), "a1": sb("a1", P, 4 * g.tiles),
            "a2": sb("a2", P, 4 * g.tiles), "gs": sb("gs", P, 4 * g.tiles), "pick": sb("pick", P, 4, g.tiles, 16),
            "best": sb("best", P, g.tiles), "w": sb("w", P, g.tiles, 16), "combT": sb("combT", P, g.tok, dt=BF16),
            "parts": sb("parts", P, g.tiles, 48, dt=BF16), "rest": sb("rest", P, g.tiles, 16),
            "h": sb("h", P, 2, g.tok)}


def block_L1x(b, i, m):
    nc, psum, c = b.nc, b.psum, b.core.c
    dve, act, pool, pe = b.dve, b.act, b.pool, b.pe
    tt = nc.vector.tensor_tensor
    x = b.core.x[:, bass.ts(i, b.tiles), :]
    heads, width, keys = 2, 64, SC + S
    got = b.load.do(nc.sync.dma_start, m["ctx"][:], b.core.ctx_tok[:, bass.ts(i, b.seqs), :])
    pairs = b.core.mask[:, bass.ts(i, b.tiles), :]
    for r in range(2):
        got_mask = b.load.do(nc.sync.dma_start, m["mask"][64 * r:64 * r + 64, :, :],
                             pairs[r:r + 1, :, :].to_broadcast([64, b.tiles, SC // 4]))
    normed = layer_norm(b, m["cn"], m["ctx"][:], LN_EPS, m["norm8"], (got,))
    c_ready = to_features(b, m["cT"], m["cn"], 0, (normed,), b.weight("xg"), b.weight("xb"))
    layer_norm(b, m["xn"], x, LN_EPS, m["norm"])
    normed = layer_norm(b, m["xn"], m["xn"], LN_EPS, m["norm"])
    l_ready = to_features(b, m["lT"], m["xn"], 1, (normed,), b.weight("lg"), b.weight("lb"))
    wql = b.weight("wql")
    qk = psum[:, 2, :].rearrange("p (t c) -> p t c", c=256)
    for t in range(b.tiles):
        pe.product(qk[:, t, :], m["lT"][:, t * P:(t + 1) * P], wql[:, 0:256], start=True, stop=True, after=(l_ready,))
    p_qk = pe.mark()
    for s in range(b.seqs):
        pe.product(psum[0:64, 3, s * P:(s + 1) * P], m["lT"][:, s * S:(s + 1) * S], wql[:, 256:384],
                   start=True, stop=True)
    p_v = pe.mark()
    qk_done = act.do(nc.scalar.copy, m["qk"][:], qk, after=(p_qk,))
    vl_done = act.do(nc.scalar.copy, m["vl"][0:64, :, :], psum[0:64, 3, :].rearrange("p (s d) -> p s d", d=P), after=(p_v,))
    kv = psum[:, 0:2, :].rearrange("p a (s c) -> p (a s) c", c=256)
    for s in range(b.seqs):
        pe.product(kv[:, s, :], m["cT"][:, s * SC:(s + 1) * SC], b.weight("wkv"), start=True, stop=True,
                   after=(c_ready, l_ready))
    kv_done = act.do(nc.scalar.copy, m["kv"][:], kv, after=(pe.mark(),))
    squares = pool.do(nc.gpsimd.tensor_tensor, m["sq"][:], m["qk"][:], m["qk"][:], ALU.mult, after=(qk_done,))
    csquares = pool.do(nc.gpsimd.tensor_tensor, m["csq"][:], m["kv"][:, :, 0:P], m["kv"][:, :, 0:P], ALU.mult,
                       after=(kv_done,))
    own, ctx = m["ss"][:, 0:4 * b.tiles], m["ss"][:, 4 * b.tiles:]
    dve.do(nc.vector.tensor_reduce, own, m["sq"][:].rearrange("p t (h d) -> p (t h) d", h=4), AX, ALU.add,
           after=(squares,))
    dve.do(nc.vector.tensor_reduce, ctx, m["csq"][:].rearrange("p s (h d) -> p (s h) d", h=heads), AX, ALU.add,
           after=(csquares,))
    scaled = inverse_root(b, m["ss"][:], m["ss"][:], 1.0 / width, 1e-16, ALU.max)
    view = m["qk"][:].rearrange("p t (h d) -> p (t h) d", h=4)
    qk_normed = dve.do(tt, view, view, bcast(own, 2, width), ALU.mult, after=(scaled,))
    kview = m["kv"][:, :, 0:P].rearrange("p s (h d) -> p s h d", h=heads)
    k_normed = dve.do(tt, kview, kview, bcast(ctx.rearrange("p (s h) -> p s h", h=heads), 3, width), ALU.mult)
    for h in range(heads):
        q_ready = to_features(b, m["qT"][:, h, :], m["qk"][:, :, 0:P], 2, (qk_normed,) if h == 0 else (q_ready,),
                              b.weight("qg")[:, h:h + 1], 0.0)
    kl_ready = to_features(b, m["klT"], m["qk"][:, :, P:256], 3, (vl_done,), b.weight("kg"), 0.0)
    kc_ready = to_features(b, m["kcT"], m["kv"][:, :, 0:P], 0, (k_normed, kv_done), b.weight("kg"), 0.0)
    for t in range(b.tiles):
        for h in range(heads):
            for first, n, kT in ((0, SC, m["kcT"]), (SC, S, m["klT"])):
                for r in range(2):
                    s = 2 * t + r
                    pe.product(psum[64 * r:64 * r + 64, h, t * keys + first:t * keys + first + n],
                               m["qT"][:, h, s * S:(s + 1) * S], kT[:, s * n:(s + 1) * n], start=True, stop=True,
                               after=(q_ready, kl_ready, kc_ready))
    p_s = pe.mark()
    dve.do(nc.vector.tensor_scalar, m["mb"][:], m["mask"][:].bitcast(U8), 1.0, 3.0e38, ALU.subtract, ALU.mult,
           after=(got_mask,))
    for h in range(heads):
        src = psum[:, h, 0:b.tiles * keys].rearrange("p (t k) -> p t k", k=keys)
        dst = m["p"][:, h, :, :]
        added = dve.do(tt, dst[:, :, 0:SC], src[:, :, 0:SC], m["mb"][:], ALU.add, after=(p_s,))
        copied = act.do(nc.scalar.copy, dst[:, :, SC:keys], src[:, :, SC:keys], after=(added,))
    prob = m["p"][:].rearrange("p h t k -> p (h t) k")
    dve.do(nc.vector.tensor_reduce, m["mx"][:], prob, AX, ALU.max, after=(copied,))
    lowered = dve.do(tt, prob, prob, bcast(m["mx"][:], 2, keys), ALU.subtract)
    grown = act.do(nc.scalar.activation, prob, prob, ACT.Exp, scale=width ** -0.5, after=(lowered,))
    dve.do(nc.vector.tensor_reduce, m["mx"][:], prob, AX, ALU.add, after=(grown,))
    dve.do(nc.vector.reciprocal, m["mx"][:], m["mx"][:])
    p_done = dve.do(tt, prob, prob, bcast(m["mx"][:], 2, keys), ALU.mult)
    for n in range(heads * b.tiles):
        pe.do(nc.tensor.transpose, psum[:, 2, n * P:(n + 1) * P], prob[:, n, 0:SC], c["ident"], after=(p_done,))
    p_c = pe.mark()
    for n in range(heads * b.tiles):
        pe.do(nc.tensor.transpose, psum[0:64, 3, n * P:(n + 1) * P], prob[:, n, SC:keys], c["ident"])
    p_l = pe.mark()
    pc_done = act.do(nc.scalar.copy, m["pcT"][:], psum[:, 2, :], after=(p_c,))
    pl_done = dve.do(nc.vector.tensor_copy, m["plT"][0:64, :], psum[0:64, 3, :], after=(p_l,))
    for s in range(b.seqs):
        t, r = s // 2, s % 2
        for h in range(heads):
            f = slice(width * h, width * h + width)
            q = slice((h * b.tiles + t) * P + 64 * r, (h * b.tiles + t) * P + 64 * r + 64)
            pe.product(psum[f, 0, s * S:(s + 1) * S], m["kv"][:, s, P + width * h:P + width * h + width],
                       m["pcT"][:, q], start=True, stop=False, skip_group_check=True, after=(pc_done, pl_done))
            pe.product(psum[f, 0, s * S:(s + 1) * S], m["vl"][:, s, f], m["plT"][:, q], start=False, stop=True,
                       skip_group_check=True)
    o_done = act.do(nc.scalar.copy, m["oT"][:], psum[:, 0, 0:b.tok], after=(pe.mark(),))
    project_out(b, x, m["oT"], b.weight("wo"), b.weight("bo"), 1, (o_done,))


def project_out(b, x, inT, w, bias, bank, after):
    nc = b.nc
    if bias is not None:
        b.dve.do(nc.vector.tensor_tensor, x, x, bcast(bias, 1, b.tiles), ALU.add)
    for t in range(b.tiles):
        b.pe.product(b.psum[:, bank, t * P:(t + 1) * P], inT[:, t * P:(t + 1) * P], w, start=True, stop=True,
                     after=after)
    return b.dve.do(nc.vector.tensor_tensor, x, x, b.psum[:, bank, 0:b.tok].rearrange("p (t d) -> p t d", t=b.tiles),
                    ALU.add, after=(b.pe.mark(),))


def room_L1x(nc, ctx, g):
    sb = lambda n, *shape, dt=F32: ctx.enter_context(nc.sbuf_tensor(f"{g.tag}L1x_{n}", list(shape), dt))
    return {"norm": norm_room(nc, ctx, g.tiles, g.tag + "L1x_norm"), "norm8": norm_room(nc, ctx, g.seqs, g.tag + "L1x_norm8"),
            "ctx": sb("ctx", P, g.seqs, CX), "mask": sb("mask", P, g.tiles, SC // 4, dt=I32),
            "cn": sb("cn", P, g.seqs, CX), "cT": sb("cT", CX, g.ctok), "xn": sb("xn", P, g.tiles, D), "lT": sb("lT", P, g.tok),
            "qk": sb("qk", P, g.tiles, 256), "vl": sb("vl", P, g.seqs, P), "kv": sb("kv", P, g.seqs, 256),
            "sq": sb("sq", P, g.tiles, 256), "csq": sb("csq", P, g.seqs, P), "ss": sb("ss", P, 4 * g.tiles + 2 * g.seqs),
            "qT": sb("qT", P, 2, g.tok), "klT": sb("klT", P, g.tok), "kcT": sb("kcT", P, g.ctok), "mb": sb("mb", P, g.tiles, SC),
            "p": sb("p", P, 2, g.tiles, SC + S), "mx": sb("mx", P, 2 * g.tiles), "pcT": sb("pcT", P, g.ctok),
            "plT": sb("plT", P, g.ctok), "oT": sb("oT", P, g.tok)}


def once_L1x(b, m):
    b.nc.vector.memset(m["vl"][64:P], 0.0)
    b.nc.vector.memset(m["plT"][64:P], 0.0)



HEADS, WIDTH, QUAD = 16, 8, 4
LANE = 32


def attention_waves(b, m, keys, scale, clip, ready):
    nc, psum, c = b.nc, b.psum, b.core.c
    dve, act, pe = b.dve, b.act, b.pe
    tiles = P // keys
    per_block = P // keys
    n_rows = 2 * tiles * QUAD
    one = WIDTH + 1
    for w in range(b.tiles // tiles):
        p_s, grown, copied = [], [], []
        for half in range(2):
            for g in (2 * half, 2 * half + 1):
                for u in range(tiles):
                    for r in range(2):
                        s = 2 * (w * tiles + u) + r
                        out = psum[64 * r:64 * r + 64, g, u * QUAD * keys:(u + 1) * QUAD * keys]
                        pe.product(out.rearrange("p (j k) -> p j k", j=QUAD), m["qx"][:, g, s * S:(s + 1) * S],
                                   m["kx"][:, :, s * keys:(s + 1) * keys], start=True, stop=True, after=ready)
            p_s.append(pe.mark())
        for half in range(2):
            p = m["p"][:, half * 1024:(half + 1) * 1024].rearrange("p (n k) -> p n k", k=keys)
            s = psum[:, 2 * half:2 * half + 2, :].rearrange("p a (n k) -> p (a n) k", k=keys)
            mx = m["mx"][:, half * n_rows:(half + 1) * n_rows]
            dve.do(nc.vector.tensor_reduce, mx, s, AX, ALU.max, after=(p_s[half],))
            if clip is None:
                low = dve.do(nc.vector.tensor_tensor, p, s, bcast(mx, 2, keys), ALU.subtract)
            else:
                limit = clip / scale
                dve.do(nc.vector.tensor_scalar, mx, mx, limit, -limit, ALU.min, ALU.max)
                dve.do(nc.vector.scalar_tensor_tensor, p, s, -limit, bcast(mx, 2, keys), ALU.max, ALU.subtract)
                low = dve.do(nc.vector.tensor_scalar, p, p, 0.0, None, ALU.min)
            grown.append(act.do(nc.scalar.activation, p, p, ACT.Exp, scale=scale, after=(low,)))
        for half in range(2):
            for n in range(8 * half, 8 * half + 8):
                pe.do(nc.tensor.transpose, psum[:, n // 4, (n % 4) * P:(n % 4 + 1) * P], m["p"][:, n * P:(n + 1) * P],
                      c["ident"], after=(grown[half],))
            queue, copy = (act, nc.scalar.copy) if half == 0 else (dve, nc.vector.tensor_copy)
            copied.append(queue.do(copy, m["pT"][:, half * 1024:(half + 1) * 1024].rearrange("p (a b) -> p a b", a=2),
                                   psum[:, 2 * half:2 * half + 2, :], after=(pe.mark(),)))
        for g in range(QUAD):
            for u in range(tiles):
                for k in range(QUAD // per_block):
                    n = (g * tiles + u) * (QUAD // per_block) + k
                    h = QUAD * g + per_block * k
                    rows = slice(LANE * per_block * k, LANE * per_block * (k + 1))
                    pe.product(psum[rows, u, g * P:(g + 1) * P],
                               m["va"][:, w * tiles + u, h:h + per_block, :].rearrange("p h e -> p (h e)"),
                               m["pT"][:, n * P:(n + 1) * P], start=True, stop=True, after=(copied[g // 2],))
            if g == 1:
                pe.mark()
        o_done = act.do(nc.scalar.copy, m["oT"][:, 0:tiles, :], psum[:, 0:tiles, :], after=(pe.mark(),))
        for u in range(tiles):
            for g in range(QUAD):
                pe.do(nc.tensor.transpose, psum[:, 2 + u, g * P:(g + 1) * P], m["oT"][:, u, g * P:(g + 1) * P],
                      c["ident"], after=(o_done,))
        p_o = pe.mark()
        out = psum[:, 2:2 + tiles, :].rearrange("p u (h e) -> p u h e", h=HEADS)
        att = m["att"][:, w * tiles:(w + 1) * tiles, :].rearrange("p u (h d) -> p u h d", h=HEADS)
        for r in range(2):
            q = slice(64 * r, 64 * r + 64)
            z = m["z"][q, 0:tiles, :]
            dve.do(nc.vector.reciprocal, z, out[q, :, :, r * one + WIDTH], after=(p_o,))
            done = dve.do(nc.vector.tensor_tensor, att[q], out[q, :, :, r * one:r * one + WIDTH], bcast(z, 3, WIDTH),
                          ALU.mult)
        ready = (done,)
    return done


def room_attention(sb, g, keys):
    return {"xn": sb("xn", P, g.tiles, D), "xT": sb("xT", P, g.tok), "qx": sb("qx", P, QUAD, g.tok),
            "kx": sb("kx", P, QUAD, g.seqs * keys), "va": sb("va", P, g.tiles, HEADS, LANE), "p": sb("p", P, 2048),
            "oT": sb("oT", P, P // keys, BANK),
            "pT": sb("pT", P, 2048), "mx": sb("mx", P, 32), "z": sb("z", P, 2, HEADS), "att": sb("att", P, g.tiles, D)}


def rotate(b, out, src, partner, cos, sin, twin, after):
    nc = b.nc
    seqs = lambda ap: ap.rearrange("p (s k) -> p s k", k=S)
    b.dve.do(nc.vector.tensor_tensor, seqs(out), seqs(src), bcast(cos, 1, b.seqs), ALU.mult, after=after)
    both = b.dve.do(nc.vector.tensor_tensor, seqs(twin), seqs(partner), bcast(sin, 1, b.seqs), ALU.mult)
    return b.pool.do(nc.gpsimd.tensor_tensor, out, out, twin, ALU.add, after=(both,))


def block_L1a(b, i, m):
    nc, psum, c = b.nc, b.psum, b.core.c
    x = b.core.x[:, bass.ts(i, b.tiles), :]
    normed = layer_norm(b, m["xn"], x, LN_EPS, m["norm"])
    ready = to_features(b, m["xT"], m["xn"], 3, (normed,))
    for n, w in enumerate(("wk", "wkp", "wq", "wqp")):
        b.pe.product(psum[:, n, :], b.weight(w), m["xT"][:], start=True, stop=True, after=(ready,))
        if n == 1:
            pk = b.pe.mark()
    pq = b.pe.mark()
    twice = b.pool.do(nc.gpsimd.tensor_copy, m["x2"][:], bcast(m["xT"][:].rearrange("p (s k) -> p s k", k=S), 2, 2),
                      after=(ready,), alone=True)
    k_ready = rotate(b, m["kT"][:], psum[:, 0, :], psum[:, 1, :], c["cos8"], c["sin8"], m["twin"][:], (pk,))
    for s in range(b.seqs):
        b.pe.product(psum[:, s // 4, (s % 4) * P:(s % 4 + 1) * P], m["x2"][:, s, :, :].rearrange("p a k -> p (a k)"),
                     b.weight("wv"), start=True, stop=True, after=(twice, k_ready))
    pv = b.pe.mark()
    q_ready = rotate(b, m["qT"][:], psum[:, 2, :], psum[:, 3, :], c["cos8"], c["sin8"], m["twin2"][:], (pq,))
    values = psum[:, 0:2, :].rearrange("p a (t r h d) -> p (a t) h r d", r=2, h=HEADS, d=WIDTH)
    for r in range(2):
        v_ready = b.dve.do(nc.vector.tensor_tensor, m["va"][:, :, :, r * (WIDTH + 1):r * (WIDTH + 1) + WIDTH], values[:, :, :, r, :],
                           bcast(bcast(c["parity"], 1, b.tiles), 3, WIDTH), ALU.mult, after=(pv,))
    for j in range(QUAD):
        k_kept = b.dve.do(nc.vector.tensor_scalar, m["kx"][:, j, :], m["kT"][:], c["lane4"][:, j:j + 1], None, ALU.mult,
                          after=(k_ready,))
    for g in range(QUAD):
        q_kept = b.act.do(nc.scalar.activation, m["qx"][:, g, :], m["qT"][:], ACT.Copy, scale=c["quad"][:, g:g + 1],
                          after=(q_ready,))
    done = attention_waves(b, m, S, WIDTH ** -0.5, None, (k_kept, q_kept, v_ready))
    turned = to_features(b, m["xT"], m["att"], 2, (done,))
    project_out(b, x, m["xT"], b.weight("wo"), b.weight("bo"), 3, (turned,))


def room_L1a(nc, ctx, g):
    sb = lambda n, *shape, dt=F32: ctx.enter_context(nc.sbuf_tensor(f"{g.tag}L1a_{n}", list(shape), dt))
    return {"norm": norm_room(nc, ctx, g.tiles, g.tag + "L1a_norm"), **room_attention(sb, g, S), "twin": sb("twin", P, g.tok),
            "qT": sb("qT", P, g.tok), "kT": sb("kT", P, g.tok), "x2": sb("x2", P, g.seqs, 2, S), "twin2": sb("twin2", P, g.tok)}


def once_L1a(b, m):
    nc, parity = b.nc, b.core.c["parity"]
    nc.vector.memset(m["va"][:, :, :, 2 * (WIDTH + 1):LANE], 0.0)
    for r in range(2):
        nc.vector.tensor_copy(m["va"][:, :, :, r * (WIDTH + 1) + WIDTH], bcast(parity, 1, b.tiles))


def context_attention(b, i, m, clip):
    nc, psum, c = b.nc, b.psum, b.core.c
    x = b.core.x[:, bass.ts(i, b.tiles), :]
    got = b.load.do(nc.sync.dma_start, m["ctxT"][:], b.core.ctxT[:, bass.ts(i, b.ctok)])
    normed = layer_norm(b, m["xn"], x, LN_EPS, m["norm"])
    for h in range(2):
        b.pe.product(psum[:, h, :], b.weight("wk"), m["ctxT"][:, h * BANK:(h + 1) * BANK], start=True, stop=True,
                     after=(got,))
    pk = b.pe.mark()
    for s in range(b.seqs):
        b.pe.product(psum[:, 2 + s // 4, (s % 4) * P:(s % 4 + 1) * P], m["ctxT"][:, s * SC:(s + 1) * SC],
                     b.weight("wv"), start=True, stop=True)
    pv = b.pe.mark()
    for j in range(QUAD):
        k_ready = b.act.do(nc.scalar.activation, m["kx"][:, j, :].rearrange("p (a b) -> p a b", a=2), psum[:, 0:2, :],
                           ACT.Identity, bias=b.weight("bk")[:, j:j + 1], scale=c["lane4"][:, j:j + 1], after=(pk,))
    values = psum[:, 2:4, :].rearrange("p a (t r h d) -> p (a t) h r d", r=2, h=HEADS, d=WIDTH)
    for r in range(2):
        v_ready = b.dve.do(nc.vector.tensor_tensor, m["va"][:, :, :, r * (WIDTH + 1):r * (WIDTH + 1) + WIDTH], values[:, :, :, r, :],
                           bcast(b.weight("bv").rearrange("p (h d) -> p h d", h=HEADS), 1, b.tiles), ALU.add, after=(pv,))
    ready = to_features(b, m["xT"], m["xn"], 0, (normed, k_ready))
    b.pe.product(psum[:, 1, :], b.weight("wq"), m["xT"][:], start=True, stop=True, after=(ready,))
    pq = b.pe.mark()
    for g in range(QUAD):
        q_ready = b.act.do(nc.scalar.activation, m["qx"][:, g, :], psum[:, 1, :], ACT.Identity,
                           bias=b.weight("bq")[:, g:g + 1], scale=c["quad"][:, g:g + 1], after=(pq,))
    return attention_waves(b, m, SC, WIDTH ** -0.5, clip, (q_ready, v_ready))


def block_L2x(b, i, m):
    done = context_attention(b, i, m, 10000.0)
    turned = to_features(b, m["xT"], m["att"], 3, (done,))
    project_out(b, b.core.x[:, bass.ts(i, b.tiles), :], m["xT"], b.weight("wo"), b.weight("bo"), 2, (turned,))


def room_L2x(nc, ctx, g, name="L2x"):
    sb = lambda n, *shape, dt=F32: ctx.enter_context(nc.sbuf_tensor(f"{g.tag}{name}_{n}", list(shape), dt))
    return {"norm": norm_room(nc, ctx, g.tiles, g.tag + name + "_norm"), **room_attention(sb, g, SC), "ctxT": sb("ctxT", CX, g.ctok)}


def once_value_ones(b, m):
    b.nc.vector.memset(m["va"][:, :, :, 2 * (WIDTH + 1):LANE], 0.0)
    for r in range(2):
        b.nc.vector.memset(m["va"][:, :, :, r * (WIDTH + 1) + WIDTH], 1.0)


def block_L3x(b, i, m):
    nc, psum = b.nc, b.psum
    x = b.core.x[:, bass.ts(i, b.tiles), :]
    done = context_attention(b, i, m, None)
    turned = to_features(b, m["xT"], m["att"], 3, (done,))
    b.dve.do(nc.vector.tensor_tensor, x, x, bcast(b.weight("b2"), 1, b.tiles), ALU.add)
    for f in range(2):
        b.pe.product(psum[:, f, :], b.weight("w1")[:, f * P:(f + 1) * P], m["xT"][:], start=True, stop=True,
                     after=(turned,))
        grown = b.act.do(nc.scalar.activation, m["hT"][:, f, :], psum[:, f, :], ACT.Relu, bias=b.weight("b1")[:, f:f + 1],
                         scale=1.0, after=(b.pe.mark(),))
    down = down_project(b, psum[:, 2, :], m["hT"], b.weight("w2"), (grown,))
    b.dve.do(nc.vector.tensor_tensor, x, x, psum[:, 2, :].rearrange("p (t d) -> p t d", t=b.tiles), ALU.add, after=(down,))


def room_L3x(nc, ctx, g):
    m = room_L2x(nc, ctx, g, "L3x")
    m["hT"] = ctx.enter_context(nc.sbuf_tensor(f"{g.tag}L3x_hT", [P, 2, g.tok], F32))
    return m


def softmax_rows(b, e, logits, bias, best, after):
    nc, dve, n = b.nc, b.dve, e.shape[2]
    dve.do(nc.vector.tensor_tensor, e, logits, bcast(bias, 1, b.tiles), ALU.add, after=after)
    dve.do(nc.vector.tensor_reduce, best, e, AX, ALU.max)
    low = dve.do(nc.vector.tensor_tensor, e, e, bcast(best, 2, n), ALU.subtract)
    grown = b.act.do(nc.scalar.activation, e, e, ACT.Exp, after=(low,))
    dve.do(nc.vector.tensor_reduce, best, e, AX, ALU.add, after=(grown,))
    dve.do(nc.vector.reciprocal, best, best)
    return dve.do(nc.vector.tensor_tensor, e, e, bcast(best, 2, n), ALU.mult)


def block_L1f(b, i, m):
    nc, psum, c = b.nc, b.psum, b.core.c
    dve, act, pe, pool = b.dve, b.act, b.pe, b.pool
    tt = nc.vector.tensor_tensor
    x = b.core.x[:, bass.ts(i, b.tiles), :]
    normed = layer_norm(b, m["xn"], x, LN_EPS, m["norm"])
    ready = to_features(b, m["xT"], m["xn"], 0, (normed,))
    logits, pl = logits_of(b, m["xT"], b.weight("gate"), EXPERTS1, 3, (ready,))
    pe.product(psum[:, 1, :], b.weight("la"), m["xT"][:], start=True, stop=True)
    a_done = act.do(nc.scalar.copy, m["aT"][:], psum[:, 1, :], after=(pe.mark(),))
    softmax_rows(b, m["e"][:], logits, b.weight("gb"), m["best"][:], (pl,))
    dve.do(nc.vector.tensor_copy, m["v"][:], m["e"][:])
    picks = [m["pick"][:, :, r, :] for r in range(2)]
    picked = pick_largest(b, picks, m["v"][:], m["best"], m["w"][:], c["first"], 2)
    both = dve.do(nc.vector.tensor_copy, m["pick16"][:], m["pick"][:].rearrange("p t r e -> p t (r e)"), after=(picked,))
    turned = turn_parts(b, m["pickT"][0:2 * EXPERTS1, :], m["pick16"][:], 2 * EXPERTS1, 3, (both,))
    for r in range(2):
        pe.product(psum[:, 2 + r, :], b.core.half[f"pick{r}"], m["pickT"][:], start=True, stop=True, after=(turned,))
        low = dve.do(tt, m["low"][:, r, :], m["aT"][:], psum[:, 2 + r, :], ALU.mult, after=(pe.mark(), a_done))
    dve.do(tt, m["w"][:], picks[0], picks[1], ALU.add)
    dve.do(tt, m["w"][:], m["w"][:], m["e"][:], ALU.mult)
    dve.do(nc.vector.tensor_reduce, m["best"][:], m["w"][:], AX, ALU.add)
    readers = [a_done, low, low]
    for f in range(4):
        cols = slice(f * P, (f + 1) * P)
        bias = b.weight("bi")[:, f:f + 1]
        for r in range(2):
            bank = 1 + (2 * f + r) % 3
            pe.product(psum[:, bank, :], b.weight("wi")[:, cols], m["xT"][:], start=True, stop=False,
                       after=(low, readers[2 * f + r]))
            pe.product(psum[:, bank, :], b.weight("lb")[:, cols], m["low"][:, r, :], start=False, stop=True)
            done = pe.mark()
            if r == 0:
                readers.append(act.do(nc.scalar.activation, m["r0"][:, f % 2, :], psum[:, bank, :], ACT.Relu, bias=bias,
                                      scale=1.0, after=(done,)))
            else:
                readers.append(dve.do(nc.vector.tensor_scalar, m["hT"][:, f, :], psum[:, bank, :], bias, 0.0, ALU.add,
                                      ALU.max, after=(done,)))
        h_done = pool.do(nc.gpsimd.tensor_tensor, m["hT"][:, f, :], m["hT"][:, f, :], m["r0"][:, f % 2, :], ALU.add,
                         after=readers[-2:])
        if f == 1:
            act.wait(h_done)
    down = down_project(b, psum[:, 0, :], m["hT"], b.weight("wo"), (h_done,))
    y = m["xn"][:]
    dve.do(nc.vector.scalar_tensor_tensor, y, bcast(b.weight("bo"), 1, b.tiles), 2.0,
           psum[:, 0, :].rearrange("p (t d) -> p t d", t=b.tiles), ALU.mult, ALU.add, after=(down,))
    dve.do(tt, y, y, bcast(m["best"][:], 2, D), ALU.mult)
    dve.do(tt, x, x, y, ALU.add)


def room_L1f(nc, ctx, g):
    sb = lambda n, *shape, dt=F32: ctx.enter_context(nc.sbuf_tensor(f"{g.tag}L1f_{n}", list(shape), dt))
    return {"norm": norm_room(nc, ctx, g.tiles, g.tag + "L1f_norm"), "xn": sb("xn", P, g.tiles, D), "xT": sb("xT", P, g.tok), "aT": sb("aT", P, g.tok),
            "e": sb("e", P, g.tiles, 8), "v": sb("v", P, g.tiles, 8), "w": sb("w", P, g.tiles, 8), "best": sb("best", P, g.tiles),
            "pick": sb("pick", P, g.tiles, 2, 8), "pick16": sb("pick16", P, g.tiles, 16, dt=BF16),
            "pickT": sb("pickT", P, g.tok, dt=BF16), "low": sb("low", P, 2, g.tok),
            "r0": sb("r0", P, 2, g.tok), "hT": sb("hT", P, 4, g.tok)}


def once_L1f(b, m):
    b.nc.vector.memset(m["pickT"][:], 0.0)


def block_L2a(b, i, m):
    x = b.core.x[:, bass.ts(i, b.tiles), :]
    normed = layer_norm(b, m["x2"], x, LN_EPS, m["norm"])
    ready = to_features(b, m["xT"], m["x2"], 3, (normed,))
    done = linear_attention(b, m, m["xT"], ready, b.core.c["same8"], b.core.c["head8"], 16, 1e-6)
    turned = to_features(b, m["xT"], m["msg"], 2, (done,))
    project_out(b, x, m["xT"], b.weight("wo"), None, 3, (turned,))


def room_L2a(nc, ctx, g):
    sb = lambda n, *shape, dt=F32: ctx.enter_context(nc.sbuf_tensor(f"{g.tag}L2a_{n}", list(shape), dt))
    return {"norm": norm_room(nc, ctx, g.tiles, g.tag + "L2a_norm"), "x2": sb("x2", P, g.tiles, D), "xT": sb("xT", P, g.tok), **room_linear(sb, g, 16)}


def rms_norm(b, out, x, square, ss, eps, after=()):
    nc, dve = b.nc, b.dve
    squares = b.pool.do(nc.gpsimd.tensor_tensor, square, x, x, ALU.mult, after=(dve.now(), *after))
    dve.do(nc.vector.tensor_reduce, ss, square, AX, ALU.add, after=(squares,))
    scaled = inverse_root(b, ss, ss, 1.0 / x.shape[2], eps)
    return dve.do(nc.vector.tensor_tensor, out, x, bcast(ss, 2, x.shape[2]), ALU.mult, after=(scaled,))


def block_L2f(b, i, m):
    nc, psum, c = b.nc, b.psum, b.core.c
    dve, act, pe, pool = b.dve, b.act, b.pe, b.pool
    tt = nc.vector.tensor_tensor
    x = b.core.x[:, bass.ts(i, b.tiles), :]
    layer_norm(b, m["x0"], x, LN_EPS, m["norm"])
    normed = rms_norm(b, m["xn"][:], m["x0"][:], m["sq"][:], m["ss"][:], 1e-5)
    ready = to_features(b, m["xT"], m["xn"], 0, (normed,), b.weight("g1"), 0.0)
    pe.product(psum[0:16, 1, 0:b.tok], b.weight("wkl"), m["xT"][:], start=True, stop=True, after=(ready,))
    p_lat = pe.mark()
    latent = act.do(nc.scalar.copy, m["latT"][0:16, :], psum[0:16, 1, 0:b.tok], after=(p_lat,))
    latent2 = act.do(nc.scalar.copy, m["lat2"][0:16], bcast(psum[0:16, 1, 0:b.tok].rearrange("p (s k) -> p s k", k=S), 2, 2))
    pe.product(psum[:, 0, 0:b.tok], b.weight("wkr"), m["xT"][:], start=True, stop=True)
    pe.product(psum[:, 0, b.tok:2 * b.tok], b.weight("wkp"), m["xT"][:], start=True, stop=True)
    kr_ready = rotate(b, m["krT"][:], psum[:, 0, 0:b.tok], psum[:, 0, b.tok:2 * b.tok], c["cos32"], c["sin32"],
                      m["twin"][:, 0, :], (pe.mark(),))
    chunk = lambda bank, n: psum[:, bank + n // 2, (n % 2) * b.tok:(n % 2 + 1) * b.tok]
    for n in range(4):
        pe.product(chunk(2, n), b.weight("wkvb")[:, n * P:(n + 1) * P], m["latT"][:], start=True, stop=True,
                   after=(latent,))
    p_kv = pe.mark()
    for j in range(4):
        kr_kept = act.do(nc.scalar.activation, m["krx"][:, j, :], m["krT"][:], ACT.Copy, scale=c["quad"][:, j:j + 1],
                         after=(kr_ready,))
    for j in range(4):
        kv_kept = act.do(nc.scalar.activation, m["knx"][:, :, j, :],
                         psum[:, 2:4, :].rearrange("p a (n k) -> p (a n) k", n=2), ACT.Copy, scale=c["quad"][:, j:j + 1],
                         after=(p_kv,))
    freed = []
    for n in range(4):
        cols = slice(n * P, (n + 1) * P)
        base = 2 * (n % 2)
        free = freed[n - 2] if n >= 2 else (kr_ready, latent2) if n == 0 else (kv_kept,)
        pe.product(psum[:, base, 0:b.tok], b.weight("wqn")[:, cols], m["xT"][:], start=True, stop=True, after=free)
        pn = pe.mark()
        pe.product(psum[:, base + 1, 0:b.tok], b.weight("wqr")[:, cols], m["xT"][:], start=True, stop=True)
        pe.product(psum[:, base + 1, b.tok:2 * b.tok], b.weight("wqp")[:, cols], m["xT"][:], start=True, stop=True)
        pr = pe.mark()
        nope = act.do(nc.scalar.copy, m["qnT"][:, n, :], psum[:, base, 0:b.tok], after=(pn,))
        q_ready = rotate(b, m["qrT"][:, n, :], psum[:, base + 1, 0:b.tok], psum[:, base + 1, b.tok:2 * b.tok], c["cos32"],
                         c["sin32"], m["twin"][:, n % 2, :], (pr,))
        if n == 1:
            dve.wait(q_ready)
        freed.append((nope, q_ready))
    own = bcast(c["parity"], 2, 32)
    for s in range(b.seqs):
        free = (freed[2 + s // 2] if s % 2 == 0 else ())
        pe.product(psum[:, s, :], m["lat2"][:, s, :, :].rearrange("p a k -> p (a k)"), b.weight("wkvb"),
                   start=True, stop=True, after=(latent2, *free))
        read = dve.do(tt, m["va"][:, s, :, 0:32], psum[:, s, :].rearrange("p (h d) -> p h d", h=16), own, ALU.mult,
                      after=(pe.mark(),))
    p_s, grown, copied = [], [], []
    for u in range(b.tiles):
        for n in range(4):
            for q_, k_, first in ((m["qnT"], m["knx"][:, n, :, :], True), (m["qrT"], m["krx"], False)):
                for r in range(2):
                    q = slice((2 * u + r) * S, (2 * u + r + 1) * S)
                    out = psum[64 * r:64 * r + 64, 2 * u + n // 2, (n % 2) * 4 * S:(n % 2 + 1) * 4 * S]
                    pe.product(out.rearrange("p (j k) -> p j k", j=4), q_[:, n, q], k_[:, :, q], start=first,
                               stop=not first, skip_group_check=True, after=(read, q_ready, nope, kr_kept, kv_kept))
        p_s.append(pe.mark())
    for u in range(b.tiles):
        p = m["p"][:, u * 1024:(u + 1) * 1024].rearrange("p (n k) -> p n k", k=S)
        mx = m["mx"][:, 16 * u:16 * u + 16]
        dve.do(tt, p, psum[:, 2 * u:2 * u + 2, :].rearrange("p a (n k) -> p (a n) k", k=S), bcast(c["causal"], 1, 16),
               ALU.add, after=(p_s[u],))
        dve.do(nc.vector.tensor_reduce, mx, p, AX, ALU.max)
        low = dve.do(tt, p, p, bcast(mx, 2, S), ALU.subtract)
        grown.append(act.do(nc.scalar.activation, p, p, ACT.Exp, scale=0.125, after=(low,)))
    for u in range(b.tiles):
        for n in range(8 * u, 8 * u + 8):
            pe.do(nc.tensor.transpose, psum[:, n // 4, (n % 4) * P:(n % 4 + 1) * P], m["p"][:, n * P:(n + 1) * P],
                  c["ident"], after=(grown[u],))
        queue, copy = (act, nc.scalar.copy) if u == 0 else (dve, nc.vector.tensor_copy)
        copied.append(queue.do(copy, m["pT"][:, u * 1024:(u + 1) * 1024].rearrange("p (a b) -> p a b", a=2),
                               psum[:, 2 * u:2 * u + 2, :], after=(pe.mark(),)))
    for u in range(b.tiles):
        for k in range(8):
            for r in range(2):
                n = 8 * u + k
                pe.product(psum[64 * r:64 * r + 64, 2 * u + k // 4, (k % 4) * 66:(k % 4 + 1) * 66],
                           m["pT"][:, n * P + 64 * r:n * P + 64 * r + 64],
                           m["va"][:, 2 * u + r, 2 * k:2 * k + 2, :].rearrange("p h e -> p (h e)"),
                           start=True, stop=True, after=(copied[u],))
        out = psum[:, 2 * u:2 * u + 2, 0:264].rearrange("p a (h e) -> p a h e", h=8)
        z = m["z"][:, 2 * u:2 * u + 2, :]
        dve.do(nc.vector.reciprocal, z, out[:, :, :, 32], after=(pe.mark(),))
        y = m["y"][:, u, :].rearrange("p (a h d) -> p a h d", a=2, h=8)
        y_done = dve.do(tt, y, out[:, :, :, 0:32], bcast(z, 3, 32), ALU.mult)
    for n in range(4):
        y_ready = to_features(b, m["qnT"][:, n, :], m["y"][:, :, n * P:(n + 1) * P], n, (y_done,))
    down = down_project(b, psum[:, 0, :], m["qnT"], b.weight("wo"), (y_ready,))
    dve.do(tt, m["x0"][:], m["x0"][:], psum[:, 0, 0:b.tok].rearrange("p (t d) -> p t d", t=b.tiles), ALU.add, after=(down,))
    normed = rms_norm(b, m["xn"][:], m["x0"][:], m["sq"][:], m["ss"][:], 1e-5)
    ready = to_features(b, m["xT"], m["xn"], 1, (normed,), b.weight("g2"), 0.0)
    logits, pl = logits_of(b, m["xT"], b.weight("router"), EXPERTS2, 3, (ready,))
    softmax_rows(b, m["e"][:], logits, b.weight("rbias"), m["best"][:], (pl,))
    dve.do(nc.vector.tensor_copy, m["v"][:], m["e"][:])
    picks = [m["pick"][:, r, :, :] for r in range(2)]
    pick_largest(b, picks, m["v"][:], m["best"], m["w"][:], c["first"], 2)
    combined = weigh_picks(b, m, picks)
    comb_ready = turn_combine(b, m, m["comb"], EXPERTS2 + 1, 3, (combined,))
    done = experts(b, m, m["xT"], b.core.half["spread2"], (EXPERTS2 + 1) * HID2, (comb_ready,))
    dve.do(tt, x, x, m["x0"][:], ALU.add)
    dve.do(tt, x, x, psum[:, 0, 0:b.tok].rearrange("p (t d) -> p t d", t=b.tiles), ALU.add, after=(done,))


def weigh_picks(b, m, picks):
    nc, dve = b.nc, b.dve
    tt = nc.vector.tensor_tensor
    dve.do(tt, m["w"][:], picks[0], picks[1], ALU.add)
    dve.do(tt, m["w"][:], m["w"][:], m["e"][:], ALU.mult)
    dve.do(nc.vector.tensor_reduce, m["best"][:], m["w"][:], AX, ALU.add)
    dve.do(nc.vector.reciprocal, m["best"][:], m["best"][:])
    return dve.do(tt, m["comb"][:, :, 0:8], m["w"][:], bcast(m["best"][:], 2, 8), ALU.mult)


def room_routed(sb, g):
    return {"e": sb("e", P, g.tiles, 8), "v": sb("v", P, g.tiles, 8), "w": sb("w", P, g.tiles, 8), "best": sb("best", P, g.tiles),
            "pick": sb("pick", P, 2, g.tiles, 8), "comb": sb("comb", P, g.tiles, 9), "combT": sb("combT", P, g.tok, dt=BF16),
            "parts": sb("parts", P, g.tiles, 27, dt=BF16), "rest": sb("rest", P, g.tiles, 9),
            "h": sb("h", P, 2, g.tok)}


def room_L2f(nc, ctx, g):
    sb = lambda n, *shape, dt=F32: ctx.enter_context(nc.sbuf_tensor(f"{g.tag}L2f_{n}", list(shape), dt))
    m = {"norm": norm_room(nc, ctx, g.tiles, g.tag + "L2f_norm"), "x0": sb("x0", P, g.tiles, D), "xn": sb("xn", P, g.tiles, D),
         "sq": sb("sq", P, g.tiles, D), "ss": sb("ss", P, g.tiles), "xT": sb("xT", P, g.tok), "latT": sb("latT", P, g.tok),
         "lat2": sb("lat2", P, g.seqs, 2, S), "krT": sb("krT", P, g.tok), "krx": sb("krx", P, 4, g.tok),
         "twin": sb("twin", P, 2, g.tok), "knx": sb("knx", P, 4, 4, g.tok), "qnT": sb("qnT", P, 4, g.tok),
         "qrT": sb("qrT", P, 4, g.tok), "va": sb("va", P, g.seqs, 16, 33), "p": sb("p", P, 2048), "mx": sb("mx", P, 32),
         "z": sb("z", P, 4, 8), **room_routed(sb, g)}
    spent = m["knx"][:].rearrange("p n j k -> p (n j k)")
    m["pT"], m["y"] = spent[:, 0:2048], spent[:, 2048:2048 + 512 * g.tiles].rearrange("p (t f) -> p t f", t=g.tiles)
    return m


def once_L2f(b, m):
    nc, parity = b.nc, b.core.c["parity"]
    nc.vector.tensor_copy(m["va"][:, :, :, 32], bcast(parity, 1, b.seqs))
    nc.vector.memset(m["latT"][:], 0.0)
    nc.vector.memset(m["lat2"][:], 0.0)
    once_shared(b, m)


def once_shared(b, m):
    b.nc.vector.memset(m["comb"][:, :, 8:9], 1.0)
    once_combine(b, m)


def block_L3a(b, i, m):
    nc, psum, c = b.nc, b.psum, b.core.c
    dve, act, pe, pool = b.dve, b.act, b.pe, b.pool
    tt = nc.vector.tensor_tensor
    x = b.core.x[:, bass.ts(i, b.tiles), :]
    tiles = lambda ap: ap.rearrange("p (t d) -> p t d", t=b.tiles)
    layer_norm(b, m["x0"], x, LN_EPS, m["norm"])
    normed = layer_norm(b, m["xn"], m["x0"], LN_EPS, m["norm"])
    ready = to_features(b, m["xT"], m["xn"], 0, (normed,), b.weight("g1"), b.weight("be1"))
    pe.product(psum[0:16, 3, :], b.weight("gk1"), m["xT"][:], start=True, stop=True, after=(ready,))
    gk_done = act.do(nc.scalar.copy, m["gkT"][:], psum[0:16, 3, :], after=(pe.mark(),))
    for bank, w in ((1, "wv"), (2, "wg")):
        for t in range(b.tiles):
            pe.product(psum[:, bank, t * P:(t + 1) * P], m["xT"][:, t * P:(t + 1) * P], b.weight(w), start=True, stop=True)
    pvg = pe.mark()
    for t in range(b.tiles):
        pe.product(psum[:, 0, t * P:(t + 1) * P], m["gkT"][:, t * P:(t + 1) * P], b.weight("gk2"), start=True, stop=True,
                   after=(gk_done,))
    pz = pe.mark()
    v_done = act.do(nc.scalar.copy, m["v"][:], tiles(psum[:, 1, :]), after=(pvg,))
    g_done = act.do(nc.scalar.activation, m["g"][:], tiles(psum[:, 2, :]), ACT.Silu)
    pe.product(psum[:, 1, :], b.weight("wq"), m["xT"][:], start=True, stop=True, after=(v_done,))
    pe.product(psum[:, 2, :], b.weight("wk"), m["xT"][:], start=True, stop=True, after=(g_done,))
    pqk = pe.mark()
    dve.do(tt, m["lz"][:], tiles(psum[:, 0, :]), bcast(b.weight("bgk"), 1, b.tiles), ALU.add, after=(pz,))
    size = dve.do(nc.vector.scalar_tensor_tensor, m["la"][:], m["lz"][:], -1.0, m["lz"][:], ALU.mult, ALU.max)
    act.do(nc.scalar.activation, m["la"][:], m["la"][:], ACT.Exp, scale=-1.0, after=(size,))
    log = act.do(nc.scalar.activation, m["la"][:], m["la"][:], ACT.Ln, bias=1.0)
    decays = dve.do(nc.vector.scalar_tensor_tensor, m["lz"][:], m["lz"][:], 0.0, m["la"][:], ALU.min, ALU.subtract,
                    after=(log,))
    for t in range(b.tiles):
        pe.product(psum[:, 3, t * P:(t + 1) * P], m["lz"][:, t, :], c["decay"], start=True, stop=True, after=(decays,))
    pg = pe.mark()
    up = act.do(nc.scalar.activation, m["eq"][:], psum[:, 3, :], ACT.Exp, after=(pg,))
    down = act.do(nc.scalar.activation, m["ek"][:], psum[:, 3, :], ACT.Exp, scale=-1.0)
    dve.do(nc.vector.scalar_tensor_tensor, m["eq"][:], psum[:, 1, :], 32 ** -0.5, m["eq"][:], ALU.mult, ALU.mult,
           after=(up, pqk))
    decayed = dve.do(tt, m["ek"][:], m["ek"][:], psum[:, 2, :], ALU.mult, after=(down,))
    for s in range(b.seqs):
        t, r = s // 2, s % 2
        q = slice(s * S, (s + 1) * S)
        for h in range(4):
            f = slice(32 * h, 32 * h + 32)
            pe.product(psum[64 * r:64 * r + 64, h, t * S:(t + 1) * S], m["ek"][f, q], m["eq"][f, q], start=True,
                       stop=True, after=(decayed,))
    masked = dve.do(tt, m["a"][:], psum[:, 0:4, 0:b.tiles * S].rearrange("p h (t q) -> p h t q", q=S),
                    bcast(bcast(c["past"], 1, b.tiles), 1, 4), ALU.mult, after=(pe.mark(),))
    for s in range(b.seqs):
        t, r = s // 2, s % 2
        q = slice(64 * r, 64 * r + 64)
        for h in range(4):
            f = slice(32 * h, 32 * h + 32)
            pe.product(psum[q, r, t * P + 32 * h:t * P + 32 * h + 32], m["a"][q, h, t, :], m["v"][q, t, f], start=True,
                       stop=True, after=(masked, v_done, g_done))
    po = pe.mark()
    for r in range(2):
        q = slice(64 * r, 64 * r + 64)
        copied = act.do(nc.scalar.copy, m["o"][q, :, :], tiles(psum[q, r, :]), after=(po,))
    heads = lambda ap: ap.rearrange("p t (h d) -> p (t h) d", h=4)
    rms_norm(b, heads(m["o"][:]), heads(m["o"][:]), heads(m["xn"][:]), m["ss"][:], 1e-5, (copied,))
    gated = dve.do(tt, m["o"][:], m["o"][:], m["g"][:], ALU.mult)
    o_ready = to_features(b, m["xT"], m["o"], 2, (gated,), b.weight("rms"), 0.0)
    project_out(b, m["x0"][:], m["xT"], b.weight("wo"), None, 3, (o_ready,))
    normed = layer_norm(b, m["xn"], m["x0"], LN_EPS, m["norm"])
    ready = to_features(b, m["xT"], m["xn"], 0, (normed,), b.weight("g2"), b.weight("be2"))
    dve.do(tt, m["x0"][:], m["x0"][:], bcast(b.weight("b2"), 1, b.tiles), ALU.add)
    dve.do(tt, x, x, m["x0"][:], ALU.add)
    for f in range(3):
        pe.product(psum[:, 1 + f, :], b.weight("w1")[:, f * P:(f + 1) * P], m["xT"][:], start=True, stop=True,
                   after=(ready,))
        biased = act.do(nc.scalar.activation, m["hT"][:, f, :], psum[:, 1 + f, :], ACT.Identity,
                        bias=b.weight("b1")[:, f:f + 1], scale=1.0, after=(pe.mark(),))
        h = m["hT"][:, f, :]
        leaky = dve.do(nc.vector.scalar_tensor_tensor, h, h, 0.01, h, ALU.mult, ALU.max, after=(biased,))
        squared = pool.do(nc.gpsimd.tensor_tensor, h, h, h, ALU.mult, after=(leaky,))
    done = down_project(b, psum[:, 0, :], m["hT"], b.weight("w2"), (squared,))
    dve.do(tt, x, x, tiles(psum[:, 0, :]), ALU.add, after=(done,))


def room_L3a(nc, ctx, g):
    sb = lambda n, *shape, dt=F32: ctx.enter_context(nc.sbuf_tensor(f"{g.tag}L3a_{n}", list(shape), dt))
    tile = ("x0", "xn", "lz", "la", "v", "g", "o")
    return {"norm": norm_room(nc, ctx, g.tiles, g.tag + "L3a_norm"), **{n: sb(n, P, g.tiles, D) for n in tile}, "xT": sb("xT", P, g.tok),
            "gkT": sb("gkT", 16, g.tok), "eq": sb("eq", P, g.tok), "ek": sb("ek", P, g.tok), "a": sb("a", P, 4, g.tiles, S),
            "ss": sb("ss", P, 4 * g.tiles), "hT": sb("hT", P, 3, g.tok)}


def block_L3f(b, i, m):
    nc, psum, c = b.nc, b.psum, b.core.c
    dve = b.dve
    tt = nc.vector.tensor_tensor
    x = b.core.x[:, bass.ts(i, b.tiles), :]
    normed = layer_norm(b, m["xn"], x, LN_EPS, m["norm"])
    ready = to_features(b, m["xT"], m["xn"], 0, (normed,))
    logits, pl = logits_of(b, m["xT"], b.weight("router"), EXPERTS3, 3, (ready,))
    dve.do(nc.vector.tensor_reduce, m["best"][:], logits, AX, ALU.max, after=(pl,))
    dve.do(nc.vector.tensor_copy, m["v"][:], logits)
    low = dve.do(tt, m["e"][:], logits, bcast(m["best"][:], 2, EXPERTS3), ALU.subtract)
    grown = b.act.do(nc.scalar.activation, m["e"][:], m["e"][:], ACT.Exp, after=(low,))
    picks = [m["pick"][:, r, :, :] for r in range(2)]
    pick_largest(b, picks, m["v"][:], m["best"], m["w"][:], c["first"], 2)
    dve.wait(grown)
    combined = weigh_picks(b, m, picks)
    comb_ready = turn_combine(b, m, m["comb"], EXPERTS3 + 1, 3, (combined,))
    done = experts(b, m, m["xT"], b.core.half["spread3"], (EXPERTS3 + 1) * HID3, (comb_ready,))
    dve.do(tt, x, x, psum[:, 0, :].rearrange("p (t d) -> p t d", t=b.tiles), ALU.add, after=(done,))


def room_L3f(nc, ctx, g):
    sb = lambda n, *shape, dt=F32: ctx.enter_context(nc.sbuf_tensor(f"{g.tag}L3f_{n}", list(shape), dt))
    return {"norm": norm_room(nc, ctx, g.tiles, g.tag + "L3f_norm"), "xn": sb("xn", P, g.tiles, D), "xT": sb("xT", P, g.tok), **room_routed(sb, g)}


TILES = {"L1x": 2, "L2f": 2}
ROOMS = {"L0x": room_L0x, "L0a": room_L0a, "L0f": room_L0f, "L1x": room_L1x, "L1a": room_L1a, "L1f": room_L1f,
         "L2x": room_L2x, "L2a": room_L2a, "L2f": room_L2f, "L3x": room_L3x, "L3a": room_L3a, "L3f": room_L3f}
BODIES = {"L0x": block_L0x, "L0a": block_L0a, "L0f": block_L0f, "L1x": block_L1x, "L1a": block_L1a, "L1f": block_L1f,
          "L2x": block_L2x, "L2a": block_L2a, "L2f": block_L2f, "L3x": block_L3x, "L3a": block_L3a, "L3f": block_L3f}
ONCE = {"L0x": once_L0x, "L0a": once_ones, "L0f": once_combine, "L1x": once_L1x, "L1a": once_L1a, "L1f": once_L1f,
        "L2x": once_value_ones, "L2a": once_ones, "L2f": once_L2f, "L3x": once_value_ones, "L3f": once_shared}
HEAD = {"L0x": 0.3, "L0a": 0.2, "L0f": 0.35, "L1x": 0.2, "L1a": 0.15, "L1f": 0.4, "L2x": 0.1, "L2a": 0.3, "L2f": 0.25,
        "L3x": 0.05, "L3a": 0.2, "L3f": 0.35}



def build(nc, n_seq, weights, constants, halves, x, ctxT, ctx_tok, mask, out, plan, blocks):
    table = weight_table()
    places, _ = weight_places(table)
    core = Core()
    core.nc, core.places = nc, places
    ctx = ExitStack()
    sb = lambda n, *shape: ctx.enter_context(nc.sbuf_tensor(n, list(shape), F32))
    core.x = sb("x_held", P, n_seq // 2, D)
    core.ctxT, core.ctx_tok = ctxT, ctx_tok
    core.mask = mask.rearrange("(t r) k -> r t k", r=2)
    core.psum = ctx.enter_context(nc.psum_tensor("psum", [P, 8, BANK], F32))
    const_tile = sb("constants_held", P, constants.shape[1])
    core.c, at = {}, 0
    for name, value in constant_table().items():
        core.c[name] = const_tile[0:value.shape[0], at:at + value.shape[1]]
        at += value.shape[1]
    half_tile = sb("halves_held", P, halves.shape[1])
    core.half, at = {}, 0
    for name, value in half_table().items():
        core.half[name] = half_tile[:].bitcast(BF16)[:, at:at + value.shape[1]]
        at += value.shape[1]
    widest = [max(places[n][1] for n in blocks[k::2]) if blocks[k::2] else 1 for k in range(2)]
    weight_rooms = [sb(f"weights{k}", P, widest[k]) for k in range(2)]
    core.weight_room = {n: weight_rooms[k % 2] for k, n in enumerate(blocks)}
    core.idle = {k: nc.alloc_semaphore(f"idle_{k}") for k in ("pe", "dve", "act", "pool", "load0", "load1")}
    loaded = nc.alloc_semaphore("loaded")
    n_loaded = 0

    def load(dst, src):
        nc.sync.dma_start(dst, src).then_inc(loaded, 16)

    def load_weights(name):
        first, n, _ = places[name]
        load(core.weight_room[name][:, 0:n], weights[:, first:first + n])

    load_weights(blocks[0])
    load(const_tile[:], constants)
    x_tiles = "(n p) d -> p n d"
    load(core.x[:], x.rearrange(x_tiles, p=P))
    load(half_tile[:], halves)
    n_loaded = 4
    for k, name in enumerate(blocks):
        with ExitStack() as own:
            b = Block(core, name, plan)
            tiles = TILES.get(name, 4)
            contexts = [Context(b, k, tiles) for k in range(CONTEXTS)]
            rooms = [ROOMS[name](nc, own, g) for g in contexts]
            for engine in (nc.tensor, nc.vector, nc.scalar, nc.gpsimd):
                engine.wait_ge(loaded, 16 * n_loaded)
            if name in ONCE:
                for g, m in zip(contexts, rooms):
                    ONCE[name](g, m)
            nc.all_engine_barrier()
            if k + 1 < len(blocks):
                load_weights(blocks[k + 1])
                n_loaded += 1
            b.run(BODIES[name], contexts, rooms, n_seq // (CONTEXTS * 2 * tiles), HEAD[name])
            nc.all_engine_barrier()
    stored = nc.alloc_semaphore("stored")
    nc.sync.dma_start(out.rearrange(x_tiles, p=P), core.x[:]).then_inc(stored, 16)
    nc.sync.wait_ge(stored, 16)
    ctx.close()


BLOCKS = ["L0x", "L0a", "L0f", "L1x", "L1a", "L1f", "L2x", "L2a", "L2f", "L3x", "L3a", "L3f"]


def program(nc, n_seq, n_weights, n_constants, n_halves, plan, blocks=BLOCKS):
    dram = lambda n, shape, dt=F32, kind="ExternalInput": nc.dram_tensor(n, shape, dt, kind=kind).ap()
    build(nc, n_seq, dram("weights", (P, n_weights)), dram("constants", (P, n_constants)), dram("halves", (P, n_halves)), dram("x", (n_seq * S, D)),
          dram("ctxT", (CX, n_seq * SC)), dram("ctx", (P, n_seq, CX)), dram("mask", (n_seq, SC // 4), I32),
          dram("out", (n_seq * S, D), kind="ExternalOutput"), plan, blocks)


def kernel(**inputs):
    import concourse.bacc as bacc
    from concourse.bass_utils import run_bass_kernel_spmd
    a = {k: np.asarray(v) for k, v in inputs.items()}
    x, context, mask = a["x"], a["ctx_768"], a["mask_BxS2_bk0"]
    n_seq = x.shape[0]
    packed = []
    for entries in weight_table().values():
        for name, rows, cols, layout in entries:
            w = layout(a)
            assert w.shape == (rows, cols), (name, w.shape)
            packed.append(pad_rows(w, P))
    weights = np.ascontiguousarray(np.concatenate(packed, 1))
    constants = np.ascontiguousarray(np.concatenate([pad_rows(v, P) for v in constant_table().values()], 1))
    halves = half_words(half_table())
    arrays = {
        "weights": weights, "constants": constants, "halves": halves, "x": np.ascontiguousarray(x.reshape(-1, D)),
        "ctxT": np.ascontiguousarray(context.transpose(2, 0, 1).reshape(CX, -1)),
        "ctx": np.ascontiguousarray(context.transpose(1, 0, 2)), "mask": np.ascontiguousarray(mask).view(np.int32)}
    plan = {}
    for _ in range(2):
        nc = bacc.Bacc("TRN2", target_bir_lowering=False, num_devices=1)
        program(nc, n_seq, weights.shape[1], constants.shape[1], halves.shape[1], plan)
    r = run_bass_kernel_spmd(nc, [arrays], core_ids=[0])
    return r.results[0]["out"].reshape(x.shape)
```
